# Optimizing a Trainium2 kernel written in Bass

```python
import numpy as np
import jax
import jax.numpy as jnp

def _softmax(x, axis=-1):
    return jax.nn.softmax(x, axis=axis)

def _gelu(x):
    return jax.nn.gelu(x, approximate=True)

def _silu(x):
    return jax.nn.silu(x)

def _sigmoid(x):
    return jax.nn.sigmoid(x)

def _layernorm(x, axis=-1, eps=1e-05):
    m = jnp.mean(x, axis=axis, keepdims=True)
    v = jnp.var(x, axis=axis, keepdims=True)
    return (x - m) / jnp.sqrt(v + eps)

def _scatter_add(tgt, idx, src, axis=0):
    return tgt.at[idx].add(src)

def _segment_sum(src, seg, n):
    return jax.ops.segment_sum(src, seg, n)
kernel_name = 'mk_hybrid_d2_jaxref_r8_19b6b9'

def setup_inputs(seed: int=0):
    np.random.seed(seed)
    _w = jnp.asarray

    def _L0_attn_a_setup():
        import jax, jax.numpy as jnp
        import numpy as np
        D_MODEL = 256
        D_INNER = 2 * D_MODEL
        D_STATE = 16
        D_CONV = 4
        DT_RANK = D_MODEL // 16
        BATCH, SEQLEN = (2, 128)

        def _mamba_forward(hidden_states, in_proj_w, conv_w, conv_b, x_proj_w, dt_proj_w, dt_proj_b, A_log, D, out_proj_w):
            B, L, _ = hidden_states.shape
            xz = jnp.einsum('bld,ed->ble', hidden_states, in_proj_w)
            x, z = jnp.split(xz, 2, axis=-1)
            x_pad = jnp.pad(x, ((0, 0), (D_CONV - 1, 0), (0, 0)))
            windows = jnp.stack([x_pad[:, k:k + L, :] for k in range(D_CONV)], axis=-1)
            x_conv = jnp.einsum('bldk,dk->bld', windows, conv_w) + conv_b
            x_act = jax.nn.silu(x_conv)
            x_dbl = jnp.einsum('bld,ed->ble', x_act, x_proj_w)
            dt, Bc, Cc = jnp.split(x_dbl, [DT_RANK, DT_RANK + D_STATE], axis=-1)
            dt = jax.nn.softplus(jnp.einsum('blr,dr->bld', dt, dt_proj_w) + dt_proj_b)
            A = -jnp.exp(A_log)

            def step(h, inp):
                x_t, dt_t, B_t, C_t = inp
                dA = jnp.exp(dt_t[:, :, None] * A[None])
                dBx = dt_t[:, :, None] * B_t[:, None, :] * x_t[:, :, None]
                h = h * dA + dBx
                y = jnp.einsum('bdn,bn->bd', h, C_t)
                return (h, y)
            xs = (x_act.transpose(1, 0, 2), dt.transpose(1, 0, 2), Bc.transpose(1, 0, 2), Cc.transpose(1, 0, 2))
            h0 = jnp.zeros((B, D_INNER, D_STATE), x_act.dtype)
            _, ys = jax.lax.scan(step, h0, xs)
            y = ys.transpose(1, 0, 2) + x_act * D
            y = y * jax.nn.silu(z)
            return jnp.einsum('bld,md->blm', y, out_proj_w)
        key = jax.random.key(seed)
        ks = jax.random.split(key, 10)
        s = 0.02
        inp = {'hidden_states': jax.random.normal(ks[0], (BATCH, SEQLEN, D_MODEL), jnp.float32), 'in_proj_w': jax.random.normal(ks[1], (2 * D_INNER, D_MODEL), jnp.float32) * s, 'conv_w': jax.random.normal(ks[2], (D_INNER, D_CONV), jnp.float32) * s, 'conv_b': jax.random.normal(ks[3], (D_INNER,), jnp.float32) * s, 'x_proj_w': jax.random.normal(ks[4], (DT_RANK + 2 * D_STATE, D_INNER), jnp.float32) * s, 'dt_proj_w': jax.random.normal(ks[5], (D_INNER, DT_RANK), jnp.float32) * s, 'dt_proj_b': jax.random.normal(ks[6], (D_INNER,), jnp.float32) * 0.1, 'A_log': jnp.log(jnp.tile(jnp.arange(1, D_STATE + 1, dtype=jnp.float32), (D_INNER, 1))), 'D': jnp.ones((D_INNER,), jnp.float32), 'out_proj_w': jax.random.normal(ks[7], (D_MODEL, D_INNER), jnp.float32) * s}
        return inp
    _L0_attn_a_in = _L0_attn_a_setup()

    def _L0_attn_b_setup():
        import jax, jax.numpy as jnp
        import numpy as np
        NUM_HEADS = 16
        ROPE_BASE = 10000.0

        def build_rope_cache(seq_len, n_elem):
            theta = 1.0 / ROPE_BASE ** (jnp.arange(0, n_elem, 2, dtype=jnp.float32) / n_elem)
            idx_theta = jnp.outer(jnp.arange(seq_len, dtype=jnp.float32), theta)
            return jnp.stack([jnp.cos(idx_theta), jnp.sin(idx_theta)], axis=-1)

        def apply_rope(x, rope):
            B, H, T, D = x.shape
            xt = x.transpose(0, 2, 1, 3)
            xs = xt.reshape(B, T, H, D // 2, 2)
            rc = rope[:T].reshape(1, T, 1, D // 2, 2)
            cos, sin = (rc[..., 0], rc[..., 1])
            x0, x1 = (xs[..., 0], xs[..., 1])
            out = jnp.stack([x0 * cos - x1 * sin, x1 * cos + x0 * sin], axis=-1)
            return out.reshape(B, T, H, D).transpose(0, 2, 1, 3)
        key = jax.random.key(seed)
        k1, k2, k3 = jax.random.split(key, 3)
        B, T, C = (2, 256, 256)
        x = jax.random.normal(k1, (B, T, C), dtype=jnp.float32)
        w_atten = jax.random.normal(k2, (3 * C, C), dtype=jnp.float32) * (1.0 / np.sqrt(C))
        w_proj = jax.random.normal(k3, (C, C), dtype=jnp.float32) * (1.0 / np.sqrt(C))
        return {'x': x, 'w_atten': w_atten, 'w_proj': w_proj}
    _L0_attn_b_in = _L0_attn_b_setup()

    def _L0_ffn_setup():
        import jax, jax.numpy as jnp
        import numpy as np
        SWIGLU_ALPHA = 1.702
        SWIGLU_LIMIT = 7.0
        B, S, H, E, K, I = (2, 256, 256, 32, 4, 128)
        key = jax.random.key(seed)
        ks = jax.random.split(key, 8)
        return {'hidden_states': jax.random.normal(ks[0], (B, S, H), jnp.float32), 'gate_w': jax.random.normal(ks[1], (E, H), jnp.float32) * 0.02, 'gate_b': jnp.zeros((E,), jnp.float32), 'w_gate': jax.random.normal(ks[2], (E, H, I), jnp.float32) * 0.02, 'b_gate': jnp.zeros((E, I), jnp.float32), 'w_up': jax.random.normal(ks[3], (E, H, I), jnp.float32) * 0.02, 'b_up': jnp.zeros((E, I), jnp.float32), 'w_down': jax.random.normal(ks[4], (E, I, H), jnp.float32) * 0.02, 'b_down': jnp.zeros((E, H), jnp.float32)}
    _L0_ffn_in = _L0_ffn_setup()

    def _L1_attn_a_setup():
        import jax, jax.numpy as jnp
        import numpy as np
        NQ, NKV, HD, SW = (32, 8, 64, 64)
        QM = NQ // NKV

        def _rope_tables(L):
            inv_freq = (1.0 / 1024.0) ** jnp.linspace(0.0, 1.0, HD // 4)
            inv_freq = jnp.concatenate([inv_freq, jnp.zeros(HD // 4)])
            theta = jnp.arange(L, dtype=jnp.float32)[:, None] * inv_freq[None, :]
            return (jnp.cos(theta), jnp.sin(theta))

        def _apply_rope(x, cos, sin):
            x1, x2 = jnp.split(x, 2, axis=-1)
            return jnp.concatenate([x1 * cos + x2 * sin, -x1 * sin + x2 * cos], axis=-1)
        key = jax.random.key(seed)
        k1, k2, k3 = jax.random.split(key, 3)
        B, L, D = (1, 256, 256)
        x = jax.random.normal(k1, (B, L, D), jnp.float32)
        W_qkv = jax.random.normal(k2, (D, (NQ + 2 * NKV) * HD), jnp.float32) * 0.02
        W_out = jax.random.normal(k3, (NQ * HD, D), jnp.float32) * 0.02
        s = jnp.zeros((1, NKV, QM), jnp.float32)
        return {'x': x, 'W_qkv': W_qkv, 'W_out': W_out, 's': s}
    _L1_attn_a_in = _L1_attn_a_setup()

    def _L1_attn_b_setup():
        import jax, jax.numpy as jnp
        import numpy as np
        import math
        B, T, C = (2, 256, 256)
        NH, L = (16, 128)
        key = jax.random.key(seed)
        ks = jax.random.split(key, 7)
        s = 0.02
        return {'x': jax.random.normal(ks[0], (B, T, C), dtype=jnp.float32), 'W_lat': jax.random.normal(ks[1], (C, L), dtype=jnp.float32) * s, 'b_lat': jnp.zeros((L,), dtype=jnp.float32), 'W_d': jax.random.normal(ks[2], (C, NH * L), dtype=jnp.float32) * s, 'b_d': jnp.zeros((NH * L,), dtype=jnp.float32), 'W_proj': jax.random.normal(ks[3], (NH * L, C), dtype=jnp.float32) * s, 'b_proj': jnp.zeros((C,), dtype=jnp.float32)}
    _L1_attn_b_in = _L1_attn_b_setup()

    def _L1_ffn_setup():
        import jax, jax.numpy as jnp
        import numpy as np
        NUM_EXPERTS = 128
        NUM_KEPT = 48
        TOP_K = 8
        HIDDEN = 256
        INTER = 96
        CAP = 96
        BATCH, SEQ = (2, 128)
        key = jax.random.key(seed)
        k1, k2, k3, k4 = jax.random.split(key, 4)
        hidden_states = jax.random.normal(k1, (BATCH, SEQ, HIDDEN), jnp.float32)
        gate_weight = jax.random.normal(k2, (NUM_EXPERTS, HIDDEN), jnp.float32) * 0.02
        gate_up_proj = jax.random.normal(k3, (NUM_KEPT, 2 * INTER, HIDDEN), jnp.float32) * 0.02
        down_proj = jax.random.normal(k4, (NUM_KEPT, HIDDEN, INTER), jnp.float32) * 0.02
        o2n = -np.ones(NUM_EXPERTS, np.int32)
        o2n[np.arange(NUM_KEPT) * 2] = np.arange(NUM_KEPT, dtype=np.int32)
        old_to_new = jnp.asarray(o2n)
        return {'hidden_states': hidden_states, 'gate_weight': gate_weight, 'gate_up_proj': gate_up_proj, 'down_proj': down_proj, 'old_to_new': old_to_new}
    _L1_ffn_in = _L1_ffn_setup()
    _d = {'L0_attn_a_hidden_states': _L0_attn_a_in['hidden_states'], 'L0_attn_a_in_proj_w': _L0_attn_a_in['in_proj_w'], 'L0_attn_a_conv_w': _L0_attn_a_in['conv_w'], 'L0_attn_a_conv_b': _L0_attn_a_in['conv_b'], 'L0_attn_a_x_proj_w': _L0_attn_a_in['x_proj_w'], 'L0_attn_a_dt_proj_w': _L0_attn_a_in['dt_proj_w'], 'L0_attn_a_dt_proj_b': _L0_attn_a_in['dt_proj_b'], 'L0_attn_a_A_log': _L0_attn_a_in['A_log'], 'L0_attn_a_D': _L0_attn_a_in['D'], 'L0_attn_a_out_proj_w': _L0_attn_a_in['out_proj_w'], 'L0_attn_b_w_atten': _L0_attn_b_in['w_atten'], 'L0_attn_b_w_proj': _L0_attn_b_in['w_proj'], 'L0_ffn_gate_w': _L0_ffn_in['gate_w'], 'L0_ffn_gate_b': _L0_ffn_in['gate_b'], 'L0_ffn_w_gate': _L0_ffn_in['w_gate'], 'L0_ffn_b_gate': _L0_ffn_in['b_gate'], 'L0_ffn_w_up': _L0_ffn_in['w_up'], 'L0_ffn_b_up': _L0_ffn_in['b_up'], 'L0_ffn_w_down': _L0_ffn_in['w_down'], 'L0_ffn_b_down': _L0_ffn_in['b_down'], 'L1_attn_a_W_qkv': _L1_attn_a_in['W_qkv'], 'L1_attn_a_W_out': _L1_attn_a_in['W_out'], 'L1_attn_a_s': _L1_attn_a_in['s'], 'L1_attn_b_W_lat': _L1_attn_b_in['W_lat'], 'L1_attn_b_b_lat': _L1_attn_b_in['b_lat'], 'L1_attn_b_W_d': _L1_attn_b_in['W_d'], 'L1_attn_b_b_d': _L1_attn_b_in['b_d'], 'L1_attn_b_W_proj': _L1_attn_b_in['W_proj'], 'L1_attn_b_b_proj': _L1_attn_b_in['b_proj'], 'L1_ffn_gate_weight': _L1_ffn_in['gate_weight'], 'L1_ffn_gate_up_proj': _L1_ffn_in['gate_up_proj'], 'L1_ffn_down_proj': _L1_ffn_in['down_proj'], 'L1_ffn_old_to_new': _L1_ffn_in['old_to_new']}
    _x0 = _d['L0_attn_a_hidden_states']
    _d['L0_attn_a_hidden_states'] = jax.random.normal(jax.random.fold_in(jax.random.key(seed), 1), (4, 512, 256), dtype=_x0.dtype)
    del _x0
    return _d

def reference(L0_attn_a_hidden_states, L0_attn_a_in_proj_w, L0_attn_a_conv_w, L0_attn_a_conv_b, L0_attn_a_x_proj_w, L0_attn_a_dt_proj_w, L0_attn_a_dt_proj_b, L0_attn_a_A_log, L0_attn_a_D, L0_attn_a_out_proj_w, L0_attn_b_w_atten, L0_attn_b_w_proj, L0_ffn_gate_w, L0_ffn_gate_b, L0_ffn_w_gate, L0_ffn_b_gate, L0_ffn_w_up, L0_ffn_b_up, L0_ffn_w_down, L0_ffn_b_down, L1_attn_a_W_qkv, L1_attn_a_W_out, L1_attn_a_s, L1_attn_b_W_lat, L1_attn_b_b_lat, L1_attn_b_W_d, L1_attn_b_b_d, L1_attn_b_W_proj, L1_attn_b_b_proj, L1_ffn_gate_weight, L1_ffn_gate_up_proj, L1_ffn_down_proj, L1_ffn_old_to_new):

    def _L0_attn_a_ref(hidden_states, in_proj_w, conv_w, conv_b, x_proj_w, dt_proj_w, dt_proj_b, A_log, D, out_proj_w):
        import jax, jax.numpy as jnp
        import numpy as np
        D_MODEL = 256
        D_INNER = 2 * D_MODEL
        D_STATE = 16
        D_CONV = 4
        DT_RANK = D_MODEL // 16
        BATCH, SEQLEN = (2, 128)

        def _mamba_forward(hidden_states, in_proj_w, conv_w, conv_b, x_proj_w, dt_proj_w, dt_proj_b, A_log, D, out_proj_w):
            B, L, _ = hidden_states.shape
            xz = jnp.einsum('bld,ed->ble', hidden_states, in_proj_w)
            x, z = jnp.split(xz, 2, axis=-1)
            x_pad = jnp.pad(x, ((0, 0), (D_CONV - 1, 0), (0, 0)))
            windows = jnp.stack([x_pad[:, k:k + L, :] for k in range(D_CONV)], axis=-1)
            x_conv = jnp.einsum('bldk,dk->bld', windows, conv_w) + conv_b
            x_act = jax.nn.silu(x_conv)
            x_dbl = jnp.einsum('bld,ed->ble', x_act, x_proj_w)
            dt, Bc, Cc = jnp.split(x_dbl, [DT_RANK, DT_RANK + D_STATE], axis=-1)
            dt = jax.nn.softplus(jnp.einsum('blr,dr->bld', dt, dt_proj_w) + dt_proj_b)
            A = -jnp.exp(A_log)

            def step(h, inp):
                x_t, dt_t, B_t, C_t = inp
                dA = jnp.exp(dt_t[:, :, None] * A[None])
                dBx = dt_t[:, :, None] * B_t[:, None, :] * x_t[:, :, None]
                h = h * dA + dBx
                y = jnp.einsum('bdn,bn->bd', h, C_t)
                return (h, y)
            xs = (x_act.transpose(1, 0, 2), dt.transpose(1, 0, 2), Bc.transpose(1, 0, 2), Cc.transpose(1, 0, 2))
            h0 = jnp.zeros((B, D_INNER, D_STATE), x_act.dtype)
            _, ys = jax.lax.scan(step, h0, xs)
            y = ys.transpose(1, 0, 2) + x_act * D
            y = y * jax.nn.silu(z)
            return jnp.einsum('bld,md->blm', y, out_proj_w)
        return _mamba_forward(hidden_states, in_proj_w, conv_w, conv_b, x_proj_w, dt_proj_w, dt_proj_b, A_log, D, out_proj_w)

    def _L0_attn_b_ref(x, w_atten, w_proj):
        import jax, jax.numpy as jnp
        import numpy as np
        NUM_HEADS = 16
        ROPE_BASE = 10000.0

        def build_rope_cache(seq_len, n_elem):
            theta = 1.0 / ROPE_BASE ** (jnp.arange(0, n_elem, 2, dtype=jnp.float32) / n_elem)
            idx_theta = jnp.outer(jnp.arange(seq_len, dtype=jnp.float32), theta)
            return jnp.stack([jnp.cos(idx_theta), jnp.sin(idx_theta)], axis=-1)

        def apply_rope(x, rope):
            B, H, T, D = x.shape
            xt = x.transpose(0, 2, 1, 3)
            xs = xt.reshape(B, T, H, D // 2, 2)
            rc = rope[:T].reshape(1, T, 1, D // 2, 2)
            cos, sin = (rc[..., 0], rc[..., 1])
            x0, x1 = (xs[..., 0], xs[..., 1])
            out = jnp.stack([x0 * cos - x1 * sin, x1 * cos + x0 * sin], axis=-1)
            return out.reshape(B, T, H, D).transpose(0, 2, 1, 3)
        B, T, C = x.shape
        H = NUM_HEADS
        D = C // H
        qkv = x @ w_atten.T
        q, k, v = jnp.split(qkv, 3, axis=2)
        q = q.reshape(B, T, H, D).transpose(0, 2, 1, 3)
        k = k.reshape(B, T, H, D).transpose(0, 2, 1, 3)
        v = v.reshape(B, T, H, D).transpose(0, 2, 1, 3)
        rope = build_rope_cache(T, D)
        q = apply_rope(q, rope)
        k = apply_rope(k, rope)
        att = jnp.einsum('bhqd,bhkd->bhqk', q, k) * (1.0 / jnp.sqrt(jnp.float32(D)))
        causal = jnp.tril(jnp.ones((T, T), dtype=bool))
        att = jnp.where(causal[None, None], att, jnp.float32(-jnp.inf))
        att = jax.nn.softmax(att, axis=-1)
        y = jnp.einsum('bhqk,bhkd->bhqd', att, v)
        y = y.transpose(0, 2, 1, 3).reshape(B, T, C)
        return y @ w_proj.T

    def _L0_ffn_ref(hidden_states, gate_w, gate_b, w_gate, b_gate, w_up, b_up, w_down, b_down):
        import jax, jax.numpy as jnp
        import numpy as np
        SWIGLU_ALPHA = 1.702
        SWIGLU_LIMIT = 7.0
        B, S, H, E, K, I = (2, 256, 256, 32, 4, 128)
        Bb, Ss, Hh = hidden_states.shape
        x = hidden_states.reshape(-1, Hh)
        logits = x @ gate_w.T + gate_b
        topk_logits, topk_idx = jax.lax.top_k(logits, K)
        topk_weight = jax.nn.softmax(topk_logits.astype(jnp.float32), axis=-1)
        flat_idx = topk_idx.reshape(-1)
        xs = jnp.repeat(x, K, axis=0)
        order = jnp.argsort(flat_idx)
        xt = xs[order]
        gid = flat_idx[order]
        group_sizes = jnp.bincount(flat_idx, length=E).astype(jnp.int32)
        gate = jax.lax.ragged_dot(xt, w_gate, group_sizes) + b_gate[gid]
        up = jax.lax.ragged_dot(xt, w_up, group_sizes) + b_up[gid]
        gate = jnp.minimum(gate, SWIGLU_LIMIT)
        up = jnp.clip(up, -SWIGLU_LIMIT, SWIGLU_LIMIT)
        glu = gate * jax.nn.sigmoid(SWIGLU_ALPHA * gate)
        activated = (up + 1.0) * glu
        outs = jax.lax.ragged_dot(activated, w_down, group_sizes) + b_down[gid]
        inv = jnp.argsort(order)
        outs = outs[inv].reshape(-1, K, Hh)
        y = jnp.sum(outs * topk_weight[..., None], axis=1).astype(x.dtype)
        return y.reshape(Bb, Ss, Hh)

    def _L1_attn_a_ref(x, W_qkv, W_out, s):
        import jax, jax.numpy as jnp
        import numpy as np
        NQ, NKV, HD, SW = (32, 8, 64, 64)
        QM = NQ // NKV

        def _rope_tables(L):
            inv_freq = (1.0 / 1024.0) ** jnp.linspace(0.0, 1.0, HD // 4)
            inv_freq = jnp.concatenate([inv_freq, jnp.zeros(HD // 4)])
            theta = jnp.arange(L, dtype=jnp.float32)[:, None] * inv_freq[None, :]
            return (jnp.cos(theta), jnp.sin(theta))

        def _apply_rope(x, cos, sin):
            x1, x2 = jnp.split(x, 2, axis=-1)
            return jnp.concatenate([x1 * cos + x2 * sin, -x1 * sin + x2 * cos], axis=-1)
        B, L, D = x.shape
        proj = x @ W_qkv
        q, k, v = jnp.split(proj, (NQ * HD, (NQ + NKV) * HD), axis=-1)
        cos, sin = _rope_tables(L)
        q = _apply_rope(q.reshape(B, L, NKV, QM, HD), cos[None, :, None, None, :], sin[None, :, None, None, :])
        k = _apply_rope(k.reshape(B, L, NKV, HD), cos[None, :, None, :], sin[None, :, None, :])
        v = v.reshape(B, L, NKV, HD)
        sm_scale = 1.0 / jnp.sqrt(jnp.float32(HD))
        attn = jnp.einsum('bqhmd,bkhd->bhmqk', q, k) * sm_scale
        q_pos = jnp.arange(L)[:, None]
        k_pos = jnp.arange(L)[None, :]
        mask = (q_pos >= k_pos) & (q_pos < k_pos + SW)
        attn = jnp.where(mask, -jnp.inf, attn)
        sink = jnp.broadcast_to(s[:, :, :, None, None], attn.shape[:-1] + (1,))
        w = jax.nn.softmax(jnp.concatenate([attn, sink], axis=-1), axis=-1)[..., :-1]
        out = jnp.einsum('bhmqk,bkhd->bqhmd', w, v).reshape(B, L, NQ * HD)
        return out @ W_out

    def _L1_attn_b_ref(x, W_lat, b_lat, W_d, b_d, W_proj, b_proj):
        import jax, jax.numpy as jnp
        import numpy as np
        import math
        B, T, C = (2, 256, 256)
        NH, L = (16, 128)
        Bx, Tx, Cx = x.shape
        k = x @ W_lat + b_lat
        q = (x @ W_d + b_d).reshape(Bx, Tx, NH, L)
        q = jnp.transpose(q, (0, 2, 1, 3))
        scale = 1.0 / math.sqrt(L)
        att = jnp.einsum('bhtl,bsl->bhts', q, k) * scale
        causal = jnp.tril(jnp.ones((Tx, Tx), dtype=bool))
        att = jnp.where(causal[None, None], att, -jnp.inf)
        att = jax.nn.softmax(att, axis=-1)
        y = jnp.einsum('bhts,bsl->bhtl', att, k)
        y = jnp.transpose(y, (0, 2, 1, 3)).reshape(Bx, Tx, NH * L)
        return y @ W_proj + b_proj

    def _L1_ffn_ref(hidden_states, gate_weight, gate_up_proj, down_proj, old_to_new):
        import jax, jax.numpy as jnp
        import numpy as np
        NUM_EXPERTS = 128
        NUM_KEPT = 48
        TOP_K = 8
        HIDDEN = 256
        INTER = 96
        CAP = 96
        BATCH, SEQ = (2, 128)
        B, S, H = hidden_states.shape
        x = hidden_states.reshape(-1, H)
        T = x.shape[0]
        logits = x @ gate_weight.T
        logits = jnp.where(old_to_new[None, :] == -1, -jnp.inf, logits)
        probs = jax.nn.softmax(logits.astype(jnp.float32), axis=-1).astype(logits.dtype)
        top_v, top_i = jax.lax.top_k(probs, TOP_K)
        top_v = top_v / jnp.sum(top_v, axis=-1, keepdims=True)
        sel_new = old_to_new[top_i]
        E = gate_up_proj.shape[0]
        flat_e = sel_new.reshape(-1)
        flat_w = top_v.reshape(-1)
        tok = jnp.repeat(jnp.arange(T), TOP_K)
        oh = (flat_e[:, None] == jnp.arange(E)[None, :]).astype(jnp.int32)
        pos = jnp.sum(jnp.cumsum(oh, axis=0) * oh, axis=-1) - 1
        valid = pos < CAP
        pos_c = jnp.where(valid, pos, CAP)
        xb = jnp.zeros((E, CAP + 1, H), x.dtype).at[flat_e, pos_c].set(x[tok])
        xb = xb[:, :CAP]
        gu = jnp.einsum('ech,eoh->eco', xb, gate_up_proj)
        g, u = jnp.split(gu, 2, axis=-1)
        h = jax.nn.silu(g) * u
        out = jnp.einsum('eci,ehi->ech', h, down_proj)
        y = out[flat_e, jnp.minimum(pos_c, CAP - 1)]
        w = flat_w * valid.astype(flat_w.dtype)
        final = jnp.zeros_like(x).at[tok].add(y * w[:, None])
        return final.reshape(B, S, H)
    x = L0_attn_a_hidden_states
    x = x + _L0_attn_a_ref(_layernorm(x, axis=-1), L0_attn_a_in_proj_w, L0_attn_a_conv_w, L0_attn_a_conv_b, L0_attn_a_x_proj_w, L0_attn_a_dt_proj_w, L0_attn_a_dt_proj_b, L0_attn_a_A_log, L0_attn_a_D, L0_attn_a_out_proj_w)
    x = x + _L0_ffn_ref(_layernorm(x, axis=-1), L0_ffn_gate_w, L0_ffn_gate_b, L0_ffn_w_gate, L0_ffn_b_gate, L0_ffn_w_up, L0_ffn_b_up, L0_ffn_w_down, L0_ffn_b_down)
    x = x + _L0_attn_b_ref(_layernorm(x, axis=-1), L0_attn_b_w_atten, L0_attn_b_w_proj)
    x = x + _L0_ffn_ref(_layernorm(x, axis=-1), L0_ffn_gate_w, L0_ffn_gate_b, L0_ffn_w_gate, L0_ffn_b_gate, L0_ffn_w_up, L0_ffn_b_up, L0_ffn_w_down, L0_ffn_b_down)
    x = x + _L1_attn_a_ref(_layernorm(x, axis=-1), L1_attn_a_W_qkv, L1_attn_a_W_out, L1_attn_a_s)
    x = x + _L1_ffn_ref(_layernorm(x, axis=-1), L1_ffn_gate_weight, L1_ffn_gate_up_proj, L1_ffn_down_proj, L1_ffn_old_to_new)
    x = x + _L1_attn_b_ref(_layernorm(x, axis=-1), L1_attn_b_W_lat, L1_attn_b_b_lat, L1_attn_b_W_d, L1_attn_b_b_d, L1_attn_b_W_proj, L1_attn_b_b_proj)
    x = x + _L1_ffn_ref(_layernorm(x, axis=-1), L1_ffn_gate_weight, L1_ffn_gate_up_proj, L1_ffn_down_proj, L1_ffn_old_to_new)
    return x

_drawn_inputs = setup_inputs


def setup_inputs(seed=0):
    import zlib

    import numpy as np

    out = dict(_drawn_inputs(seed))
    spreads = {'L0_attn_a_D': (1.0, 0.6),
     'L0_ffn_gate_b': (0.0, 0.8),
     'L0_ffn_b_gate': (0.0, 2.0),
     'L0_ffn_b_up': (0.0, 2.0),
     'L0_ffn_b_down': (0.0, 0.8),
     'L1_attn_a_s': (0.0, 2.0),
     'L1_attn_b_b_lat': (0.0, 0.8),
     'L1_attn_b_b_d': (0.0, 2.0),
     'L1_attn_b_b_proj': (0.0, 0.8)}
    factors = {'L0_attn_a_in_proj_w': 8.0,
     'L0_attn_a_conv_w': 8.0,
     'L0_attn_a_conv_b': 8.0,
     'L0_attn_a_x_proj_w': 8.0,
     'L0_attn_a_dt_proj_w': 8.0,
     'L0_attn_a_dt_proj_b': 8.0,
     'L0_attn_a_A_log': 8.0,
     'L0_attn_a_out_proj_w': 8.0,
     'L0_ffn_w_up': 33.256,
     'L1_attn_b_W_d': 64.0,
     'L1_ffn_gate_weight': 8.0,
     'L1_ffn_gate_up_proj': 8.0,
     'L1_ffn_down_proj': 8.0,
     'L0_attn_b_w_atten': 8.0,
     'L0_attn_b_w_proj': 8.0,
     'L0_ffn_gate_w': 8.0,
     'L0_ffn_w_gate': 8.0,
     'L0_ffn_w_down': 8.0,
     'L1_attn_a_W_qkv': 8.0,
     'L1_attn_a_W_out': 8.0,
     'L1_attn_b_W_lat': 8.0,
     'L1_attn_b_W_proj': 8.0}
    for name, (base, spread) in spreads.items():
        noise = np.random.default_rng([zlib.crc32(name.encode()), seed]).standard_normal(out[name].shape)
        drawn = base * np.exp(spread * noise) if base else spread * noise
        out[name] = jnp.asarray(drawn.astype(out[name].dtype))
    for name, factor in factors.items():
        out[name] = (out[name] * factor).astype(out[name].dtype)
    return out
```

```python
from contextlib import ExitStack

import numpy as np

import concourse.bass as bass
from concourse import mybir
from concourse.alu_op_type import AluOpType as ALU

F32 = mybir.dt.float32
BF16 = mybir.dt.bfloat16
I32 = mybir.dt.int32
U32 = mybir.dt.uint32
ACT = mybir.ActivationFunctionType
AX = mybir.AxisListType.X

P = 128
BATCH, SEQ, D_MODEL = 4, 512, 256
TOKENS = BATCH * SEQ
TILES = TOKENS // P
TPB = SEQ // P
KC = D_MODEL // P
LN_EPS = 1e-5
NEG = -1.0e30

D_INNER, D_STATE, D_CONV, DT_RANK = 512, 16, 4, 16
BLK = D_INNER // P
HALF = TOKENS // 2

M0_E, M0_K, M0_I = 32, 4, 128
M0_TILES = TOKENS * M0_K // P + M0_E
M1_E, M1_K, M1_I, M1_CAP, M1_OLD = 48, 8, 96, 96, 128
FAR = 1.0e6


class Counter:

    def __init__(self, ctx, nc, name, base=0):
        self.sem = ctx.enter_context(nc.semaphore(name))
        self.base = base

    def at(self, n):
        return self.base + n

    def counted(self, n):
        self.base += n


FROM_ONE = ("mb_fetched", "mb_conved", "mb_acted", "sc_scanned", "sc_out", "ex_rows_out0", "ex_rows_out1", "ex_rows_out2",
            "ex_rows_out3",
            "ex_y_kept") + tuple("at_" + n for n in (
                "kput", "vput", "kturned", "kkept", "qput", "qturned", "qkept", "scored", "exped", "turned",
                "kept_d", "kept_a", "summed", "normed", "ykept", "outp", "added"))


class Steps:

    def __init__(self, eng, counter):
        self.eng, self.counter, self.n, self.loop = eng, counter, 0, 0

    def then(self, instruction):
        self.n += 1
        instruction.then_inc(self.counter.sem, 1)
        self.eng.wait_ge(self.counter.sem, self.counter.at(self.loop + self.n))


class Core:
    pass


def setup(nc, ctx, t):
    c = Core()
    c.nc, c.t, c.ctx = nc, t, ctx
    c.counters = {n: Counter(ctx, nc, n, 1) for n in FROM_ONE}
    c.x = ctx.enter_context(nc.sbuf_tensor("residual", [P, TILES * D_MODEL], F32))
    c.ident = ctx.enter_context(nc.sbuf_tensor("ident", [P, P], F32))
    c.banks = [ctx.enter_context(nc.psum_tensor(f"bank{i}", [P, 512], F32)) for i in range(8)]
    c.zeros = ctx.enter_context(nc.sbuf_tensor("zeros", [P, 512], BF16))
    c.ones = ctx.enter_context(nc.sbuf_tensor("ones", [P, P], BF16))
    return c


def counter(c, name):
    if name not in c.counters:
        c.counters[name] = Counter(c.ctx, c.nc, name)
    return c.counters[name]


def load_residual(c):
    nc = c.nc
    FILL = 8192
    loaded, made, filled = counter(c, "x_loaded"), counter(c, "const_made"), counter(c, "filled")
    with nc.sbuf_tensor("blank", [P, FILL], F32) as blank, nc.Block() as block:

        @block.sync
        def _(sp):
            sp.dma_start(c.x[:, :].rearrange("p (t d) -> p t d", d=D_MODEL),
                         c.t["x"].rearrange("b (t p) d -> p (b t) d", p=P)).then_inc(loaded.sem, 16)
            sp.wait_ge(made.sem, 2)
            fills = 0
            for name in ("scratch_xs0", "scratch_xs1"):
                flat = c.t[name].rearrange("(p n) d -> p (n d)", p=P)
                for at in range(0, flat.shape[1], FILL):
                    n = min(FILL, flat.shape[1] - at)
                    sp.dma_start(flat[:, at:at + n], blank[:, 0:n]).then_inc(filled.sem, 16)
                    fills += 1
            sp.wait_ge(loaded.sem, 16)
            sp.wait_ge(filled.sem, 16 * fills)

        @block.vector
        def _(dve):
            for name in FROM_ONE:
                dve.sem_inc(c.counters[name].sem, 1)

        @block.gpsimd
        def _(pool):
            pool.memset(blank[:, :], 0.0).then_inc(made.sem, 1)
            pool.memset(c.ident[:, :], 0.0).then_inc(made.sem, 1)
            pool.memset(c.zeros[:, :], 0.0)
            pool.memset(c.ones[:, :], 1.0)
            pool.wait_ge(made.sem, 2)
            pool.affine_select(out=c.ident[:, :], in_=c.ident[:, :], compare_op=ALU.not_equal, fill=1.0,
                               base=0, pattern=[[-1, P]], channel_multiplier=1)
    loaded.counted(16)
    made.counted(2)


def store_residual(c):
    nc = c.nc
    stored = counter(c, "x_stored")
    with nc.Block() as block:

        @block.sync
        def _(sp):
            sp.dma_start(c.t["out"].rearrange("b (t p) d -> p (b t) d", p=P),
                         c.x[:, :].rearrange("p (t d) -> p t d", d=D_MODEL)).then_inc(stored.sem, 16)
            sp.wait_ge(stored.sem, 16)


def layer_norm(c, xnT, xn=None, loads=None):
    nc = c.nc
    own, root, stat = counter(c, "ln_own"), counter(c, "ln_root"), counter(c, "ln_stat")
    normed, turned, kept = counter(c, "ln_normed"), counter(c, "ln_turned"), counter(c, "ln_kept")
    with ExitStack() as s:
        sb = lambda name, shape: s.enter_context(nc.sbuf_tensor(name, shape, F32, allow_name_mangling=True))
        bn = sb("ln_bn", [P, TILES * 6])
        mean, var, tmp, rstd = (sb(n, [P, TILES]) for n in ("ln_mean", "ln_var", "ln_tmp", "ln_rstd"))
        stage = sb("ln_stage", [P, 2 * D_MODEL]) if xn is None else None
        bnv = bn[:, :].rearrange("p (t s) -> p t s", s=6)

        def normal(tile, u):
            if xn is None:
                return stage[:, u * D_MODEL:(u + 1) * D_MODEL]
            return xn[:, tile * D_MODEL:(tile + 1) * D_MODEL]

        with nc.Block() as block:
            if loads is not None:
                @block.sync
                def _(sp):
                    loads(sp)

            @block.vector
            def _(dve):
                st = Steps(dve, own)
                with dve.Fori(0, TILES) as i:
                    dve.bn_stats(bn[:, bass.ds(i * 6, 6)], c.x[:, bass.ds(i * D_MODEL, D_MODEL)]) \
                       .then_inc(stat.sem, 1)
                dve.wait_ge(stat.sem, stat.at(TILES))
                st.then(dve.tensor_tensor(mean[:, :], bnv[:, :, 1], bnv[:, :, 4], ALU.add))
                st.then(dve.tensor_tensor(tmp[:, :], bnv[:, :, 1], bnv[:, :, 4], ALU.subtract))
                st.then(dve.tensor_tensor(var[:, :], bnv[:, :, 2], bnv[:, :, 5], ALU.add))
                st.then(dve.tensor_tensor(tmp[:, :], tmp[:, :], tmp[:, :], ALU.mult))
                st.then(dve.tensor_scalar(var[:, :], var[:, :], 1.0 / D_MODEL, LN_EPS, ALU.mult, ALU.add))
                st.then(dve.tensor_scalar(mean[:, :], mean[:, :], 0.5, None, ALU.mult))
                st.then(dve.scalar_tensor_tensor(out=var[:, :], in0=tmp[:, :], scalar=0.25, in1=var[:, :],
                                                 op0=ALU.mult, op1=ALU.add))
                dve.wait_ge(root.sem, root.at(1))
                st.then(dve.reciprocal(rstd[:, :], tmp[:, :]))
                for i in range(TILES):
                    if i >= 2 and xn is None:
                        dve.wait_ge(turned.sem, turned.at(i - 1))
                    dve.tensor_scalar(normal(i, i % 2), c.x[:, i * D_MODEL:(i + 1) * D_MODEL],
                                      mean[:, i:i + 1], rstd[:, i:i + 1], ALU.subtract, ALU.mult) \
                       .then_inc(normed.sem, 1)

            @block.scalar
            def _(act):
                act.wait_ge(own.sem, own.at(7))
                act.activation(tmp[:, :], var[:, :], ACT.Sqrt).then_inc(root.sem, 1)
                for i in range(TILES):
                    act.wait_ge(turned.sem, turned.at(i + 1))
                    act.activation(xnT[:, :].rearrange("p (k n) -> p k n", k=KC)[:, :, i * P:(i + 1) * P],
                                   c.banks[i % 2][:, 0:KC * P].rearrange("p (k n) -> p k n", k=KC),
                                   ACT.Copy).then_inc(kept.sem, 1)

            @block.tensor
            def _(pe):
                for i in range(TILES):
                    pe.wait_ge(normed.sem, normed.at(i + 1))
                    if i >= 2:
                        pe.wait_ge(kept.sem, kept.at(i - 1))
                    src = normal(i, i % 2)
                    for k in range(KC):
                        last = pe.transpose(c.banks[i % 2][:, k * P:(k + 1) * P],
                                            src[:, k * P:(k + 1) * P], c.ident[:, :])
                    last.then_inc(turned.sem, 1)
    own.counted(8)
    root.counted(1)
    stat.counted(TILES)
    for q in (normed, turned, kept):
        q.counted(TILES)


def mamba(c):
    nc, t = c.nc, c.t
    with ExitStack() as s:
        sb = lambda name, shape, dt=F32: s.enter_context(nc.sbuf_tensor(name, shape, dt))
        xact = sb("mb_xact", [P, BLK * TOKENS])
        zgate = sb("mb_zgate", [P, BLK * TOKENS])
        cw, cb = sb("mb_conv_w", [P, BLK * D_CONV]), sb("mb_conv_b", [P, BLK])
        a_coef = sb("mb_a", [P, BLK * D_STATE])
        dskip, dtb = sb("mb_d", [P, BLK]), sb("mb_dt_b", [P, BLK])
        w_x = sb("mb_w_x", [P, BLK * 48])
        w_dt = sb("mb_w_dt", [DT_RANK, D_INNER])
        w_out = sb("mb_w_out", [P, BLK * D_MODEL])
        loaded = counter(c, "mb_loaded")
        inner = s.enter_context(ExitStack())
        xnT = inner.enter_context(nc.sbuf_tensor("mb_xnT", [P, KC * TOKENS], F32))
        w_in = inner.enter_context(nc.sbuf_tensor("mb_w_in", [P, KC * 2 * D_INNER], F32))
        LOADS = [
            (w_in[:, :].rearrange("p (k e) -> p k e", k=KC), t["in_wT"].rearrange("(k p) e -> p k e", p=P)),
            (cw[:, :].rearrange("p (b k) -> p b k", b=BLK), t["conv_w"].rearrange("(b p) k -> p b k", p=P)),
            (cb[:, :], t["conv_b"]), (dskip[:, :], t["D"]), (dtb[:, :], t["dt_b"]),
            (a_coef[:, :].rearrange("p (b n) -> p b n", b=BLK), t["A_log"].rearrange("(b p) n -> p b n", p=P)),
            (w_x[:, :].rearrange("p (b e) -> p b e", b=BLK), t["x_wT"].rearrange("(b p) e -> p b e", p=P)),
            (w_dt[:, :], t["dt_wT"]),
            (w_out[:, :].rearrange("p (b e) -> p b e", b=BLK), t["out_wT"].rearrange("(b p) e -> p b e", p=P)),
        ]

        def loads(sp):
            for dst, src in LOADS:
                sp.dma_start(dst, src).then_inc(loaded.sem, 16)

        layer_norm(c, xnT, loads=loads)

        proj, fetched, padded = counter(c, "mb_proj"), counter(c, "mb_fetched"), counter(c, "mb_padded")
        own, conved, acted = counter(c, "mb_own"), counter(c, "mb_conved"), counter(c, "mb_acted")
        LEAD = D_CONV - 1
        WP = LEAD + SEQ
        with ExitStack() as q:
            xp = q.enter_context(nc.sbuf_tensor("mb_xpad", [P, 2 * WP], F32))
            cv = q.enter_context(nc.sbuf_tensor("mb_cv", [P, 2 * SEQ], F32))
            with nc.Block() as block:

                @block.tensor
                def _(pe):
                    pe.wait_ge(loaded.sem, loaded.at(16 * len(LOADS)))
                    for eb in range(2 * BLK):
                        with pe.Fori(0, BATCH // 2) as j:
                            for u in range(2):
                                n = eb * BATCH + j * 2 + u
                                if eb > 0:
                                    pe.wait_ge(fetched.sem, fetched.at(n - 1))
                                else:
                                    pe.wait_ge(fetched.sem, fetched.at(j * 2))
                                for k in range(KC):
                                    last = pe.matmul(c.banks[u][:, :],
                                                     w_in[:, k * 2 * D_INNER + eb * P:k * 2 * D_INNER + (eb + 1) * P],
                                                     xnT[:, bass.ds(j * (2 * SEQ) + (k * TOKENS + u * SEQ), SEQ)],
                                                     start=(k == 0), stop=(k == KC - 1))
                                last.then_inc(proj.sem, 1)

                @block.scalar
                def _(act):
                    for b in range(BLK):
                        with act.Fori(0, BATCH // 2) as j:
                            for u in range(2):
                                n = b * BATCH + j * 2 + u
                                act.wait_ge(proj.sem, proj.at(n + 1))
                                if b == 0:
                                    act.wait_ge(conved.sem, conved.at(j * 2))
                                else:
                                    act.wait_ge(conved.sem, conved.at(n - 1))
                                act.activation(xp[:, u * WP + LEAD:(u + 1) * WP], c.banks[u][:, :],
                                               ACT.Copy).then_inc(fetched.sem, 1)
                            for u in range(2):
                                n = b * BATCH + j * 2 + u
                                act.wait_ge(conved.sem, conved.at(n + 1))
                                act.activation(xact[:, bass.ds(j * (2 * SEQ) + (b * TOKENS + u * SEQ), SEQ)],
                                               cv[:, u * SEQ:(u + 1) * SEQ], ACT.Silu).then_inc(acted.sem, 1)
                    for b in range(BLK):
                        with act.Fori(0, BATCH // 2) as j:
                            for u in range(2):
                                act.wait_ge(proj.sem, proj.at((BLK + b) * BATCH + j * 2 + u + 1))
                                act.activation(zgate[:, bass.ds(j * (2 * SEQ) + (b * TOKENS + u * SEQ), SEQ)],
                                               c.banks[u][:, :], ACT.Silu).then_inc(fetched.sem, 1)

                @block.vector
                def _(dve):
                    dve.wait_ge(loaded.sem, loaded.at(16 * len(LOADS)))
                    for u in range(2):
                        dve.memset(xp[:, u * WP:u * WP + LEAD], 0.0).then_inc(padded.sem, 1)
                    dve.wait_ge(padded.sem, padded.at(2))
                    for b in range(BLK):
                        with dve.Fori(0, BATCH // 2) as j:
                            for u in range(2):
                                n = b * BATCH + j * 2 + u
                                st = Steps(dve, own)
                                st.loop = n * (D_CONV - 1)
                                dst = cv[:, u * SEQ:(u + 1) * SEQ]
                                tap = lambda k: cw[:, b * D_CONV + k:b * D_CONV + k + 1]
                                dve.wait_ge(fetched.sem, fetched.at(n + 1))
                                if b == 0:
                                    dve.wait_ge(acted.sem, acted.at(j * 2))
                                else:
                                    dve.wait_ge(acted.sem, acted.at(n - 1))
                                st.then(dve.tensor_scalar(dst, xp[:, u * WP + LEAD:(u + 1) * WP], tap(LEAD),
                                                          cb[:, b:b + 1], ALU.mult, ALU.add))
                                for k in reversed(range(LEAD)):
                                    op = dve.scalar_tensor_tensor(
                                        out=dst, in0=xp[:, u * WP + k:u * WP + k + SEQ], scalar=tap(k),
                                        in1=dst, op0=ALU.mult, op1=ALU.add)
                                    if k:
                                        st.then(op)
                                    else:
                                        op.then_inc(conved.sem, 1)
        proj.counted(2 * BLK * BATCH)
        fetched.counted(2 * BLK * BATCH)
        padded.counted(2)
        own.counted(BLK * BATCH * (D_CONV - 1))
        conved.counted(BLK * BATCH)
        acted.counted(BLK * BATCH)
        inner.close()

        dt = sb("mb_dt", [P, BLK * TOKENS])
        ux = sb("mb_ux", [P, BLK * TOKENS])
        bcT = t["scratch_bc"]
        xdbl, xkept, stored = counter(c, "mb_xdbl"), counter(c, "mb_xkept"), counter(c, "mb_bc_stored")
        dtp, dtr = counter(c, "mb_dtp"), counter(c, "mb_dtr")
        soft, summed = counter(c, "mb_soft"), counter(c, "mb_summed")
        with ExitStack() as q:
            dbl = q.enter_context(nc.sbuf_tensor("mb_dbl", [48, TOKENS], F32))
            with nc.Block() as block:

                @block.tensor
                def _(pe):
                    for b in range(BATCH):
                        if b >= 2:
                            pe.wait_ge(xkept.sem, xkept.at(b - 1))
                        for k in range(BLK):
                            last = pe.matmul(c.banks[b % 2][0:48, :], w_x[:, k * 48:(k + 1) * 48],
                                             xact[:, k * TOKENS + b * SEQ:k * TOKENS + (b + 1) * SEQ],
                                             start=(k == 0), stop=(k == BLK - 1))
                        last.then_inc(xdbl.sem, 1)
                    pe.wait_ge(xkept.sem, xkept.at(BATCH))
                    for n in range(BLK * BATCH):
                        k, b = divmod(n, BATCH)
                        if n >= 2:
                            pe.wait_ge(dtr.sem, dtr.at(2 * (n - 1)))
                        pe.matmul(c.banks[2 + n % 2][:, :], w_dt[:, k * P:(k + 1) * P],
                                  dbl[0:DT_RANK, b * SEQ:(b + 1) * SEQ], start=True, stop=True) \
                          .then_inc(dtp.sem, 1)

                @block.vector
                def _(dve):
                    for n in range(BLK * BATCH):
                        k = n // BATCH
                        at = slice(n * SEQ, (n + 1) * SEQ)
                        dve.wait_ge(dtp.sem, dtp.at(n + 1))
                        dve.tensor_scalar(ux[:, at], c.banks[2 + n % 2][:, :], dtb[:, k:k + 1], 0.0,
                                          ALU.add, ALU.max).then_inc(dtr.sem, 1)
                        dve.wait_ge(dtr.sem, dtr.at(2 * n + 1))
                        dve.scalar_tensor_tensor(out=dt[:, at], in0=ux[:, at], scalar=-2.0,
                                                 in1=c.banks[2 + n % 2][:, :], op0=ALU.mult, op1=ALU.add) \
                           .then_inc(dtr.sem, 1)
                    for k in range(BLK):
                        at = slice(k * TOKENS, (k + 1) * TOKENS)
                        dve.wait_ge(soft.sem, soft.at(2 + BLK + k + 1))
                        dve.tensor_tensor(dt[:, at], dt[:, at], ux[:, at], ALU.add).then_inc(summed.sem, 1)
                        dve.wait_ge(summed.sem, summed.at(k + 1))
                        dve.tensor_tensor(ux[:, at], dt[:, at], xact[:, at], ALU.mult)

                @block.scalar
                def _(act):
                    for b in range(BATCH):
                        act.wait_ge(xdbl.sem, xdbl.at(b + 1))
                        act.activation(dbl[:, b * SEQ:(b + 1) * SEQ], c.banks[b % 2][0:48, :],
                                       ACT.Copy).then_inc(xkept.sem, 1)
                    act.activation(a_coef[:, :], a_coef[:, :], ACT.Exp).then_inc(soft.sem, 1)
                    act.wait_ge(soft.sem, soft.at(1))
                    act.activation(a_coef[:, :], a_coef[:, :], ACT.Copy, scale=-1.0).then_inc(soft.sem, 1)
                    for k in range(BLK):
                        at = slice(k * TOKENS, (k + 1) * TOKENS)
                        act.wait_ge(dtr.sem, dtr.at(2 * (k + 1) * BATCH))
                        act.activation(dt[:, at], dt[:, at], ACT.Exp, bias=dtb[:, k:k + 1]).then_inc(soft.sem, 1)
                    for k in range(BLK):
                        at = slice(k * TOKENS, (k + 1) * TOKENS)
                        act.wait_ge(soft.sem, soft.at(2 + k + 1))
                        act.activation(dt[:, at], dt[:, at], ACT.Ln, bias=1.0).then_inc(soft.sem, 1)

                @block.sync
                def _(sp):
                    sp.wait_ge(xkept.sem, xkept.at(BATCH))
                    sp.dma_start(bcT, dbl[DT_RANK:48, :]).then_inc(stored.sem, 16)
                    sp.wait_ge(stored.sem, stored.at(16))
        for q, n in ((xdbl, BATCH), (xkept, BATCH), (stored, 16), (dtp, BLK * BATCH),
                     (dtr, 2 * BLK * BATCH), (soft, 2 + 2 * BLK), (summed, BLK)):
            q.counted(n)

        mamba_scan(c, xact, zgate, dt, ux, a_coef, dskip, bcT)

        outp, added = counter(c, "mb_outp"), counter(c, "mb_added")
        with nc.Block() as block:

            @block.tensor
            def _(pe):
                for i in range(TILES):
                    if i >= 2:
                        pe.wait_ge(added.sem, added.at(i - 1))
                    for k in range(BLK):
                        last = pe.matmul(c.banks[i % 2][:, 0:D_MODEL],
                                         xact[:, k * TOKENS + i * P:k * TOKENS + (i + 1) * P],
                                         w_out[:, k * D_MODEL:(k + 1) * D_MODEL],
                                         start=(k == 0), stop=(k == BLK - 1))
                    last.then_inc(outp.sem, 1)

            @block.vector
            def _(dve):
                for i in range(TILES):
                    at = slice(i * D_MODEL, (i + 1) * D_MODEL)
                    dve.wait_ge(outp.sem, outp.at(i + 1))
                    dve.tensor_tensor(c.x[:, at], c.x[:, at], c.banks[i % 2][:, 0:D_MODEL],
                                      ALU.add).then_inc(added.sem, 1)
        outp.counted(TILES)
        added.counted(TILES)


def mamba_scan(c, xact, zgate, dt, ux, a_coef, dskip, bcT):
    nc = c.nc
    ST = BLK * D_STATE
    NH = 3
    rows = [counter(c, f"sc_rows{u}") for u in range(2)]
    decay, input_, scanned = (counter(c, n) for n in ("sc_decay", "sc_input", "sc_scanned"))
    used, out, opened, edge = (counter(c, n) for n in ("sc_used", "sc_out", "sc_opened", "sc_edge"))
    summed, gated, own = counter(c, "sc_summed"), counter(c, "sc_gated"), counter(c, "sc_own")
    with ExitStack() as s:
        sb = lambda name, shape, dt=F32: s.enter_context(nc.sbuf_tensor(name, shape, dt))
        da = sb("sc_da", [P, 2 * HALF])
        hb = sb("sc_h", [P, 4 * HALF])
        bc = sb("sc_bc", [P, 4 * HALF])
        DA = [da[:, u * HALF:(u + 1) * HALF] for u in range(2)]
        H = [hb[:, u * HALF:(u + 1) * HALF] for u in range(4)]
        B = [bc[:, u * 2 * HALF:u * 2 * HALF + HALF] for u in range(2)]
        C = [bc[:, u * 2 * HALF + HALF:(u + 1) * 2 * HALF] for u in range(2)]
        POOL_B = (0,)
        for half in range(2):
            lo = half * HALF
            with nc.Block() as block:

                @block.sync
                def _(sp):
                    def fetch(n, u):
                        for dst, row in ((B[u], n), (C[u], n + D_STATE)):
                            sp.dma_start(dst, bcT[bass.ds(row, 1), lo:lo + HALF].to_broadcast([P, HALF])) \
                              .then_inc(rows[u].sem, 16)

                    for u in range(2):
                        fetch(u, u)
                    with sp.Fori(0, D_STATE // 2 - 1) as j:
                        for u in range(2):
                            sp.wait_ge(used.sem, used.at(j * (2 * BLK) + (u + 1) * BLK))
                            fetch(j * 2 + (u + 2), u)

                @block.scalar
                def _(act):
                    with act.Fori(0, D_STATE // 2) as j:
                        for v in range(2 * BLK):
                            n, b = divmod(v, BLK)
                            step = j * (2 * BLK) + v
                            if v >= 2:
                                act.wait_ge(scanned.sem, scanned.at(step - 1))
                            else:
                                act.wait_ge(scanned.sem, scanned.at(j * (2 * BLK)))
                            act.wait_ge(edge.sem, edge.at(2))
                            act.activation(
                                DA[v % 2].rearrange("p (b t) -> p b t", b=2)[:, :, 1:SEQ],
                                dt[:, b * TOKENS + lo:b * TOKENS + lo + HALF]
                                .rearrange("p (b t) -> p b t", b=2)[:, :, 1:SEQ],
                                ACT.Exp, scale=a_coef[:, bass.ds(j * 2 + (b * D_STATE + n), 1)]) \
                               .then_inc(decay.sem, 1)

                @block.gpsimd
                def _(pool):
                    with pool.Fori(0, D_STATE // 2) as j:
                        for v in range(2 * BLK):
                            n, b = divmod(v, BLK)
                            step = j * (2 * BLK) + v
                            if b in POOL_B:
                                pool.wait_ge(rows[n].sem, rows[n].at(j * 32 + 32))
                                if v >= 4:
                                    pool.wait_ge(out.sem, out.at(step - 3))
                                else:
                                    pool.wait_ge(out.sem, out.at(j * (2 * BLK)))
                                pool.tensor_tensor(H[v % 4], ux[:, b * TOKENS + lo:b * TOKENS + lo + HALF],
                                                   B[n], ALU.mult).then_inc(input_.sem, 1)
                            pool.wait_ge(scanned.sem, scanned.at(step + 1))
                            pool.tensor_tensor(H[v % 4], H[v % 4], C[n], ALU.mult).then_inc(used.sem, 1)

                @block.vector
                def _(dve):
                    for u in range(2):
                        dve.memset(DA[u].rearrange("p (b t) -> p b t", b=2)[:, :, 0:1], 0.0) \
                           .then_inc(edge.sem, 1)
                    dve.wait_ge(edge.sem, edge.at(2))
                    with dve.Fori(0, D_STATE // 2) as j:
                        for v in range(2 * BLK):
                            n, b = divmod(v, BLK)
                            step = j * (2 * BLK) + v
                            if b in POOL_B:
                                dve.wait_ge(input_.sem, input_.at(j * (2 * len(POOL_B)) + n + 1))
                            else:
                                dve.wait_ge(rows[n].sem, rows[n].at(j * 32 + 32))
                                if v >= 4:
                                    dve.wait_ge(out.sem, out.at(step - 3))
                                else:
                                    dve.wait_ge(out.sem, out.at(j * (2 * BLK)))
                                dve.tensor_tensor(H[v % 4], ux[:, b * TOKENS + lo:b * TOKENS + lo + HALF],
                                                  B[n], ALU.mult).then_inc(own.sem, 1)
                                dve.wait_ge(own.sem, own.at(j * (2 * (BLK - 1)) + n * (BLK - 1) + b))
                            dve.wait_ge(decay.sem, decay.at(step + 1))
                            dve.tensor_tensor_scan(H[v % 4], DA[v % 2], H[v % 4], 0.0, ALU.mult, ALU.add) \
                               .then_inc(scanned.sem, 1)
                    for b in range(BLK):
                        at = slice(b * TOKENS + lo, b * TOKENS + lo + HALF)
                        for q in range(2):
                            cut = slice(b * TOKENS + lo + q * SEQ, b * TOKENS + lo + (q + 1) * SEQ)
                            dve.wait_ge(summed.sem, summed.at(1))
                            dve.scalar_tensor_tensor(out=xact[:, cut], in0=xact[:, cut],
                                                     scalar=dskip[:, b:b + 1], in1=c.banks[2 * b + q][:, :],
                                                     op0=ALU.mult, op1=ALU.add).then_inc(gated.sem, 1)
                    dve.wait_ge(gated.sem, gated.at(2 * BLK))
                    for b in range(BLK):
                        at = slice(b * TOKENS + lo, b * TOKENS + lo + HALF)
                        dve.tensor_tensor(xact[:, at], xact[:, at], zgate[:, at], ALU.mult)

                @block.tensor
                def _(pe):
                    for k in range(8):
                        pe.matmul(c.banks[k][:, :], c.zeros[:, 0:P], c.zeros[:, :], start=True, stop=False)
                    with pe.Fori(0, D_STATE // 2) as j:
                        for v in range(2 * BLK):
                            b = v % BLK
                            pe.wait_ge(used.sem, used.at(j * (2 * BLK) + v + 1))
                            for q in range(2):
                                last = pe.matmul(c.banks[2 * b + q][:, :], c.ident[:, :],
                                                 H[v % 4][:, q * SEQ:(q + 1) * SEQ], start=False, stop=False)
                            last.then_inc(out.sem, 1)
                    for k in range(8):
                        last = pe.matmul(c.banks[k][:, :], c.zeros[:, 0:P], c.zeros[:, :], start=False, stop=True)
                    last.then_inc(summed.sem, 1)
            for q, n in ((rows[0], 16 * D_STATE), (rows[1], 16 * D_STATE), (decay, ST), (scanned, ST), (used, ST), (out, ST), (edge, 2),
                         (input_, len(POOL_B) * D_STATE), (own, (BLK - len(POOL_B)) * D_STATE),
                         (summed, 1), (gated, 2 * BLK)):
                q.counted(n)


def moe(c, which):
    nc, t = c.nc, c.t
    if which == 0:
        E, K, I, ROWS, NT, cap = M0_E, M0_K, M0_I, P, M0_TILES, None
    else:
        E, K, I, ROWS, NT, cap = M1_E, M1_K, M1_I, M1_CAP, M1_E, M1_CAP
    xs, ys = t[f"scratch_xs{which}"], t[f"scratch_ys{which}"]
    GU = 2 * I
    TK = TILES * K
    EB = -(-E * TILES // 512)
    TPBANK = TILES // EB
    with ExitStack() as s:
        sb = lambda name, shape, dt=F32: s.enter_context(nc.sbuf_tensor(name, shape, dt, allow_name_mangling=True))
        slots = sb("mo_slots", [P, TK], I32)
        weights = sb("mo_weights", [P, TK])
        tile_expert = sb("mo_tile_expert", [1, NT], I32) if cap is None else None
        w_gu = sb("mo_w_gu", [P, E * KC * GU])
        w_dn = sb("mo_w_dn", [I, E * D_MODEL])
        if which == 0:
            b_gu, b_dn = sb("mo_b_gu", [3, E * GU], BF16), sb("mo_b_dn", [3, E * D_MODEL], BF16)
        loaded, weights_in = counter(c, "mo_loaded"), counter(c, "mo_weights_in")
        scope = s.enter_context(ExitStack())
        sc = lambda name, shape, dt=F32: scope.enter_context(nc.sbuf_tensor(name, shape, dt, allow_name_mangling=True))
        xn = sc("mo_xn", [P, TILES * D_MODEL])
        gate = sc("mo_gate", [P, KC * E])
        bias = sc("mo_gate_b", [P, E])
        if which == 0:
            braw = sc("mo_braw", [E, GU + D_MODEL])
        else:
            gold, o2n = sc("mo_gold", [M1_OLD, D_MODEL]), sc("mo_o2n", [M1_OLD, 1], I32)
        WEIGHTS = [(w_gu[:, :], t[f"w_gu{which}"]), (w_dn[:, :], t[f"w_dn{which}"])]
        if which == 0:
            LOADS = [(gate[:, :].rearrange("p (k e) -> p k e", k=KC), t["gate0T"].rearrange("(k p) e -> p k e", p=P)),
                      (bias[:, :], t["gate_b"].to_broadcast([P, E])), (braw[:, :], t["b_all"])]
        else:
            LOADS = [(gold[:, :], t["gate1"]), (o2n[:, :], t["o2n"])]

        def loads(sp):
            for dst, src in LOADS:
                sp.dma_start(dst, src).then_inc(loaded.sem, 16)
            for dst, src in WEIGHTS:
                sp.dma_start(dst, src).then_inc(weights_in.sem, 16)
            sp.wait_ge(loaded.sem, loaded.at(16 * len(LOADS)))

        logit, ldone, own, pown = (counter(c, n) for n in ("mo_logit", "mo_ldone", "mo_own", "mo_pown"))
        made, ranked, expd, counted_, moved, bsplit, bstored = (
            counter(c, n) for n in ("mo_made", "mo_ranked", "mo_expd", "mo_counted", "mo_moved", "mo_bsplit", "mo_bstored"))
        placed = counter(c, "mo_placed")
        with ExitStack() as q:
            sq = lambda name, shape, dt=F32: q.enter_context(nc.sbuf_tensor(name, shape, dt, allow_name_mangling=True))
            lg = sq("mo_lg", [P, TILES * E])
            iota_e = sq("mo_iota_e", [P, E])
            with ExitStack() as qq:
                xnT = qq.enter_context(nc.sbuf_tensor("mo_xnT", [P, KC * TOKENS], F32, allow_name_mangling=True))
                layer_norm(c, xnT, xn=xn, loads=loads)
                if which == 1:
                    remap_gate(c, gold, o2n, iota_e, gate, bias)
                with nc.Block() as block:

                    @block.tensor
                    def _(pe):
                        for i in range(TILES):
                            for k in range(KC):
                                last = pe.matmul(c.banks[i // TPBANK][:, (i % TPBANK) * E:(i % TPBANK + 1) * E],
                                                 xnT[:, k * TOKENS + i * P:k * TOKENS + (i + 1) * P],
                                                 gate[:, k * E:(k + 1) * E], start=(k == 0), stop=(k == KC - 1))
                        last.then_inc(logit.sem, 1)

                    @block.vector
                    def _(dve):
                        dve.wait_ge(logit.sem, logit.at(1))
                        for g in range(EB):
                            cut = slice(g * TPBANK * E, (g + 1) * TPBANK * E)
                            dve.tensor_tensor(lg[:, cut].rearrange("p (t e) -> p t e", e=E),
                                              c.banks[g][:, 0:TPBANK * E].rearrange("p (t e) -> p t e", e=E),
                                              bias[:, :].rearrange("p (t e) -> p t e", t=1)
                                              .to_broadcast([P, TPBANK, E]), ALU.add).then_inc(ldone.sem, 1)
            logit.counted(1)
            ldone.counted(EB)
            upper = sq("mo_upper", [P, P], BF16)
            top, topi, topf = sq("mo_top", [P, TILES * 8]), sq("mo_topi", [P, TILES * 8], U32), sq("mo_topf", [P, TK])
            hot = sq("mo_hot", [P, TK * E])
            mask = sq("mo_mask", [P, TILES * E], BF16)
            reset = sq("mo_reset", [P, E * TILES])
            incl = sq("mo_incl", [P, E * TILES])
            pos = sq("mo_pos", [P, TILES * E])
            cnt, nt, start, off = (sq(n, [P, E]) for n in ("mo_cnt", "mo_nt", "mo_start", "mo_off"))
            ssum = sq("mo_ssum", [P, TILES])
            slotf = sq("mo_slotf", [P, TK])
            te = lambda a: a[:, :].rearrange("p (t e) -> p t e", e=E)
            et = lambda a: a[:, :].rearrange("p (e t) -> p e t", t=TILES)
            if cap is None:
                steps16 = sq("mo_steps16", [P, E * TILES])
                over = sq("mo_over", [P, E * TILES])
                tile_id = sq("mo_tile_id", [NT, 1])
                before = sq("mo_before", [NT, E])
                texp = sq("mo_texp", [NT, 1])
                bparts = [sq(f"mo_bpart{i}", [E, GU + D_MODEL], BF16) for i in range(3)]

            with nc.Block() as block:

                @block.gpsimd
                def _(pool):
                    small = dict(allow_small_or_imprecise_dtypes=True)
                    pool.iota(iota_e[:, :], [[1, E]], 0, 0, **small).then_inc(made.sem, 1)
                    pool.memset(reset[:, :], 1.0).then_inc(pown.sem, 1)
                    pool.wait_ge(pown.sem, pown.at(1))
                    pool.memset(et(reset)[:, :, 0:1], 0.0)
                    pool.memset(upper[:, :], 1.0).then_inc(pown.sem, 1)
                    pool.wait_ge(pown.sem, pown.at(2))
                    pool.affine_select(out=upper[:, :], in_=upper[:, :], compare_op=ALU.is_gt, fill=0.0,
                                       base=0, pattern=[[1, P]], channel_multiplier=-1).then_inc(made.sem, 1)
                    if cap is None:
                        pool.iota(steps16[:, :], [[0, E], [ROWS, TILES]], 0, 0, **small).then_inc(made.sem, 1)
                        pool.iota(tile_id[:, :], [[0, 1]], 0, 1, **small).then_inc(made.sem, 1)
                    else:
                        pool.iota(off[:, :], [[ROWS, E]], 0, 0, **small).then_inc(made.sem, 2)

                @block.tensor
                def _(pe):
                    pe.wait_ge(ranked.sem, ranked.at(1))
                    pe.wait_ge(made.sem, made.at(4))
                    for g in range(EB):
                        cut = slice(g * TPBANK * E, (g + 1) * TPBANK * E)
                        pe.matmul(c.banks[g][:, 0:TPBANK * E], upper[:, :], mask[:, cut], start=True, stop=True)
                        last = pe.matmul(c.banks[EB + g][:, 0:TPBANK * E], c.ones[:, :], mask[:, cut],
                                         start=True, stop=True)
                    last.then_inc(counted_.sem, 1)
                    if cap is None:
                        pe.wait_ge(placed.sem, placed.at(1))
                        pe.matmul(c.banks[7][0:1, 0:NT], texp[:, :], c.ident[0:NT, 0:NT], start=True, stop=True) \
                          .then_inc(placed.sem, 1)

                @block.scalar
                def _(act):
                    act.wait_ge(expd.sem, expd.at(1))
                    act.activation(weights[:, :], weights[:, :], ACT.Exp).then_inc(expd.sem, 1)

                if which == 0:
                    @block.sync
                    def _(sp):
                        sp.wait_ge(bsplit.sem, bsplit.at(5))
                        for i in range(3):
                            sp.dma_start(b_gu[i:i + 1, :].rearrange("a (e n) -> a e n", e=E),
                                         bparts[i][:, 0:GU]) \
                              .then_inc(bstored.sem, 16)
                            sp.dma_start(b_dn[i:i + 1, :].rearrange("a (e n) -> a e n", e=E),
                                         bparts[i][:, GU:]) \
                              .then_inc(bstored.sem, 16)
                        sp.wait_ge(bstored.sem, bstored.at(96))

                @block.vector
                def _(dve):
                    st = Steps(dve, own)
                    if which == 0:
                        sp_ = Steps(dve, bsplit)
                        sp_.then(dve.tensor_copy(bparts[0][:, :], braw[:, :]))
                        sp_.then(dve.tensor_tensor(braw[:, :], braw[:, :], bparts[0][:, :], ALU.subtract))
                        sp_.then(dve.tensor_copy(bparts[1][:, :], braw[:, :]))
                        sp_.then(dve.tensor_tensor(braw[:, :], braw[:, :], bparts[1][:, :], ALU.subtract))
                        sp_.then(dve.tensor_copy(bparts[2][:, :], braw[:, :]))
                    for i in range(TILES):
                        dve.max(top[:, i * 8:(i + 1) * 8], lg[:, i * E:(i + 1) * E]).then_inc(own.sem, 1)
                    dve.wait_ge(own.sem, own.at(TILES))
                    for i in range(TILES):
                        dve.max_index(topi[:, i * 8:(i + 1) * 8], top[:, i * 8:(i + 1) * 8],
                                      lg[:, i * E:(i + 1) * E]).then_inc(own.sem, 1)
                    dve.wait_ge(own.sem, own.at(2 * TILES))
                    st.n = 2 * TILES
                    top3 = top[:, :].rearrange("p (t k) -> p t k", k=8)
                    wk = weights[:, :].rearrange("p (t k) -> p t k", k=K)
                    st.then(dve.tensor_copy(topf[:, :].rearrange("p (t k) -> p t k", k=K),
                                            topi[:, :].rearrange("p (t k) -> p t k", k=8)[:, :, 0:K]))
                    dve.tensor_tensor(wk, top3[:, :, 0:K], top3[:, :, 0:1].to_broadcast([P, TILES, K]),
                                      ALU.subtract).then_inc(expd.sem, 1)
                    dve.wait_ge(made.sem, made.at(1))
                    hot3 = hot[:, :].rearrange("p (n e) -> p n e", e=E)
                    st.then(dve.tensor_tensor(
                        hot3, topf[:, :].rearrange("p (n o) -> p n o", o=1).to_broadcast([P, TK, E]),
                        iota_e[:, :].rearrange("p (o e) -> p o e", o=1).to_broadcast([P, TK, E]), ALU.is_equal))
                    hot4 = hot[:, :].rearrange("p (t k e) -> p t k e", k=K, e=E)
                    for k in range(1, K):
                        if k == 1:
                            st.then(dve.tensor_tensor(te(mask), hot4[:, :, 0, :], hot4[:, :, 1, :], ALU.add))
                        else:
                            op = dve.tensor_tensor(te(mask), te(mask), hot4[:, :, k, :], ALU.add)
                            if k < K - 1:
                                st.then(op)
                            else:
                                op.then_inc(ranked.sem, 1)
                    dve.wait_ge(expd.sem, expd.at(2))
                    st.then(dve.tensor_reduce(ssum[:, :], wk, AX, ALU.add))
                    st.then(dve.reciprocal(ssum[:, :], ssum[:, :]))
                    st.then(dve.tensor_tensor(wk, wk, ssum[:, :].rearrange("p (t o) -> p t o", o=1)
                                              .to_broadcast([P, TILES, K]), ALU.mult))
                    dve.wait_ge(made.sem, made.at(4))
                    dve.wait_ge(counted_.sem, counted_.at(1))
                    for g in range(EB):
                        st.then(dve.tensor_copy(
                            et(incl)[:, :, g * TPBANK:(g + 1) * TPBANK],
                            c.banks[EB + g][:, 0:TPBANK * E].rearrange("p (t e) -> p e t", e=E)))
                    st.then(dve.tensor_copy(pos[:, :].rearrange("p (t e) -> p e t", e=E), et(incl)))
                    st.then(dve.tensor_tensor_scan(incl[:, :], reset[:, :], incl[:, :], 0.0, ALU.mult, ALU.add))
                    st.then(dve.tensor_tensor(te(pos), incl[:, :].rearrange("p (e t) -> p t e", t=TILES),
                                              te(pos), ALU.subtract))
                    for g in range(EB):
                        cut = slice(g * TPBANK * E, (g + 1) * TPBANK * E)
                        st.then(dve.tensor_tensor(pos[:, cut], pos[:, cut], c.banks[g][:, 0:TPBANK * E], ALU.add))
                    whole = lambda a, n: a.rearrange("p (o e) -> p o e", o=1).to_broadcast([a.shape[0], n, E])
                    if cap is None:
                        st.then(dve.tensor_copy(cnt[:, :], et(incl)[:, :, TILES - 1]))
                        st.then(dve.tensor_tensor(et(over), cnt[:, :].rearrange("p (e o) -> p e o", o=1)
                                                  .to_broadcast([P, E, TILES]), et(steps16), ALU.is_gt))
                        st.then(dve.tensor_reduce(nt[:, :], et(over), AX, ALU.add))
                        st.then(dve.memset(cnt[:, :], 1.0))
                        st.then(dve.tensor_tensor_scan(start[:, :], cnt[:, :], nt[:, :], 0.0, ALU.mult, ALU.add))
                        st.then(dve.tensor_tensor(start[:, :], start[:, :], nt[:, :], ALU.subtract))
                        st.then(dve.tensor_scalar(off[:, :], start[:, :], float(ROWS), None, ALU.mult))
                        st.then(dve.tensor_scalar(before[:, :], start[0:NT, :], tile_id[:, 0:1], None, ALU.is_le))
                        st.then(dve.tensor_reduce(texp[:, :], before[:, :], AX, ALU.add))
                        dve.tensor_scalar(texp[:, :], texp[:, :], -1.0, None, ALU.add).then_inc(placed.sem, 1)
                        dve.wait_ge(placed.sem, placed.at(2))
                        st.then(dve.tensor_copy(tile_expert[:, :], c.banks[7][0:1, 0:NT]))
                        st.then(dve.tensor_tensor(te(pos), te(pos), whole(off[:, :], TILES), ALU.add))
                    else:
                        st.then(dve.tensor_scalar(incl[:, :], pos[:, :], float(cap), FAR, ALU.is_ge, ALU.mult))
                        st.then(dve.tensor_tensor(pos[:, :], pos[:, :], incl[:, :], ALU.add))
                        st.then(dve.tensor_tensor(te(pos), te(pos), whole(off[:, :], TILES), ALU.add))
                    for k in range(K):
                        st.then(dve.tensor_tensor(hot4[:, :, k, :], hot4[:, :, k, :], te(pos), ALU.mult))
                    st.then(dve.tensor_reduce(slotf[:, :], hot3, AX, ALU.add))
                    st.then(dve.tensor_copy(slots[:, :], slotf[:, :]))
                    if cap is not None:
                        st.then(dve.tensor_scalar(slotf[:, :], slotf[:, :], float(NT * ROWS), None, ALU.is_lt))
                        st.then(dve.tensor_tensor(weights[:, :], weights[:, :], slotf[:, :], ALU.mult))
                    moe.own = st.n
            own.counted(moe.own)
            for w, n in ((placed, 2 if cap is None else 0), (made, 4), (pown, 2), (expd, 2), (ranked, 1), (counted_, 1),
                         (bsplit, 5 if which == 0 else 0), (bstored, 96 if which == 0 else 0)):
                w.counted(n)

            with nc.Block() as block:

                @block.gpsimd
                def _(pool):
                    for n in range(TK):
                        i = n // K
                        pool.indirect_dma_start(xs, bass.IndirectOffsetOnAxis(ap=slots[:, n:n + 1], axis=0),
                                                xn[:, i * D_MODEL:(i + 1) * D_MODEL], None,
                                                bounds_check=NT * ROWS - 1, oob_is_err=False) \
                            .then_inc(moved.sem, 16)
                    pool.wait_ge(moved.sem, moved.at(16 * TK))
            moved.counted(16 * TK)
        scope.close()
        loaded.counted(16 * len(LOADS))

        experts(c, which, E, I, ROWS, NT, xs, ys, w_gu, w_dn, (b_gu, b_dn) if which == 0 else None, tile_expert,
                (weights_in.sem, weights_in.at(16 * len(WEIGHTS))))
        weights_in.counted(16 * len(WEIGHTS))

        NB = 16
        fetched = [counter(c, f"mo_fetched{i}") for i in range(NB)]
        added = counter(c, "mo_added")
        with ExitStack() as q:
            yb = q.enter_context(nc.sbuf_tensor("mo_yb", [P, NB * D_MODEL], F32, allow_name_mangling=True))
            with nc.Block() as block:

                @block.gpsimd
                def _(pool):
                    if cap is not None:
                        pool.memset(yb[:, :], 0.0).then_inc(pown.sem, 1)
                        pool.wait_ge(pown.sem, pown.at(1))
                    for n in range(TK):
                        u = n % NB
                        if n >= NB:
                            pool.wait_ge(added.sem, added.at(n - NB + 1))
                        pool.indirect_dma_start(yb[:, u * D_MODEL:(u + 1) * D_MODEL], None, ys,
                                                bass.IndirectOffsetOnAxis(ap=slots[:, n:n + 1], axis=0),
                                                bounds_check=NT * ROWS - 1, oob_is_err=False) \
                            .then_inc(fetched[u].sem, 16)

                @block.vector
                def _(dve):
                    for n in range(TK):
                        u, i = n % NB, n // K
                        at = slice(i * D_MODEL, (i + 1) * D_MODEL)
                        dve.wait_ge(fetched[u].sem, fetched[u].at(16 * (n // NB + 1)))
                        if n % K:
                            dve.wait_ge(added.sem, added.at(n))
                        dve.scalar_tensor_tensor(out=c.x[:, at], in0=yb[:, u * D_MODEL:(u + 1) * D_MODEL],
                                                 scalar=weights[:, n:n + 1], in1=c.x[:, at],
                                                 op0=ALU.mult, op1=ALU.add).then_inc(added.sem, 1)
        added.counted(TK)
        if cap is not None:
            pown.counted(1)
        for u in range(NB):
            fetched[u].counted(16 * (TK // NB))


def remap_gate(c, gold, o2n, iota_e, gate, bias):
    nc = c.nc
    E = M1_E
    made, own, mm = counter(c, "rg_made"), counter(c, "rg_own"), counter(c, "rg_mm")
    with ExitStack() as s:
        sb = lambda name, shape, dt=F32: s.enter_context(nc.sbuf_tensor(name, shape, dt, allow_name_mangling=True))
        o2f, m, mb = sb("rg_o2f", [P, 1]), sb("rg_m", [P, E]), sb("rg_mb", [P, E], BF16)
        with nc.Block() as block:

            @block.gpsimd
            def _(pool):
                pool.iota(m[:, :], [[1, E]], 0, 0, allow_small_or_imprecise_dtypes=True).then_inc(made.sem, 1)

            @block.vector
            def _(dve):
                st = Steps(dve, own)
                st.then(dve.tensor_copy(o2f[:, :], o2n[:, :]))
                dve.wait_ge(made.sem, made.at(1))
                st.then(dve.tensor_scalar(m[:, :], m[:, :], o2f[:, 0:1], None, ALU.is_equal))
                st.then(dve.tensor_copy(mb[:, :], m[:, :]))
                dve.wait_ge(mm.sem, mm.at(1))
                for k in range(KC):
                    dve.tensor_copy(gate[:, k * E:(k + 1) * E], c.banks[k][:, 0:E])
                st.then(dve.tensor_scalar(bias[:, :], c.banks[KC][:, 0:E], 0.5, None, ALU.is_lt))
                dve.tensor_scalar(bias[:, :], bias[:, :], NEG, None, ALU.mult)

            @block.tensor
            def _(pe):
                pe.wait_ge(own.sem, own.at(3))
                for k in range(KC):
                    pe.matmul(c.banks[k][:, 0:E], gold[:, k * P:(k + 1) * P], m[:, :], start=True, stop=True)
                pe.matmul(c.banks[KC][:, 0:E], c.ones[:, :], mb[:, :], start=True, stop=True).then_inc(mm.sem, 1)
    made.counted(1)
    own.counted(4)
    mm.counted(1)


def experts(c, which, E, I, ROWS, NT, xs, ys, w_gu, w_dn, biases, tile_expert, weights_in):
    nc = c.nc
    GU = 2 * I
    NR = 4
    rows_in = [counter(c, f"ex_rows_in{u}") for u in range(NR)]
    rows_out = [counter(c, f"ex_rows_out{u}") for u in range(NR)]
    x_turned, x_kept, gate_done, clipped, act_done, gated, hidden_done, h_turned, h_kept, down_done, y_kept = (
        counter(c, "ex_" + n) for n in ("x_turned", "x_kept", "gate_up", "clipped", "act", "gated", "hidden",
                                       "h_turned", "h_kept", "down", "y_kept"))

    def steps(eng, step):
        for i in range(NR):
            step(i, i)
        with eng.Fori(0, NT // NR - 2) as j:
            for v in range(NR):
                step(j * NR + (NR + v), v)
        for i in range(NT - NR, NT + NR):
            step(i, i % NR)

    def exists(i):
        return not isinstance(i, int) or 0 <= i < NT

    with ExitStack() as s:
        sb = lambda name, shape, dt=F32: s.enter_context(nc.sbuf_tensor(name, shape, dt, allow_name_mangling=True))
        xr = [sb(f"ex_xr{u}", [ROWS, D_MODEL]) for u in range(NR)]
        yo = [sb(f"ex_yo{u}", [ROWS, D_MODEL]) for u in range(NR)]
        xT = [sb(f"ex_xT{u}", [P, KC * ROWS]) for u in range(2)]
        g, up, sg, h = ([sb(f"ex_{n}{u}", [ROWS, I]) for u in range(2)] for n in ("g", "up", "sg", "h"))
        hT = [sb(f"ex_hT{u}", [I, ROWS]) for u in range(2)]
        XT, GUB, HT, YB = (c.banks[2 * k:2 * k + 2] for k in range(4))

        with nc.Block() as block:

            @block.sync
            def _(sp):
                def load(i, u):
                    sp.dma_start(xr[u][:, :], xs[bass.ds(i * ROWS, ROWS), :]).then_inc(rows_in[u].sem, 16)

                def store(i, u):
                    sp.wait_ge(y_kept.sem, y_kept.at(i + 1))
                    sp.dma_start(ys[bass.ds(i * ROWS, ROWS), :], yo[u][:, :]).then_inc(rows_out[u].sem, 16)

                def turn(i, u):
                    sp.wait_ge(x_turned.sem, x_turned.at(i + 1))
                    load(i + NR, u)

                for u in range(NR):
                    load(u, u)
                for u in range(NR):
                    turn(u, u)
                with sp.Fori(0, NT // NR - 2) as j:
                    for u in range(NR):
                        turn(j * NR + (u + NR), u)
                        store(j * NR + u, u)
                for i in range(NT - 2 * NR, NT):
                    store(i, i % NR)
                for u in range(NR):
                    sp.wait_ge(rows_out[u].sem, rows_out[u].at(16 * (NT // NR)))

            @block.tensor
            def _(pe):
                def turn_x(i, phase):
                    u, r = phase % 2, phase % NR
                    pe.wait_ge(rows_in[r].sem, rows_in[r].at(i * (16 // NR) + (NR - r) * (16 // NR)))
                    for k in range(KC):
                        last = pe.transpose(XT[u][:, k * ROWS:(k + 1) * ROWS], xr[r][:, k * P:(k + 1) * P],
                                            c.ident[0:ROWS, 0:ROWS])
                    last.then_inc(x_turned.sem, 1)

                def expert_of(i):
                    if tile_expert is None:
                        return i
                    return pe.value_load(tile_expert[0:1, bass.ds(i, 1)], min_val=0, max_val=E - 1)

                def gate_up(i, phase):
                    u, e = phase % 2, expert_of(i)
                    pe.wait_ge(x_kept.sem, x_kept.at(i + 1))
                    for k in range(KC):
                        last = pe.matmul(GUB[u][0:ROWS, 0:GU], xT[u][:, k * ROWS:(k + 1) * ROWS],
                                         w_gu[:, bass.ds(e * (KC * GU) + k * GU, GU)],
                                         start=(k == 0), stop=(k == KC - 1 and biases is None))
                    if biases is not None:
                        last = pe.matmul(GUB[u][0:ROWS, 0:GU], c.ones[0:3, 0:ROWS],
                                         biases[0][:, bass.ds(e * GU, GU)], start=False, stop=True)
                    last.then_inc(gate_done.sem, 1)

                def turn_h(i, phase):
                    u = phase % 2
                    pe.wait_ge(hidden_done.sem, hidden_done.at(i + 1))
                    pe.transpose(HT[u][0:I, 0:ROWS], h[u][:, :], c.ident[0:ROWS, 0:ROWS]) \
                      .then_inc(h_turned.sem, 1)

                def down(i, phase):
                    u, e = phase % 2, expert_of(i)
                    pe.wait_ge(y_kept.sem, y_kept.at(i - 1))
                    pe.wait_ge(h_kept.sem, h_kept.at(i + 1))
                    last = pe.matmul(YB[u][0:ROWS, 0:D_MODEL], hT[u][:, :],
                                     w_dn[:, bass.ds(e * D_MODEL, D_MODEL)], start=True, stop=(biases is None))
                    if biases is not None:
                        last = pe.matmul(YB[u][0:ROWS, 0:D_MODEL], c.ones[0:3, 0:ROWS],
                                         biases[1][:, bass.ds(e * D_MODEL, D_MODEL)], start=False, stop=True)
                    last.then_inc(down_done.sem, 1)

                def step(i, phase):
                    if exists(i + 1):
                        turn_x(i + 1, phase + 1)
                    if exists(i - 2):
                        turn_h(i - 2, phase - 2)
                    if exists(i):
                        gate_up(i, phase)
                    if exists(i - 3):
                        down(i - 3, phase - 3)

                pe.wait_ge(*weights_in)
                turn_x(0, 0)
                steps(pe, step)

            @block.scalar
            def _(act):
                def keep_x(i, phase):
                    u = phase % 2
                    act.wait_ge(x_turned.sem, x_turned.at(i + 1))
                    act.activation(xT[u][:, :], XT[u][:, 0:KC * ROWS], ACT.Copy).then_inc(x_kept.sem, 1)

                def gate_act(i, phase):
                    u = phase % 2
                    if which == 0:
                        act.wait_ge(clipped.sem, clipped.at(i * 2 + 1))
                        act.activation(sg[u][:, :], g[u][:, :], ACT.Sigmoid, scale=1.702).then_inc(act_done.sem, 1)
                    else:
                        act.wait_ge(gate_done.sem, gate_done.at(i + 1))
                        act.activation(sg[u][:, :], GUB[u][0:ROWS, 0:I], ACT.Silu).then_inc(act_done.sem, 1)

                def keep_h(i, phase):
                    u = phase % 2
                    act.wait_ge(h_turned.sem, h_turned.at(i + 1))
                    act.activation(hT[u][:, :], HT[u][0:I, 0:ROWS], ACT.Copy).then_inc(h_kept.sem, 1)

                def step(i, phase):
                    if exists(i + 1):
                        keep_x(i + 1, phase + 1)
                    if exists(i - 2):
                        keep_h(i - 2, phase - 2)
                    if exists(i):
                        gate_act(i, phase)

                keep_x(0, 0)
                steps(act, step)

            @block.vector
            def _(dve):
                def clip(i, phase):
                    u = phase % 2
                    dve.wait_ge(gate_done.sem, gate_done.at(i + 1))
                    dve.tensor_scalar(g[u][:, :], GUB[u][0:ROWS, 0:I], 7.0, None, ALU.min) \
                       .then_inc(clipped.sem, 1)
                    dve.tensor_scalar(up[u][:, :], GUB[u][0:ROWS, I:GU], -7.0, 7.0, ALU.max, ALU.min) \
                       .then_inc(clipped.sem, 1)

                def hidden(i, phase):
                    u = phase % 2
                    if which == 0:
                        dve.wait_ge(clipped.sem, clipped.at(i * 2 + 2))
                        dve.wait_ge(act_done.sem, act_done.at(i + 1))
                        dve.tensor_tensor(g[u][:, :], g[u][:, :], sg[u][:, :], ALU.mult).then_inc(gated.sem, 1)
                        dve.wait_ge(gated.sem, gated.at(i + 1))
                        dve.scalar_tensor_tensor(out=h[u][:, :], in0=up[u][:, :], scalar=1.0, in1=g[u][:, :],
                                                 op0=ALU.add, op1=ALU.mult).then_inc(hidden_done.sem, 1)
                    else:
                        dve.wait_ge(act_done.sem, act_done.at(i + 1))
                        dve.tensor_tensor(h[u][:, :], sg[u][:, :], GUB[u][0:ROWS, I:GU], ALU.mult) \
                           .then_inc(hidden_done.sem, 1)

                def keep_y(i, phase):
                    u, r = phase % 2, phase % NR
                    dve.wait_ge(rows_out[r].sem, rows_out[r].at(i * (16 // NR) - r * (16 // NR)))
                    dve.wait_ge(down_done.sem, down_done.at(i + 1))
                    dve.tensor_copy(yo[r][:, :], YB[u][0:ROWS, 0:D_MODEL]).then_inc(y_kept.sem, 1)

                def step(i, phase):
                    if exists(i) and which == 0:
                        clip(i, phase)
                    if exists(i - 4):
                        keep_y(i - 4, phase)
                    if exists(i):
                        hidden(i, phase)

                steps(dve, step)
    for u in range(NR):
        rows_in[u].counted(16 * (NT // NR))
        rows_out[u].counted(16 * (NT // NR))
    for w in (x_turned, x_kept, gate_done, act_done, hidden_done, h_turned, h_kept, down_done, y_kept):
        w.counted(NT)
    if which == 0:
        clipped.counted(2 * NT)
        gated.counted(NT)


class Heads:

    def __init__(self, name, heads, dim, kv_heads, scale, causal, rot=0, interleaved=False, window=0):
        self.name, self.H, self.D, self.KH, self.scale, self.causal = name, heads, dim, kv_heads, scale, causal
        self.rot, self.interleaved, self.window = rot, interleaved, window
        self.HG = 4
        self.G = heads // self.HG
        self.latent = kv_heads == 1
        self.KT = min(4, kv_heads)


ROTARY = Heads("ra", 16, 16, 16, 0.25, True, rot=8, interleaved=True)
SINKS = Heads("sa", 32, 64, 8, 0.125, False, rot=16, window=64)
LATENT = Heads("la", 16, 128, 1, 1.0 / float(np.sqrt(128.0)), True)


def rotate(st, a, dst, src, n, tile, cos, sin, t1, t2):
    dve, R = st.eng, a.rot
    if a.interleaved:
        v = lambda x: x.rearrange("p (h r s) -> p h s r", h=n, s=2)
    else:
        v = lambda x: x.rearrange("p (h s r) -> p h s r", h=n, s=2)
    small = lambda x: x[:, 0:n * 2 * R].rearrange("p (h s r) -> p h s r", h=n, s=2)
    c_, s_ = (x[:, tile * R:(tile + 1) * R].rearrange("p (h r) -> p h r", h=1).to_broadcast([P, n, R])
              for x in (cos, sin))
    for half in range(2):
        dve.tensor_tensor(small(t1)[:, :, half, :], v(src)[:, :, half, 0:R], c_, ALU.mult)
        op = dve.tensor_tensor(small(t2)[:, :, half, :], v(src)[:, :, 1 - half, 0:R], s_, ALU.mult)
        if half == 0 and R * 2 < a.D:
            dve.tensor_copy(v(dst)[:, :, :, R:], v(src)[:, :, :, R:])
    st.then(op)
    for half in range(2):
        minus = (half == 0) == a.interleaved
        op = dve.tensor_tensor(v(dst)[:, :, half, 0:R], small(t1)[:, :, half, :], small(t2)[:, :, half, :],
                               ALU.subtract if minus else ALU.add)
    return op


def attention(c, a):
    nc, t = c.nc, c.t
    QW = a.HG * a.D
    KW = a.KH * a.D
    HD = a.H * a.D
    OC = HD // P
    UN = TPB * a.HG
    with ExitStack() as s:
        sb = lambda name, shape, dt=F32: s.enter_context(nc.sbuf_tensor(f"{a.name}_{name}", shape, dt))
        sig = {n: counter(c, "at_" + n) for n in (
            "loaded", "made", "xkept", "kvp", "kput", "vput", "kturned", "kkept", "qp", "qput", "qturned", "qkept",
            "scored", "maxed", "negged", "exped", "turned", "kept_d", "kept_a", "summed", "normed", "own_k",
            "own_q", "own_n", "own_o", "yturned", "ykept", "outp", "added")}
        at = lambda n, v: (sig[n].sem, sig[n].at(v))
        inc = lambda n: (sig[n].sem, 1)
        w_q, w_k = sb("w_q", [P, KC * HD]), sb("w_k", [P, KC * KW])
        w_v = None if a.latent else sb("w_v", [P, KC * KW])
        w_o = sb("w_o", [P, OC * D_MODEL])
        fold = lambda w, src: (w[:, :].rearrange("p (k n) -> p k n", k=KC), src.rearrange("(k p) n -> p k n", p=P))
        LOADS = [fold(w_q, t[a.name + "_wq"]), fold(w_k, t[a.name + "_wk"]),
                 (w_o[:, :].rearrange("p (k n) -> p k n", k=OC), t[a.name + "_wo"].rearrange("(k p) n -> p k n", p=P))]
        if not a.latent:
            LOADS.append(fold(w_v, t[a.name + "_wv"]))
        if a.rot:
            cos, sin = sb("cos", [P, TPB * a.rot]), sb("sin", [P, TPB * a.rot])
            for x, n in ((cos, "_cos"), (sin, "_sin")):
                LOADS.append((x[:, :].rearrange("p (t r) -> p t r", t=TPB),
                              t[a.name + n].rearrange("(t p) r -> p t r", p=P)))
        if a.latent:
            b_q, b_k, b_o = sb("b_q", [P, HD]), sb("b_k", [P, KW]), sb("b_o", [P, D_MODEL])
            LOADS += [(b_q[:, :], t["la_bq"].to_broadcast([P, HD])), (b_k[:, :], t["la_bk"].to_broadcast([P, KW])),
                      (b_o[:, :], t["la_bo"].to_broadcast([P, D_MODEL]))]
        if a.window:
            sink = sb("sink", [P, a.H])
            negsink = sb("negsink", [P, a.H])
            LOADS.append((sink[:, :], t["sinks"].to_broadcast([P, a.H])))

        def loads(sp):
            for dst, src in LOADS:
                sp.dma_start(dst, src).then_inc(sig["loaded"].sem, 16)

        xnT = sb("xnT", [P, KC * TOKENS])
        layer_norm(c, xnT, loads=loads)

        MW = 2 * P if a.window else P
        mask, identb = sb("mask", [P, MW], BF16), sb("identb", [P, P], BF16)
        xb = sb("xb", [P, KC * SEQ])
        kst = sb("kst", [P, KW])
        kT = sb("kT", [a.D, a.KH * SEQ])
        VW = KW + P - a.D
        vv = sb("v", [P, TPB * VW])
        qst = sb("qst", [P, QW])
        qT = [sb(f"qT{u}", [a.D, a.HG * P]) for u in range(2)]
        pr = [sb(f"p{u}", [P, SEQ]) for u in range(2)]
        pT = [sb(f"pT{u}", [P, SEQ]) for u in range(2)]
        mx, nm, rs = (sb(n, [P, 2 * a.HG]) for n in ("mx", "nm", "rs"))
        es, rinv = (sb(n, [P, 2 * a.HG]) for n in ("es", "rinv"))
        yb = sb("y", [P, TPB * HD])
        yT = sb("yT", [P, OC * P])
        t1, t2 = (sb(n, [P, max(a.KH, a.HG) * 2 * a.rot]) if a.rot else None for n in ("t1", "t2"))
        SC, PT, OB, QB, TQ = c.banks[0:2], c.banks[2:4], c.banks[4:6], c.banks[6], c.banks[7]
        keys = lambda qt: (qt + 1) * P if a.causal else SEQ
        kvh = lambda g, hh: 0 if a.latent else (g * a.HG + hh if a.KH == a.H else g)
        KG = a.KH // a.KT

        with nc.Block() as block:

            @block.gpsimd
            def _(pool):
                pool.memset(mask[:, :], 0.0).then_inc(*inc("made"))
                pool.memset(identb[:, :], 0.0).then_inc(*inc("made"))
                pool.wait_ge(*at("made", 2))
                pool.affine_select(out=identb[:, :], in_=identb[:, :], compare_op=ALU.not_equal, fill=1.0,
                                   base=0, pattern=[[-1, P]], channel_multiplier=1).then_inc(*inc("made"))
                if a.window:
                    pool.memset(mask[:, :], NEG).then_inc(*inc("made"))
                    pool.wait_ge(*at("made", 4))
                    pool.affine_select(out=mask[:, :], in_=mask[:, :], compare_op=ALU.is_ge, fill=0.0,
                                       base=P, pattern=[[-1, MW]], channel_multiplier=1).then_inc(*inc("made"))
                    pool.wait_ge(*at("made", 5))
                    pool.affine_select(out=mask[:, :], in_=mask[:, :], compare_op=ALU.is_gt, fill=0.0,
                                       base=a.window - P, pattern=[[1, MW]], channel_multiplier=-1) \
                        .then_inc(*inc("made"))
                else:
                    pool.affine_select(out=mask[:, :], in_=mask[:, :], compare_op=ALU.is_ge, fill=NEG,
                                       base=0, pattern=[[-1, P]], channel_multiplier=1).then_inc(sig["made"].sem, 3)
                if VW > KW:
                    pool.memset(vv[:, :].rearrange("p (t n) -> p t n", t=TPB)[:, :, KW:], 0.0) \
                        .then_inc(*inc("made"))

            @block.tensor
            def _(pe):
                pe.wait_ge(*at("made", 6 + (VW > KW)))
                pe.wait_ge(*at("loaded", 16 * len(LOADS)))

                def carry_wait(bank):
                    if a.D == 64:
                        pe.matmul(bank[:, 0:1], c.zeros[:, 0:P], c.zeros[:, 0:1], start=True, stop=True)

                with pe.Fori(0, BATCH) as b:
                    pe.wait_ge(*at("xkept", b + 1))
                    for i in range(TPB):
                        n = b * TPB + i
                        pe.wait_ge(*at("kput", n))
                        if not a.latent:
                            pe.wait_ge(*at("vput", n))
                        for w, bank in ((w_k, SC[0]),) + (() if a.latent else ((w_v, SC[1]),)):
                            for k in range(KC):
                                last = pe.matmul(bank[:, 0:KW], xb[:, k * SEQ + i * P:k * SEQ + (i + 1) * P],
                                                 w[:, k * KW:(k + 1) * KW], start=(k == 0), stop=(k == KC - 1))
                        last.then_inc(*inc("kvp"))
                        pe.wait_ge(*at("kput", n + 1))
                        for m in range(KG):
                            pe.wait_ge(*at("kkept", n * KG + max(m - 1, 0)))
                            carry_wait(PT[m % 2])
                            for hh in range(a.KT):
                                h = m * a.KT + hh
                                src = vv[:, i * VW:i * VW + KW] if a.latent else kst[:, h * a.D:(h + 1) * a.D]
                                last = pe.transpose(PT[m % 2][0:a.D, hh * P:(hh + 1) * P], src, c.ident[:, :])
                            last.then_inc(*inc("kturned"))
                    with pe.Fori(0, a.G) as g:
                        I = b * a.G + g
                        n0 = I * UN

                        def project(qt):
                            pe.wait_ge(*at("qput", I * TPB + qt))
                            for k in range(KC):
                                last = pe.matmul(QB[:, 0:QW], xb[:, k * SEQ + qt * P:k * SEQ + (qt + 1) * P],
                                                 w_q[:, bass.ds(g * QW + k * HD, QW)],
                                                 start=(k == 0), stop=(k == KC - 1))
                            last.then_inc(*inc("qp"))

                        def turn_q(qt):
                            pe.wait_ge(*at("qput", I * TPB + qt + 1))
                            pe.wait_ge(*at("qkept", I * TPB + qt))
                            carry_wait(TQ)
                            for hh in range(a.HG):
                                last = pe.transpose(TQ[0:a.D, hh * P:(hh + 1) * P], qst[:, hh * a.D:(hh + 1) * a.D],
                                                    c.ident[:, :])
                            last.then_inc(*inc("qturned"))

                        def score(u):
                            qt, hh = divmod(u, a.HG)
                            bank = SC[u % 2]
                            if a.latent:
                                key = kT[:, 0:keys(qt)]
                            else:
                                key = kT[:, bass.ds(g * (SEQ * (a.HG if a.KH == a.H else 1))
                                                    + (hh * SEQ if a.KH == a.H else 0), keys(qt))]
                            pe.matmul(bank[:, 0:keys(qt)], qT[qt % 2][:, hh * P:(hh + 1) * P], key,
                                      start=True, stop=False)
                            lo = max(qt * P - (MW - P), 0)
                            hi = (qt + 1) * P
                            pe.matmul(bank[:, lo:hi], identb[:, :], mask[:, MW - (hi - lo):MW],
                                      start=False, stop=True).then_inc(*inc("scored"))

                        def turn_p(u):
                            qt = u // a.HG
                            pe.wait_ge(*at("exped", n0 + u + 1))
                            if u >= 2:
                                pe.wait_ge(*at("kept_d" if u % 2 == 0 else "kept_a", I * (UN // 2) + u // 2))
                            else:
                                pe.wait_ge(*at("kept_d" if u % 2 == 0 else "kept_a", I * (UN // 2)))
                            for kb in range(keys(qt) // P):
                                last = pe.transpose(PT[u % 2][:, kb * P:(kb + 1) * P],
                                                    pr[u % 2][:, kb * P:(kb + 1) * P], c.ident[:, :])
                            last.then_inc(*inc("turned"))

                        def values(u):
                            qt, hh = divmod(u, a.HG)
                            pe.wait_ge(*at("kept_d" if u % 2 == 0 else "kept_a", I * (UN // 2) + (u // 2 + 1)))
                            if hh == 0:
                                pe.wait_ge(*at("normed", I * TPB + max(qt - 1, 0)))
                            nb = keys(qt) // P
                            for kb in range(nb):
                                if a.latent:
                                    v = vv[:, kb * VW:kb * VW + P]
                                elif a.KH == a.H:
                                    v = vv[:, bass.ds(g * (a.HG * a.D) + (kb * VW + hh * a.D), P)]
                                else:
                                    v = vv[:, bass.ds(g * a.D + kb * VW, P)]
                                last = pe.matmul(OB[qt % 2][:, hh * P:(hh + 1) * P],
                                                 pT[u % 2][:, kb * P:(kb + 1) * P], v,
                                                 start=(kb == 0), stop=(kb == nb - 1))
                            last.then_inc(*inc("summed"))

                        project(0)
                        turn_q(0)
                        pe.wait_ge(*at("kkept", (b + 1) * (TPB * KG)))
                        pe.wait_ge(*at("qkept", I * TPB + 1))
                        for u in range(UN + 2):
                            if u < UN:
                                if u % a.HG == 0 and u // a.HG + 1 < TPB:
                                    project(u // a.HG + 1)
                                if u % a.HG == 2 and u // a.HG + 1 < TPB:
                                    turn_q(u // a.HG + 1)
                                score(u)
                            if 1 <= u <= UN:
                                turn_p(u - 1)
                            if u >= 2:
                                values(u - 2)
                    pe.wait_ge(*at("normed", (b + 1) * (a.G * TPB)))
                    for qt in range(TPB):
                        for m in range(-(-OC // 4)):
                            w = min(4, OC - m * 4)
                            n = (b * TPB + qt) * (-(-OC // 4)) + m
                            pe.wait_ge(*at("ykept", n))
                            for k in range(w):
                                last = pe.transpose(PT[m % 2][:, k * P:(k + 1) * P],
                                                    yb[:, qt * HD + (m * 4 + k) * P:qt * HD + (m * 4 + k + 1) * P],
                                                    c.ident[:, :])
                            last.then_inc(*inc("yturned"))
                        pe.wait_ge(*at("ykept", (b * TPB + qt + 1) * (-(-OC // 4))))
                        pe.wait_ge(*at("added", b * TPB + qt))
                        for k in range(OC):
                            last = pe.matmul(OB[0][:, 0:D_MODEL], yT[:, k * P:(k + 1) * P],
                                             w_o[:, k * D_MODEL:(k + 1) * D_MODEL],
                                             start=(k == 0), stop=(k == OC - 1))
                        last.then_inc(*inc("outp"))

            @block.scalar
            def _(act):
                with act.Fori(0, BATCH) as b:
                    act.wait_ge(*at("added", b * TPB))
                    act.activation(xb[:, :].rearrange("p (k n) -> p k n", k=KC),
                                   xnT[:, :].rearrange("p (k n) -> p k n", k=KC)[:, :, bass.ds(b * SEQ, SEQ)],
                                   ACT.Copy).then_inc(*inc("xkept"))
                    for i in range(TPB):
                        n = b * TPB + i
                        if not a.latent:
                            act.wait_ge(*at("kvp", n + 1))
                            act.activation(vv[:, i * VW:i * VW + KW], SC[1][:, 0:KW], ACT.Copy).then_inc(*inc("vput"))
                        for m in range(KG):
                            act.wait_ge(*at("kturned", n * KG + m + 1))
                            act.activation(kT[:, :].rearrange("p (h n) -> p h n", h=a.KH)
                                           [:, m * a.KT:(m + 1) * a.KT, i * P:(i + 1) * P],
                                           PT[m % 2][0:a.D, 0:a.KT * P].rearrange("p (h n) -> p h n", h=a.KT),
                                           ACT.Copy).then_inc(*inc("kkept"))
                    with act.Fori(0, a.G) as g:
                        I = b * a.G + g
                        n0 = I * UN

                        def keep_q(qt):
                            act.wait_ge(*at("qturned", I * TPB + qt + 1))
                            act.wait_ge(*at("scored", n0 + max(qt - 1, 0) * a.HG))
                            act.activation(qT[qt % 2][:, :], TQ[0:a.D, :], ACT.Copy).then_inc(*inc("qkept"))

                        def expo(u):
                            qt, hh = divmod(u, a.HG)
                            col = (qt % 2) * a.HG + hh
                            act.wait_ge(*at("negged", n0 + u + 1))
                            act.wait_ge(*at("turned", n0 + max(u - 1, 0)))
                            act.activation(pr[u % 2][:, 0:keys(qt)], SC[u % 2][:, 0:keys(qt)], ACT.Exp,
                                           bias=nm[:, col:col + 1], scale=a.scale,
                                           accum_out=rs[:, col:col + 1]).then_inc(*inc("exped"))

                        def keep_p(u):
                            qt = u // a.HG
                            act.wait_ge(*at("turned", n0 + u + 1))
                            act.wait_ge(*at("summed", n0 + max(u - 1, 0)))
                            act.activation(pT[u % 2][:, 0:keys(qt)], PT[u % 2][:, 0:keys(qt)],
                                           ACT.Copy).then_inc(*inc("kept_a"))

                        keep_q(0)
                        for u in range(UN + 1):
                            if u < UN:
                                if u % a.HG == 2 and u // a.HG + 1 < TPB:
                                    keep_q(u // a.HG + 1)
                                expo(u)
                            if u >= 1 and (u - 1) % 2 == 1:
                                keep_p(u - 1)
                            if a.window and u % a.HG == a.HG - 1 and u < UN:
                                qt = u // a.HG
                                cut = slice((qt % 2) * a.HG, (qt % 2 + 1) * a.HG)
                                act.wait_ge(*at("own_n", (I * TPB + qt) * 3 + 1))
                                act.activation(es[:, cut], es[:, cut], ACT.Exp).then_inc(*inc("maxed"))
                    for qt in range(TPB):
                        for m in range(-(-OC // 4)):
                            w = min(4, OC - m * 4)
                            n = (b * TPB + qt) * (-(-OC // 4)) + m
                            act.wait_ge(*at("yturned", n + 1))
                            act.wait_ge(*at("outp", b * TPB + qt))
                            act.activation(yT[:, m * 4 * P:(m * 4 + w) * P], PT[m % 2][:, 0:w * P],
                                           ACT.Copy).then_inc(*inc("ykept"))

            @block.vector
            def _(dve):
                dve.wait_ge(*at("loaded", 16 * len(LOADS)))
                if a.window:
                    dve.tensor_scalar(negsink[:, :], sink[:, :], -1.0, None, ALU.mult).then_inc(*inc("own_o"))
                    dve.wait_ge(*at("own_o", 1))
                with dve.Fori(0, BATCH) as b:
                    for i in range(TPB):
                        n = b * TPB + i
                        dve.wait_ge(*at("kvp", n + 1))
                        dve.wait_ge(*at("kturned", n * KG))
                        if a.latent:
                            dve.tensor_tensor(vv[:, i * VW:i * VW + KW], SC[0][:, 0:KW], b_k[:, :], ALU.add) \
                               .then_inc(*inc("kput"))
                        else:
                            st = Steps(dve, sig["own_k"])
                            st.loop = n
                            rotate(st, a, kst[:, :], SC[0][:, 0:KW], a.KH, i, cos, sin, t1, t2) \
                                .then_inc(*inc("kput"))
                    with dve.Fori(0, a.G) as g:
                        I = b * a.G + g
                        n0 = I * UN

                        def put_q(qt):
                            dve.wait_ge(*at("qp", I * TPB + qt + 1))
                            dve.wait_ge(*at("qturned", I * TPB + qt))
                            if a.latent:
                                dve.tensor_tensor(qst[:, :], QB[:, :], b_q[:, bass.ds(g * QW, QW)], ALU.add) \
                                   .then_inc(*inc("qput"))
                            else:
                                st = Steps(dve, sig["own_q"])
                                st.loop = I * TPB + qt
                                rotate(st, a, qst[:, :], QB[:, 0:QW], a.HG, qt, cos, sin, t1, t2) \
                                    .then_inc(*inc("qput"))

                        def maximum(u):
                            qt, hh = divmod(u, a.HG)
                            col = (qt % 2) * a.HG + hh
                            dve.wait_ge(*at("scored", n0 + u + 1))
                            dve.reduce_max(mx[:, col:col + 1], SC[u % 2][:, 0:keys(qt)], AX) \
                               .then_inc(*inc("own_o"))
                            dve.wait_ge(*at("own_o", n0 + (u + 1 + bool(a.window))))
                            if a.window:
                                dve.scalar_tensor_tensor(out=nm[:, col:col + 1], in0=mx[:, col:col + 1],
                                                         scalar=-a.scale, in1=negsink[:, bass.ds(g * a.HG + hh, 1)],
                                                         op0=ALU.mult, op1=ALU.min).then_inc(*inc("negged"))
                            else:
                                dve.tensor_scalar(nm[:, col:col + 1], mx[:, col:col + 1], -a.scale, None,
                                                  ALU.mult).then_inc(*inc("negged"))

                        def keep_p(u):
                            qt = u // a.HG
                            dve.wait_ge(*at("turned", n0 + u + 1))
                            dve.wait_ge(*at("summed", n0 + max(u - 1, 0)))
                            dve.tensor_copy(pT[u % 2][:, 0:keys(qt)], PT[u % 2][:, 0:keys(qt)]) \
                               .then_inc(*inc("kept_d"))

                        def sink_minus_max(qt):
                            cut = slice((qt % 2) * a.HG, (qt % 2 + 1) * a.HG)
                            dve.wait_ge(*at("negged", n0 + (qt + 1) * a.HG))
                            dve.tensor_tensor(es[:, cut], nm[:, cut], sink[:, bass.ds(g * a.HG, a.HG)],
                                              ALU.add).then_inc(*inc("own_n"))

                        def normalize(qt):
                            cut = slice((qt % 2) * a.HG, (qt % 2 + 1) * a.HG)
                            base = (I * TPB + qt) * 3
                            dve.wait_ge(*at("summed", n0 + (qt + 1) * a.HG))
                            if a.window:
                                dve.wait_ge(*at("maxed", I * TPB + qt + 1))
                                dve.tensor_tensor(rs[:, cut], rs[:, cut], es[:, cut], ALU.add) \
                                   .then_inc(*inc("own_n"))
                                dve.wait_ge(*at("own_n", base + 2))
                                dve.reciprocal(rinv[:, cut], rs[:, cut]).then_inc(*inc("own_n"))
                                dve.wait_ge(*at("own_n", base + 3))
                            else:
                                dve.reciprocal(rinv[:, cut], rs[:, cut]).then_inc(*inc("own_n"))
                                dve.wait_ge(*at("own_n", I * TPB + qt + 1))
                            dve.tensor_tensor(
                                yb[:, bass.ds(g * QW + qt * HD, QW)].rearrange("p (h d) -> p h d", h=a.HG),
                                OB[qt % 2][:, :].rearrange("p (h d) -> p h d", h=a.HG)[:, :, 0:a.D],
                                rinv[:, cut].rearrange("p (h o) -> p h o", o=1).to_broadcast([P, a.HG, a.D]),
                                ALU.mult).then_inc(*inc("normed"))

                        put_q(0)
                        for u in range(UN + 2):
                            if u < UN:
                                maximum(u)
                                if a.window and u % a.HG == a.HG - 1:
                                    sink_minus_max(u // a.HG)
                                if u % a.HG == 0 and u // a.HG + 1 < TPB:
                                    put_q(u // a.HG + 1)
                            if 1 <= u <= UN and (u - 1) % 2 == 0:
                                keep_p(u - 1)
                            if u >= 2 and (u - 2) % a.HG == a.HG - 1:
                                normalize((u - 2) // a.HG)
                    for qt in range(TPB):
                        n = b * TPB + qt
                        dve.wait_ge(*at("outp", n + 1))
                        at_x = c.x[:, bass.ds(b * (TPB * D_MODEL) + qt * D_MODEL, D_MODEL)]
                        if a.latent:
                            dve.tensor_tensor(at_x, at_x, b_o[:, :], ALU.add).then_inc(*inc("own_k"))
                            dve.wait_ge(*at("own_k", n + 1))
                        dve.tensor_tensor(at_x, at_x, OB[0][:, 0:D_MODEL], ALU.add).then_inc(*inc("added"))
        NI = BATCH * a.G
        rounds = -(-OC // 4)
        for n, v in dict(
                loaded=16 * len(LOADS), made=6 + (VW > KW), xkept=BATCH, kvp=TILES, kput=TILES, vput=0 if a.latent else TILES,
                kturned=TILES * KG, kkept=TILES * KG, qp=NI * TPB, qput=NI * TPB, qturned=NI * TPB, qkept=NI * TPB,
                scored=NI * UN, negged=NI * UN, exped=NI * UN, turned=NI * UN, kept_d=NI * UN // 2,
                kept_a=NI * UN // 2, summed=NI * UN, normed=NI * TPB, maxed=NI * TPB if a.window else 0,
                own_k=TILES, own_q=0 if a.latent else NI * TPB,
                own_n=NI * TPB * (3 if a.window else 1), own_o=NI * UN + bool(a.window),
                yturned=TILES * rounds, ykept=TILES * rounds, outp=TILES, added=TILES).items():
            sig[n].counted(v)


LAYERS = ["mamba", "moe0", "rotary", "moe0", "sinks", "moe1", "latent", "moe1"]
STAGES = {"mamba": mamba, "moe0": lambda c: moe(c, 0), "moe1": lambda c: moe(c, 1),
          "rotary": lambda c: attention(c, ROTARY), "sinks": lambda c: attention(c, SINKS),
          "latent": lambda c: attention(c, LATENT)}


def build_program(nc, t, layers=LAYERS):
    with ExitStack() as ctx:
        c = setup(nc, ctx, t)
        load_residual(c)
        for name in layers:
            STAGES[name](c)
        store_residual(c)


def host_layout(inputs):
    f = lambda name: np.asarray(inputs[name])
    cols = lambda a: np.ascontiguousarray(a.reshape(-1, P).T)
    gu0 = np.concatenate([f("L0_ffn_w_gate"), f("L0_ffn_w_up")], axis=2)
    gu1 = f("L1_ffn_gate_up_proj").transpose(0, 2, 1)
    pack = lambda w: w.reshape(w.shape[0], KC, P, w.shape[2]).transpose(2, 0, 1, 3).reshape(P, -1)
    rq, rk, rv = np.split(f("L0_attn_b_w_atten").T, 3, axis=1)
    sq, sk, sv = np.split(f("L1_attn_a_W_qkv"), (SINKS.H * SINKS.D, (SINKS.H + SINKS.KH) * SINKS.D), axis=1)
    position = np.arange(SEQ, dtype=np.float32)
    theta_r = np.outer(position, 1.0 / np.float32(10000.0) ** (np.arange(0, 16, 2, dtype=np.float32) / 16))
    theta_s = np.outer(position, np.float32(1.0 / 1024.0) ** np.linspace(0.0, 1.0, 16, dtype=np.float32))
    return {
        "ra_wq": rq, "ra_wk": rk, "ra_wv": rv, "ra_wo": f("L0_attn_b_w_proj").T,
        "ra_cos": np.cos(theta_r).astype(np.float32), "ra_sin": np.sin(theta_r).astype(np.float32),
        "sa_wq": sq, "sa_wk": sk, "sa_wv": sv, "sa_wo": f("L1_attn_a_W_out"),
        "sa_cos": np.cos(theta_s).astype(np.float32), "sa_sin": np.sin(theta_s).astype(np.float32),
        "sinks": f("L1_attn_a_s").reshape(1, -1),
        "la_wq": f("L1_attn_b_W_d"), "la_wk": f("L1_attn_b_W_lat"), "la_wo": f("L1_attn_b_W_proj"),
        "la_bq": f("L1_attn_b_b_d")[None, :], "la_bk": f("L1_attn_b_b_lat")[None, :],
        "la_bo": f("L1_attn_b_b_proj")[None, :],
        "w_gu0": pack(gu0), "w_gu1": pack(gu1),
        "w_dn0": f("L0_ffn_w_down").transpose(1, 0, 2).reshape(M0_I, -1),
        "w_dn1": f("L1_ffn_down_proj").transpose(2, 0, 1).reshape(M1_I, -1),
        "gate0T": f("L0_ffn_gate_w").T, "gate_b": f("L0_ffn_gate_b")[None, :],
        "b_all": np.concatenate([f("L0_ffn_b_gate"), f("L0_ffn_b_up"), f("L0_ffn_b_down")], axis=1),
        "gate1": f("L1_ffn_gate_weight"), "o2n": f("L1_ffn_old_to_new")[:, None],
        "x": f("L0_attn_a_hidden_states"),
        "in_wT": f("L0_attn_a_in_proj_w").T, "conv_w": f("L0_attn_a_conv_w"),
        "conv_b": cols(f("L0_attn_a_conv_b")), "D": cols(f("L0_attn_a_D")), "dt_b": cols(f("L0_attn_a_dt_proj_b")),
        "A_log": f("L0_attn_a_A_log"), "x_wT": f("L0_attn_a_x_proj_w").T,
        "dt_wT": f("L0_attn_a_dt_proj_w").T, "out_wT": f("L0_attn_a_out_proj_w").T,
    }


SCRATCH = {"scratch_bc": (2 * D_STATE, TOKENS)}
for _which, _rows in ((0, M0_TILES * P), (1, M1_E * M1_CAP)):
    SCRATCH[f"scratch_xs{_which}"] = SCRATCH[f"scratch_ys{_which}"] = (_rows, D_MODEL)


def make(nc, arrays, layers=LAYERS):
    t = {n: nc.dram_tensor(f"in_{n}", a.shape, mybir.dt.from_np(a.dtype), kind="ExternalInput").ap()
         for n, a in arrays.items()}
    for n, shape in SCRATCH.items():
        t[n] = nc.dram_tensor(n, shape, F32, kind="Internal").ap()
    t["out"] = nc.dram_tensor("out", (BATCH, SEQ, D_MODEL), F32, kind="ExternalOutput").ap()
    build_program(nc, t, layers)


def kernel(**inputs):
    import concourse.bacc as bacc
    from concourse.bass_utils import run_bass_kernel_spmd

    nc = bacc.Bacc("TRN2", target_bir_lowering=False, num_devices=1)
    arrays = {n: np.ascontiguousarray(a) for n, a in host_layout(inputs).items()}
    make(nc, arrays)
    got = run_bass_kernel_spmd(nc, [{f"in_{n}": a for n, a in arrays.items()}], core_ids=[0])
    return got.results[0]["out"]
```

```python
from contextlib import ExitStack

import numpy as np

import concourse.bass as bass
from concourse import mybir
from concourse.alu_op_type import AluOpType as ALU

F32 = mybir.dt.float32
BF16 = mybir.dt.bfloat16
I32 = mybir.dt.int32
U32 = mybir.dt.uint32
ACT = mybir.ActivationFunctionType
AX = mybir.AxisListType.X

P = 128
BATCH, SEQ, D_MODEL = 4, 512, 256
TOKENS = BATCH * SEQ
TILES = TOKENS // P
TPB = SEQ // P
KC = D_MODEL // P
LN_EPS = 1e-5
NEG = -1.0e30

D_INNER, D_STATE, D_CONV, DT_RANK = 512, 16, 4, 16
BLK = D_INNER // P
HALF = TOKENS // 2

M0_E, M0_K, M0_I = 32, 4, 128
M0_TILES = TOKENS * M0_K // P + M0_E
M1_E, M1_K, M1_I, M1_CAP, M1_OLD = 48, 8, 96, 96, 128
FAR = 1.0e6


class Counter:

    def __init__(self, ctx, nc, name, base=0):
        self.sem = ctx.enter_context(nc.semaphore(name))
        self.base = base

    def at(self, n):
        return self.base + n

    def counted(self, n):
        self.base += n


FROM_ONE = ("mb_fetched", "mb_conved", "mb_acted", "sc_scanned", "sc_out", "ex_rows_out0", "ex_rows_out1", "ex_rows_out2",
            "ex_rows_out3",
            "ex_y_kept") + tuple("at_" + n for n in (
                "kput", "vput", "kturned", "kkept", "qput", "qturned", "qkept", "scored", "exped", "turned",
                "kept_d", "kept_a", "summed", "normed", "ykept", "outp", "added"))


class Steps:

    def __init__(self, eng, counter):
        self.eng, self.counter, self.n, self.loop = eng, counter, 0, 0

    def then(self, instruction):
        self.n += 1
        instruction.then_inc(self.counter.sem, 1)
        self.eng.wait_ge(self.counter.sem, self.counter.at(self.loop + self.n))


class Core:
    pass


def setup(nc, ctx, t):
    c = Core()
    c.nc, c.t, c.ctx = nc, t, ctx
    c.counters = {n: Counter(ctx, nc, n, 1) for n in FROM_ONE}
    c.x = ctx.enter_context(nc.sbuf_tensor("residual", [P, TILES * D_MODEL], F32))
    c.ident = ctx.enter_context(nc.sbuf_tensor("ident", [P, P], F32))
    c.banks = [ctx.enter_context(nc.psum_tensor(f"bank{i}", [P, 512], F32)) for i in range(8)]
    c.zeros = ctx.enter_context(nc.sbuf_tensor("zeros", [P, 512], BF16))
    c.ones = ctx.enter_context(nc.sbuf_tensor("ones", [P, P], BF16))
    return c


def counter(c, name):
    if name not in c.counters:
        c.counters[name] = Counter(c.ctx, c.nc, name)
    return c.counters[name]


def load_residual(c):
    nc = c.nc
    loaded, made = counter(c, "x_loaded"), counter(c, "const_made")
    with nc.Block() as block:

        @block.sync
        def _(sp):
            sp.dma_start(c.x[:, :].rearrange("p (t d) -> p t d", d=D_MODEL),
                         c.t["x"].rearrange("b (t p) d -> p (b t) d", p=P)).then_inc(loaded.sem, 16)
            sp.wait_ge(loaded.sem, 16)

        @block.vector
        def _(dve):
            for name in FROM_ONE:
                dve.sem_inc(c.counters[name].sem, 1)

        @block.gpsimd
        def _(pool):
            pool.memset(c.ident[:, :], 0.0).then_inc(made.sem, 1)
            pool.memset(c.zeros[:, :], 0.0)
            pool.memset(c.ones[:, :], 1.0)
            pool.wait_ge(made.sem, 1)
            pool.affine_select(out=c.ident[:, :], in_=c.ident[:, :], compare_op=ALU.not_equal, fill=1.0,
                               base=0, pattern=[[-1, P]], channel_multiplier=1)
    loaded.counted(16)
    made.counted(1)
    c.filled, c.fills = counter(c, "filled"), 0


def zero_scratch(c, sp):
    blank = c.zeros[:, :].bitcast(F32)
    for name in ("scratch_xs0", "scratch_xs1"):
        rows = c.t[name].shape[0]
        sp.dma_start(c.t[name].rearrange("(p n) d -> p n d", p=P),
                     blank.rearrange("p (n d) -> p n d", n=1).to_broadcast([P, rows // P, D_MODEL])) \
          .then_inc(c.filled.sem, 16)
        c.fills += 1


def store_residual(c):
    nc = c.nc
    stored = counter(c, "x_stored")
    with nc.Block() as block:

        @block.sync
        def _(sp):
            sp.dma_start(c.t["out"].rearrange("b (t p) d -> p (b t) d", p=P),
                         c.x[:, :].rearrange("p (t d) -> p t d", d=D_MODEL)).then_inc(stored.sem, 16)
            sp.wait_ge(stored.sem, 16)


def layer_norm(c, xnT, xn=None, loads=None):
    nc = c.nc
    own, root, stat = counter(c, "ln_own"), counter(c, "ln_root"), counter(c, "ln_stat")
    normed, turned, kept = counter(c, "ln_normed"), counter(c, "ln_turned"), counter(c, "ln_kept")
    with ExitStack() as s:
        sb = lambda name, shape: s.enter_context(nc.sbuf_tensor(name, shape, F32, allow_name_mangling=True))
        bn = sb("ln_bn", [P, TILES * 6])
        mean, var, tmp, rstd = (sb(n, [P, TILES]) for n in ("ln_mean", "ln_var", "ln_tmp", "ln_rstd"))
        stage = sb("ln_stage", [P, 2 * D_MODEL]) if xn is None else None
        bnv = bn[:, :].rearrange("p (t s) -> p t s", s=6)

        def normal(tile, u):
            if xn is None:
                return stage[:, u * D_MODEL:(u + 1) * D_MODEL]
            return xn[:, tile * D_MODEL:(tile + 1) * D_MODEL]

        with nc.Block() as block:
            if loads is not None:
                @block.sync
                def _(sp):
                    loads(sp)
                    if c.fills == 0:
                        zero_scratch(c, sp)

            @block.vector
            def _(dve):
                st = Steps(dve, own)
                with dve.Fori(0, TILES) as i:
                    dve.bn_stats(bn[:, bass.ds(i * 6, 6)], c.x[:, bass.ds(i * D_MODEL, D_MODEL)]) \
                       .then_inc(stat.sem, 1)
                dve.wait_ge(stat.sem, stat.at(TILES))
                st.then(dve.tensor_tensor(mean[:, :], bnv[:, :, 1], bnv[:, :, 4], ALU.add))
                st.then(dve.tensor_tensor(tmp[:, :], bnv[:, :, 1], bnv[:, :, 4], ALU.subtract))
                st.then(dve.tensor_tensor(var[:, :], bnv[:, :, 2], bnv[:, :, 5], ALU.add))
                st.then(dve.tensor_tensor(tmp[:, :], tmp[:, :], tmp[:, :], ALU.mult))
                st.then(dve.tensor_scalar(var[:, :], var[:, :], 1.0 / D_MODEL, LN_EPS, ALU.mult, ALU.add))
                st.then(dve.tensor_scalar(mean[:, :], mean[:, :], 0.5, None, ALU.mult))
                st.then(dve.scalar_tensor_tensor(out=var[:, :], in0=tmp[:, :], scalar=0.25, in1=var[:, :],
                                                 op0=ALU.mult, op1=ALU.add))
                dve.wait_ge(root.sem, root.at(1))
                st.then(dve.reciprocal(rstd[:, :], tmp[:, :]))
                for i in range(TILES):
                    if i >= 2 and xn is None:
                        dve.wait_ge(turned.sem, turned.at(i - 1))
                    dve.tensor_scalar(normal(i, i % 2), c.x[:, i * D_MODEL:(i + 1) * D_MODEL],
                                      mean[:, i:i + 1], rstd[:, i:i + 1], ALU.subtract, ALU.mult) \
                       .then_inc(normed.sem, 1)

            @block.scalar
            def _(act):
                act.wait_ge(own.sem, own.at(7))
                act.activation(tmp[:, :], var[:, :], ACT.Sqrt).then_inc(root.sem, 1)
                for i in range(TILES):
                    act.wait_ge(turned.sem, turned.at(i + 1))
                    act.activation(xnT[:, 0:KC * TOKENS].rearrange("p (k n) -> p k n", k=KC)[:, :, i * P:(i + 1) * P],
                                   c.banks[i % 2][:, 0:KC * P].rearrange("p (k n) -> p k n", k=KC),
                                   ACT.Copy).then_inc(kept.sem, 1)

            @block.tensor
            def _(pe):
                for i in range(TILES):
                    pe.wait_ge(normed.sem, normed.at(i + 1))
                    if i >= 2:
                        pe.wait_ge(kept.sem, kept.at(i - 1))
                    src = normal(i, i % 2)
                    for k in range(KC):
                        last = pe.transpose(c.banks[i % 2][:, k * P:(k + 1) * P],
                                            src[:, k * P:(k + 1) * P], c.ident[:, :])
                    last.then_inc(turned.sem, 1)
    own.counted(8)
    root.counted(1)
    stat.counted(TILES)
    for q in (normed, turned, kept):
        q.counted(TILES)


def mamba(c):
    nc, t = c.nc, c.t
    with ExitStack() as s:
        sb = lambda name, shape, dt=F32: s.enter_context(nc.sbuf_tensor(name, shape, dt))
        xact = sb("mb_xact", [P, BLK * TOKENS])
        zgate = sb("mb_zgate", [P, BLK * TOKENS])
        cw, cb = sb("mb_conv_w", [P, BLK * D_CONV]), sb("mb_conv_b", [P, BLK])
        a_coef = sb("mb_a", [P, BLK * D_STATE])
        dskip, dtb = sb("mb_d", [P, BLK]), sb("mb_dt_b", [P, BLK])
        w_x = sb("mb_w_x", [P, BLK * 48])
        w_dt = sb("mb_w_dt", [DT_RANK, D_INNER])
        w_out = sb("mb_w_out", [P, BLK * D_MODEL])
        loaded = counter(c, "mb_loaded")
        inner = s.enter_context(ExitStack())
        xnT = inner.enter_context(nc.sbuf_tensor("mb_xnT", [P, KC * TOKENS], F32))
        w_in = inner.enter_context(nc.sbuf_tensor("mb_w_in", [P, KC * 2 * D_INNER], F32))
        LOADS = [
            (w_in[:, :].rearrange("p (k e) -> p k e", k=KC), t["in_wT"].rearrange("(k p) e -> p k e", p=P)),
            (cw[:, :].rearrange("p (b k) -> p b k", b=BLK), t["conv_w"].rearrange("(b p) k -> p b k", p=P)),
            (cb[:, :], t["conv_b"]), (dskip[:, :], t["D"]), (dtb[:, :], t["dt_b"]),
            (a_coef[:, :].rearrange("p (b n) -> p b n", b=BLK), t["A_log"].rearrange("(b p) n -> p b n", p=P)),
            (w_x[:, :].rearrange("p (b e) -> p b e", b=BLK), t["x_wT"].rearrange("(b p) e -> p b e", p=P)),
            (w_dt[:, :], t["dt_wT"]),
            (w_out[:, :].rearrange("p (b e) -> p b e", b=BLK), t["out_wT"].rearrange("(b p) e -> p b e", p=P)),
        ]

        def loads(sp):
            for dst, src in LOADS:
                sp.dma_start(dst, src).then_inc(loaded.sem, 16)

        layer_norm(c, xnT, loads=loads)

        proj, fetched, padded = counter(c, "mb_proj"), counter(c, "mb_fetched"), counter(c, "mb_padded")
        own, conved, acted = counter(c, "mb_own"), counter(c, "mb_conved"), counter(c, "mb_acted")
        LEAD = D_CONV - 1
        WP = LEAD + SEQ
        with ExitStack() as q:
            xp = q.enter_context(nc.sbuf_tensor("mb_xpad", [P, 2 * WP], F32))
            cv = q.enter_context(nc.sbuf_tensor("mb_cv", [P, 2 * SEQ], F32))
            with nc.Block() as block:

                @block.tensor
                def _(pe):
                    pe.wait_ge(loaded.sem, loaded.at(16 * len(LOADS)))
                    for eb in range(2 * BLK):
                        with pe.Fori(0, BATCH // 2) as j:
                            for u in range(2):
                                n = eb * BATCH + j * 2 + u
                                if eb > 0:
                                    pe.wait_ge(fetched.sem, fetched.at(n - 1))
                                else:
                                    pe.wait_ge(fetched.sem, fetched.at(j * 2))
                                for k in range(KC):
                                    last = pe.matmul(c.banks[u][:, :],
                                                     w_in[:, k * 2 * D_INNER + eb * P:k * 2 * D_INNER + (eb + 1) * P],
                                                     xnT[:, bass.ds(j * (2 * SEQ) + (k * TOKENS + u * SEQ), SEQ)],
                                                     start=(k == 0), stop=(k == KC - 1))
                                last.then_inc(proj.sem, 1)

                @block.scalar
                def _(act):
                    for b in range(BLK):
                        with act.Fori(0, BATCH // 2) as j:
                            for u in range(2):
                                n = b * BATCH + j * 2 + u
                                act.wait_ge(proj.sem, proj.at(n + 1))
                                if b == 0:
                                    act.wait_ge(conved.sem, conved.at(j * 2))
                                else:
                                    act.wait_ge(conved.sem, conved.at(n - 1))
                                act.activation(xp[:, u * WP + LEAD:(u + 1) * WP], c.banks[u][:, :],
                                               ACT.Copy).then_inc(fetched.sem, 1)
                            for u in range(2):
                                n = b * BATCH + j * 2 + u
                                act.wait_ge(conved.sem, conved.at(n + 1))
                                act.activation(xact[:, bass.ds(j * (2 * SEQ) + (b * TOKENS + u * SEQ), SEQ)],
                                               cv[:, u * SEQ:(u + 1) * SEQ], ACT.Silu).then_inc(acted.sem, 1)
                    for b in range(BLK):
                        with act.Fori(0, BATCH // 2) as j:
                            for u in range(2):
                                act.wait_ge(proj.sem, proj.at((BLK + b) * BATCH + j * 2 + u + 1))
                                act.activation(zgate[:, bass.ds(j * (2 * SEQ) + (b * TOKENS + u * SEQ), SEQ)],
                                               c.banks[u][:, :], ACT.Silu).then_inc(fetched.sem, 1)

                @block.vector
                def _(dve):
                    dve.wait_ge(loaded.sem, loaded.at(16 * len(LOADS)))
                    for u in range(2):
                        dve.memset(xp[:, u * WP:u * WP + LEAD], 0.0).then_inc(padded.sem, 1)
                    dve.wait_ge(padded.sem, padded.at(2))
                    for b in range(BLK):
                        with dve.Fori(0, BATCH // 2) as j:
                            for u in range(2):
                                n = b * BATCH + j * 2 + u
                                st = Steps(dve, own)
                                st.loop = n * (D_CONV - 1)
                                dst = cv[:, u * SEQ:(u + 1) * SEQ]
                                tap = lambda k: cw[:, b * D_CONV + k:b * D_CONV + k + 1]
                                dve.wait_ge(fetched.sem, fetched.at(n + 1))
                                if b == 0:
                                    dve.wait_ge(acted.sem, acted.at(j * 2))
                                else:
                                    dve.wait_ge(acted.sem, acted.at(n - 1))
                                st.then(dve.tensor_scalar(dst, xp[:, u * WP + LEAD:(u + 1) * WP], tap(LEAD),
                                                          cb[:, b:b + 1], ALU.mult, ALU.add))
                                for k in reversed(range(LEAD)):
                                    op = dve.scalar_tensor_tensor(
                                        out=dst, in0=xp[:, u * WP + k:u * WP + k + SEQ], scalar=tap(k),
                                        in1=dst, op0=ALU.mult, op1=ALU.add)
                                    if k:
                                        st.then(op)
                                    else:
                                        op.then_inc(conved.sem, 1)
        proj.counted(2 * BLK * BATCH)
        fetched.counted(2 * BLK * BATCH)
        padded.counted(2)
        own.counted(BLK * BATCH * (D_CONV - 1))
        conved.counted(BLK * BATCH)
        acted.counted(BLK * BATCH)
        inner.close()

        dt = sb("mb_dt", [P, BLK * TOKENS])
        ux = sb("mb_ux", [P, BLK * TOKENS])
        bcT = t["scratch_bc"]
        xdbl, xkept, stored = counter(c, "mb_xdbl"), counter(c, "mb_xkept"), counter(c, "mb_bc_stored")
        dtp, dtr = counter(c, "mb_dtp"), counter(c, "mb_dtr")
        soft, summed = counter(c, "mb_soft"), counter(c, "mb_summed")
        with ExitStack() as q:
            dbl = q.enter_context(nc.sbuf_tensor("mb_dbl", [48, TOKENS], F32))
            with nc.Block() as block:

                @block.tensor
                def _(pe):
                    for b in range(BATCH):
                        if b >= 2:
                            pe.wait_ge(xkept.sem, xkept.at(b - 1))
                        for k in range(BLK):
                            last = pe.matmul(c.banks[b % 2][0:48, :], w_x[:, k * 48:(k + 1) * 48],
                                             xact[:, k * TOKENS + b * SEQ:k * TOKENS + (b + 1) * SEQ],
                                             start=(k == 0), stop=(k == BLK - 1))
                        last.then_inc(xdbl.sem, 1)
                    pe.wait_ge(xkept.sem, xkept.at(BATCH))
                    for n in range(BLK * BATCH):
                        k, b = divmod(n, BATCH)
                        if n >= 2:
                            pe.wait_ge(dtr.sem, dtr.at(2 * (n - 1)))
                        pe.matmul(c.banks[2 + n % 2][:, :], w_dt[:, k * P:(k + 1) * P],
                                  dbl[0:DT_RANK, b * SEQ:(b + 1) * SEQ], start=True, stop=True) \
                          .then_inc(dtp.sem, 1)

                @block.vector
                def _(dve):
                    for n in range(BLK * BATCH):
                        k = n // BATCH
                        at = slice(n * SEQ, (n + 1) * SEQ)
                        dve.wait_ge(dtp.sem, dtp.at(n + 1))
                        dve.tensor_scalar(ux[:, at], c.banks[2 + n % 2][:, :], dtb[:, k:k + 1], 0.0,
                                          ALU.add, ALU.max).then_inc(dtr.sem, 1)
                        dve.wait_ge(dtr.sem, dtr.at(2 * n + 1))
                        dve.scalar_tensor_tensor(out=dt[:, at], in0=ux[:, at], scalar=-2.0,
                                                 in1=c.banks[2 + n % 2][:, :], op0=ALU.mult, op1=ALU.add) \
                           .then_inc(dtr.sem, 1)
                    for k in range(BLK):
                        at = slice(k * TOKENS, (k + 1) * TOKENS)
                        dve.wait_ge(soft.sem, soft.at(2 + BLK + k + 1))
                        dve.tensor_tensor(dt[:, at], dt[:, at], ux[:, at], ALU.add).then_inc(summed.sem, 1)
                        dve.wait_ge(summed.sem, summed.at(k + 1))
                        dve.tensor_tensor(ux[:, at], dt[:, at], xact[:, at], ALU.mult)

                @block.scalar
                def _(act):
                    for b in range(BATCH):
                        act.wait_ge(xdbl.sem, xdbl.at(b + 1))
                        act.activation(dbl[:, b * SEQ:(b + 1) * SEQ], c.banks[b % 2][0:48, :],
                                       ACT.Copy).then_inc(xkept.sem, 1)
                    act.activation(a_coef[:, :], a_coef[:, :], ACT.Exp).then_inc(soft.sem, 1)
                    act.wait_ge(soft.sem, soft.at(1))
                    act.activation(a_coef[:, :], a_coef[:, :], ACT.Copy, scale=-1.0).then_inc(soft.sem, 1)
                    for k in range(BLK):
                        at = slice(k * TOKENS, (k + 1) * TOKENS)
                        act.wait_ge(dtr.sem, dtr.at(2 * (k + 1) * BATCH))
                        act.activation(dt[:, at], dt[:, at], ACT.Exp, bias=dtb[:, k:k + 1]).then_inc(soft.sem, 1)
                    for k in range(BLK):
                        at = slice(k * TOKENS, (k + 1) * TOKENS)
                        act.wait_ge(soft.sem, soft.at(2 + k + 1))
                        act.activation(dt[:, at], dt[:, at], ACT.Ln, bias=1.0).then_inc(soft.sem, 1)

                @block.sync
                def _(sp):
                    sp.wait_ge(xkept.sem, xkept.at(BATCH))
                    sp.dma_start(bcT, dbl[DT_RANK:48, :]).then_inc(stored.sem, 16)
                    sp.wait_ge(stored.sem, stored.at(16))
        for q, n in ((xdbl, BATCH), (xkept, BATCH), (stored, 16), (dtp, BLK * BATCH),
                     (dtr, 2 * BLK * BATCH), (soft, 2 + 2 * BLK), (summed, BLK)):
            q.counted(n)

        mamba_scan(c, xact, zgate, dt, ux, a_coef, dskip, bcT)

        outp, added = counter(c, "mb_outp"), counter(c, "mb_added")
        with nc.Block() as block:

            @block.tensor
            def _(pe):
                for i in range(TILES):
                    if i >= 2:
                        pe.wait_ge(added.sem, added.at(i - 1))
                    for k in range(BLK):
                        last = pe.matmul(c.banks[i % 2][:, 0:D_MODEL],
                                         xact[:, k * TOKENS + i * P:k * TOKENS + (i + 1) * P],
                                         w_out[:, k * D_MODEL:(k + 1) * D_MODEL],
                                         start=(k == 0), stop=(k == BLK - 1))
                    last.then_inc(outp.sem, 1)

            @block.vector
            def _(dve):
                for i in range(TILES):
                    at = slice(i * D_MODEL, (i + 1) * D_MODEL)
                    dve.wait_ge(outp.sem, outp.at(i + 1))
                    dve.tensor_tensor(c.x[:, at], c.x[:, at], c.banks[i % 2][:, 0:D_MODEL],
                                      ALU.add).then_inc(added.sem, 1)
        outp.counted(TILES)
        added.counted(TILES)


def mamba_scan(c, xact, zgate, dt, ux, a_coef, dskip, bcT):
    nc = c.nc
    ST = BLK * D_STATE
    NH = 3
    rows = [counter(c, f"sc_rows{u}") for u in range(2)]
    decay, input_, scanned = (counter(c, n) for n in ("sc_decay", "sc_input", "sc_scanned"))
    used, out, opened, edge = (counter(c, n) for n in ("sc_used", "sc_out", "sc_opened", "sc_edge"))
    summed, gated, own = counter(c, "sc_summed"), counter(c, "sc_gated"), counter(c, "sc_own")
    with ExitStack() as s:
        sb = lambda name, shape, dt=F32: s.enter_context(nc.sbuf_tensor(name, shape, dt))
        da = sb("sc_da", [P, 2 * HALF])
        hb = sb("sc_h", [P, 4 * HALF])
        bc = sb("sc_bc", [P, 4 * HALF])
        DA = [da[:, u * HALF:(u + 1) * HALF] for u in range(2)]
        H = [hb[:, u * HALF:(u + 1) * HALF] for u in range(4)]
        B = [bc[:, u * 2 * HALF:u * 2 * HALF + HALF] for u in range(2)]
        C = [bc[:, u * 2 * HALF + HALF:(u + 1) * 2 * HALF] for u in range(2)]
        POOL_B = (0,)
        for half in range(2):
            lo = half * HALF
            with nc.Block() as block:

                @block.sync
                def _(sp):
                    def fetch(n, u):
                        for dst, row in ((B[u], n), (C[u], n + D_STATE)):
                            sp.dma_start(dst, bcT[bass.ds(row, 1), lo:lo + HALF].to_broadcast([P, HALF])) \
                              .then_inc(rows[u].sem, 16)

                    for u in range(2):
                        fetch(u, u)
                    with sp.Fori(0, D_STATE // 2 - 1) as j:
                        for u in range(2):
                            sp.wait_ge(used.sem, used.at(j * (2 * BLK) + (u + 1) * BLK))
                            fetch(j * 2 + (u + 2), u)

                @block.scalar
                def _(act):
                    with act.Fori(0, D_STATE // 2) as j:
                        for v in range(2 * BLK):
                            n, b = divmod(v, BLK)
                            step = j * (2 * BLK) + v
                            if v >= 2:
                                act.wait_ge(scanned.sem, scanned.at(step - 1))
                            else:
                                act.wait_ge(scanned.sem, scanned.at(j * (2 * BLK)))
                            act.wait_ge(edge.sem, edge.at(2))
                            act.activation(
                                DA[v % 2].rearrange("p (b t) -> p b t", b=2)[:, :, 1:SEQ],
                                dt[:, b * TOKENS + lo:b * TOKENS + lo + HALF]
                                .rearrange("p (b t) -> p b t", b=2)[:, :, 1:SEQ],
                                ACT.Exp, scale=a_coef[:, bass.ds(j * 2 + (b * D_STATE + n), 1)]) \
                               .then_inc(decay.sem, 1)

                @block.gpsimd
                def _(pool):
                    with pool.Fori(0, D_STATE // 2) as j:
                        for v in range(2 * BLK):
                            n, b = divmod(v, BLK)
                            step = j * (2 * BLK) + v
                            if b in POOL_B:
                                pool.wait_ge(rows[n].sem, rows[n].at(j * 32 + 32))
                                if v >= 4:
                                    pool.wait_ge(out.sem, out.at(step - 3))
                                else:
                                    pool.wait_ge(out.sem, out.at(j * (2 * BLK)))
                                pool.tensor_tensor(H[v % 4], ux[:, b * TOKENS + lo:b * TOKENS + lo + HALF],
                                                   B[n], ALU.mult).then_inc(input_.sem, 1)
                            pool.wait_ge(scanned.sem, scanned.at(step + 1))
                            pool.tensor_tensor(H[v % 4], H[v % 4], C[n], ALU.mult).then_inc(used.sem, 1)

                @block.vector
                def _(dve):
                    for u in range(2):
                        dve.memset(DA[u].rearrange("p (b t) -> p b t", b=2)[:, :, 0:1], 0.0) \
                           .then_inc(edge.sem, 1)
                    dve.wait_ge(edge.sem, edge.at(2))
                    with dve.Fori(0, D_STATE // 2) as j:
                        for v in range(2 * BLK):
                            n, b = divmod(v, BLK)
                            step = j * (2 * BLK) + v
                            if b in POOL_B:
                                dve.wait_ge(input_.sem, input_.at(j * (2 * len(POOL_B)) + n + 1))
                            else:
                                dve.wait_ge(rows[n].sem, rows[n].at(j * 32 + 32))
                                if v >= 4:
                                    dve.wait_ge(out.sem, out.at(step - 3))
                                else:
                                    dve.wait_ge(out.sem, out.at(j * (2 * BLK)))
                                dve.tensor_tensor(H[v % 4], ux[:, b * TOKENS + lo:b * TOKENS + lo + HALF],
                                                  B[n], ALU.mult).then_inc(own.sem, 1)
                                dve.wait_ge(own.sem, own.at(j * (2 * (BLK - 1)) + n * (BLK - 1) + b))
                            dve.wait_ge(decay.sem, decay.at(step + 1))
                            dve.tensor_tensor_scan(H[v % 4], DA[v % 2], H[v % 4], 0.0, ALU.mult, ALU.add) \
                               .then_inc(scanned.sem, 1)
                    for b in range(BLK):
                        at = slice(b * TOKENS + lo, b * TOKENS + lo + HALF)
                        for q in range(2):
                            cut = slice(b * TOKENS + lo + q * SEQ, b * TOKENS + lo + (q + 1) * SEQ)
                            dve.wait_ge(summed.sem, summed.at(1))
                            dve.scalar_tensor_tensor(out=xact[:, cut], in0=xact[:, cut],
                                                     scalar=dskip[:, b:b + 1], in1=c.banks[2 * b + q][:, :],
                                                     op0=ALU.mult, op1=ALU.add).then_inc(gated.sem, 1)
                    dve.wait_ge(gated.sem, gated.at(2 * BLK))
                    for b in range(BLK):
                        at = slice(b * TOKENS + lo, b * TOKENS + lo + HALF)
                        dve.tensor_tensor(xact[:, at], xact[:, at], zgate[:, at], ALU.mult)

                @block.tensor
                def _(pe):
                    for k in range(8):
                        pe.matmul(c.banks[k][:, :], c.zeros[:, 0:P], c.zeros[:, :], start=True, stop=False)
                    with pe.Fori(0, D_STATE // 2) as j:
                        for v in range(2 * BLK):
                            b = v % BLK
                            pe.wait_ge(used.sem, used.at(j * (2 * BLK) + v + 1))
                            for q in range(2):
                                last = pe.matmul(c.banks[2 * b + q][:, :], c.ident[:, :],
                                                 H[v % 4][:, q * SEQ:(q + 1) * SEQ], start=False, stop=False)
                            last.then_inc(out.sem, 1)
                    for k in range(8):
                        last = pe.matmul(c.banks[k][:, :], c.zeros[:, 0:P], c.zeros[:, :], start=False, stop=True)
                    last.then_inc(summed.sem, 1)
            for q, n in ((rows[0], 16 * D_STATE), (rows[1], 16 * D_STATE), (decay, ST), (scanned, ST), (used, ST), (out, ST), (edge, 2),
                         (input_, len(POOL_B) * D_STATE), (own, (BLK - len(POOL_B)) * D_STATE),
                         (summed, 1), (gated, 2 * BLK)):
                q.counted(n)


def moe(c, which):
    nc, t = c.nc, c.t
    if which == 0:
        E, K, I, ROWS, NT, cap = M0_E, M0_K, M0_I, P, M0_TILES, None
    else:
        E, K, I, ROWS, NT, cap = M1_E, M1_K, M1_I, M1_CAP, M1_E, M1_CAP
    xs, ys = t[f"scratch_xs{which}"], t[f"scratch_ys{which}"]
    GU = 2 * I
    TK = TILES * K
    EB = -(-E * TILES // 512)
    TPBANK = TILES // EB
    with ExitStack() as s:
        sb = lambda name, shape, dt=F32: s.enter_context(nc.sbuf_tensor(name, shape, dt, allow_name_mangling=True))
        slots = sb("mo_slots", [P, TK], I32)
        weights = sb("mo_weights", [P, TK])
        tile_expert = sb("mo_tile_expert", [1, NT], I32) if cap is None else None
        w_gu = sb("mo_w_gu", [P, E * KC * GU])
        w_dn = sb("mo_w_dn", [I, E * D_MODEL])
        if which == 0:
            b_gu, b_dn = sb("mo_b_gu", [3, E * GU], BF16), sb("mo_b_dn", [3, E * D_MODEL], BF16)
        loaded, weights_in = counter(c, "mo_loaded"), counter(c, "mo_weights_in")
        scope = s.enter_context(ExitStack())
        sc = lambda name, shape, dt=F32: scope.enter_context(nc.sbuf_tensor(name, shape, dt, allow_name_mangling=True))
        xn = sc("mo_xn", [P, TILES * D_MODEL])
        gate = sc("mo_gate", [P, KC * E])
        bias = sc("mo_gate_b", [P, E])
        if which == 0:
            braw = sc("mo_braw", [E, GU + D_MODEL])
        else:
            gold, o2n = sc("mo_gold", [M1_OLD, D_MODEL]), sc("mo_o2n", [M1_OLD, 1], I32)
        WEIGHTS = [(w_gu[:, :], t[f"w_gu{which}"]), (w_dn[:, :], t[f"w_dn{which}"])]
        if which == 0:
            LOADS = [(gate[:, :].rearrange("p (k e) -> p k e", k=KC), t["gate0T"].rearrange("(k p) e -> p k e", p=P)),
                      (bias[:, :], t["gate_b"].to_broadcast([P, E])), (braw[:, :], t["b_all"])]
        else:
            LOADS = [(gold[:, :], t["gate1"]), (o2n[:, :], t["o2n"])]

        def loads(sp):
            for dst, src in LOADS:
                sp.dma_start(dst, src).then_inc(loaded.sem, 16)
            for dst, src in WEIGHTS:
                sp.dma_start(dst, src).then_inc(weights_in.sem, 16)
            sp.wait_ge(loaded.sem, loaded.at(16 * len(LOADS)))

        logit, ldone, own, pown = (counter(c, n) for n in ("mo_logit", "mo_ldone", "mo_own", "mo_pown"))
        made, ranked, expd, counted_, moved, bsplit, bstored = (
            counter(c, n) for n in ("mo_made", "mo_ranked", "mo_expd", "mo_counted", "mo_moved", "mo_bsplit", "mo_bstored"))
        placed = counter(c, "mo_placed")
        with ExitStack() as q:
            sq = lambda name, shape, dt=F32: q.enter_context(nc.sbuf_tensor(name, shape, dt, allow_name_mangling=True))
            lg = sq("mo_lg", [P, TILES * E])
            iota_e = sq("mo_iota_e", [P, E])
            with ExitStack() as qq:
                xnT = qq.enter_context(nc.sbuf_tensor("mo_xnT", [P, KC * TOKENS], F32, allow_name_mangling=True))
                layer_norm(c, xnT, xn=xn, loads=loads)
                if which == 1:
                    remap_gate(c, gold, o2n, iota_e, gate, bias)
                with nc.Block() as block:

                    @block.tensor
                    def _(pe):
                        for i in range(TILES):
                            for k in range(KC):
                                last = pe.matmul(c.banks[i // TPBANK][:, (i % TPBANK) * E:(i % TPBANK + 1) * E],
                                                 xnT[:, k * TOKENS + i * P:k * TOKENS + (i + 1) * P],
                                                 gate[:, k * E:(k + 1) * E], start=(k == 0), stop=(k == KC - 1))
                        last.then_inc(logit.sem, 1)

                    @block.vector
                    def _(dve):
                        dve.wait_ge(logit.sem, logit.at(1))
                        for g in range(EB):
                            cut = slice(g * TPBANK * E, (g + 1) * TPBANK * E)
                            dve.tensor_tensor(lg[:, cut].rearrange("p (t e) -> p t e", e=E),
                                              c.banks[g][:, 0:TPBANK * E].rearrange("p (t e) -> p t e", e=E),
                                              bias[:, :].rearrange("p (t e) -> p t e", t=1)
                                              .to_broadcast([P, TPBANK, E]), ALU.add).then_inc(ldone.sem, 1)
            logit.counted(1)
            ldone.counted(EB)
            upper = sq("mo_upper", [P, P], BF16)
            top, topi, topf = sq("mo_top", [P, TILES * 8]), sq("mo_topi", [P, TILES * 8], U32), sq("mo_topf", [P, TK])
            hot = sq("mo_hot", [P, TK * E])
            mask = sq("mo_mask", [P, TILES * E], BF16)
            reset = sq("mo_reset", [P, E * TILES])
            incl = sq("mo_incl", [P, E * TILES])
            pos = sq("mo_pos", [P, TILES * E])
            cnt, nt, start, off = (sq(n, [P, E]) for n in ("mo_cnt", "mo_nt", "mo_start", "mo_off"))
            ssum = sq("mo_ssum", [P, TILES])
            slotf = sq("mo_slotf", [P, TK])
            te = lambda a: a[:, :].rearrange("p (t e) -> p t e", e=E)
            et = lambda a: a[:, :].rearrange("p (e t) -> p e t", t=TILES)
            if cap is None:
                steps16 = sq("mo_steps16", [P, E * TILES])
                over = sq("mo_over", [P, E * TILES])
                tile_id = sq("mo_tile_id", [NT, 1])
                before = sq("mo_before", [NT, E])
                texp = sq("mo_texp", [NT, 1])
                bparts = [sq(f"mo_bpart{i}", [E, GU + D_MODEL], BF16) for i in range(3)]

            with nc.Block() as block:

                @block.gpsimd
                def _(pool):
                    small = dict(allow_small_or_imprecise_dtypes=True)
                    pool.iota(iota_e[:, :], [[1, E]], 0, 0, **small).then_inc(made.sem, 1)
                    pool.memset(reset[:, :], 1.0).then_inc(pown.sem, 1)
                    pool.wait_ge(pown.sem, pown.at(1))
                    pool.memset(et(reset)[:, :, 0:1], 0.0)
                    pool.memset(upper[:, :], 1.0).then_inc(pown.sem, 1)
                    pool.wait_ge(pown.sem, pown.at(2))
                    pool.affine_select(out=upper[:, :], in_=upper[:, :], compare_op=ALU.is_gt, fill=0.0,
                                       base=0, pattern=[[1, P]], channel_multiplier=-1).then_inc(made.sem, 1)
                    if cap is None:
                        pool.iota(steps16[:, :], [[0, E], [ROWS, TILES]], 0, 0, **small).then_inc(made.sem, 1)
                        pool.iota(tile_id[:, :], [[0, 1]], 0, 1, **small).then_inc(made.sem, 1)
                    else:
                        pool.iota(off[:, :], [[ROWS, E]], 0, 0, **small).then_inc(made.sem, 2)

                @block.tensor
                def _(pe):
                    pe.wait_ge(ranked.sem, ranked.at(1))
                    pe.wait_ge(made.sem, made.at(4))
                    for g in range(EB):
                        cut = slice(g * TPBANK * E, (g + 1) * TPBANK * E)
                        pe.matmul(c.banks[g][:, 0:TPBANK * E], upper[:, :], mask[:, cut], start=True, stop=True)
                        last = pe.matmul(c.banks[EB + g][:, 0:TPBANK * E], c.ones[:, :], mask[:, cut],
                                         start=True, stop=True)
                    last.then_inc(counted_.sem, 1)
                    if cap is None:
                        pe.wait_ge(placed.sem, placed.at(1))
                        pe.matmul(c.banks[7][0:1, 0:NT], texp[:, :], c.ident[0:NT, 0:NT], start=True, stop=True) \
                          .then_inc(placed.sem, 1)

                @block.scalar
                def _(act):
                    act.wait_ge(expd.sem, expd.at(1))
                    act.activation(weights[:, :], weights[:, :], ACT.Exp).then_inc(expd.sem, 1)

                if which == 0:
                    @block.sync
                    def _(sp):
                        sp.wait_ge(bsplit.sem, bsplit.at(5))
                        for i in range(3):
                            sp.dma_start(b_gu[i:i + 1, :].rearrange("a (e n) -> a e n", e=E),
                                         bparts[i][:, 0:GU]) \
                              .then_inc(bstored.sem, 16)
                            sp.dma_start(b_dn[i:i + 1, :].rearrange("a (e n) -> a e n", e=E),
                                         bparts[i][:, GU:]) \
                              .then_inc(bstored.sem, 16)
                        sp.wait_ge(bstored.sem, bstored.at(96))

                @block.vector
                def _(dve):
                    st = Steps(dve, own)
                    if which == 0:
                        sp_ = Steps(dve, bsplit)
                        sp_.then(dve.tensor_copy(bparts[0][:, :], braw[:, :]))
                        sp_.then(dve.tensor_tensor(braw[:, :], braw[:, :], bparts[0][:, :], ALU.subtract))
                        sp_.then(dve.tensor_copy(bparts[1][:, :], braw[:, :]))
                        sp_.then(dve.tensor_tensor(braw[:, :], braw[:, :], bparts[1][:, :], ALU.subtract))
                        sp_.then(dve.tensor_copy(bparts[2][:, :], braw[:, :]))
                    for i in range(TILES):
                        dve.max(top[:, i * 8:(i + 1) * 8], lg[:, i * E:(i + 1) * E]).then_inc(own.sem, 1)
                    dve.wait_ge(own.sem, own.at(TILES))
                    for i in range(TILES):
                        dve.max_index(topi[:, i * 8:(i + 1) * 8], top[:, i * 8:(i + 1) * 8],
                                      lg[:, i * E:(i + 1) * E]).then_inc(own.sem, 1)
                    dve.wait_ge(own.sem, own.at(2 * TILES))
                    st.n = 2 * TILES
                    top3 = top[:, :].rearrange("p (t k) -> p t k", k=8)
                    wk = weights[:, :].rearrange("p (t k) -> p t k", k=K)
                    st.then(dve.tensor_copy(topf[:, :].rearrange("p (t k) -> p t k", k=K),
                                            topi[:, :].rearrange("p (t k) -> p t k", k=8)[:, :, 0:K]))
                    dve.tensor_tensor(wk, top3[:, :, 0:K], top3[:, :, 0:1].to_broadcast([P, TILES, K]),
                                      ALU.subtract).then_inc(expd.sem, 1)
                    dve.wait_ge(made.sem, made.at(1))
                    hot3 = hot[:, :].rearrange("p (n e) -> p n e", e=E)
                    st.then(dve.tensor_tensor(
                        hot3, topf[:, :].rearrange("p (n o) -> p n o", o=1).to_broadcast([P, TK, E]),
                        iota_e[:, :].rearrange("p (o e) -> p o e", o=1).to_broadcast([P, TK, E]), ALU.is_equal))
                    hot4 = hot[:, :].rearrange("p (t k e) -> p t k e", k=K, e=E)
                    for k in range(1, K):
                        if k == 1:
                            st.then(dve.tensor_tensor(te(mask), hot4[:, :, 0, :], hot4[:, :, 1, :], ALU.add))
                        else:
                            op = dve.tensor_tensor(te(mask), te(mask), hot4[:, :, k, :], ALU.add)
                            if k < K - 1:
                                st.then(op)
                            else:
                                op.then_inc(ranked.sem, 1)
                    dve.wait_ge(expd.sem, expd.at(2))
                    st.then(dve.tensor_reduce(ssum[:, :], wk, AX, ALU.add))
                    st.then(dve.reciprocal(ssum[:, :], ssum[:, :]))
                    st.then(dve.tensor_tensor(wk, wk, ssum[:, :].rearrange("p (t o) -> p t o", o=1)
                                              .to_broadcast([P, TILES, K]), ALU.mult))
                    dve.wait_ge(made.sem, made.at(4))
                    dve.wait_ge(counted_.sem, counted_.at(1))
                    for g in range(EB):
                        st.then(dve.tensor_copy(
                            et(incl)[:, :, g * TPBANK:(g + 1) * TPBANK],
                            c.banks[EB + g][:, 0:TPBANK * E].rearrange("p (t e) -> p e t", e=E)))
                    st.then(dve.tensor_copy(pos[:, :].rearrange("p (t e) -> p e t", e=E), et(incl)))
                    st.then(dve.tensor_tensor_scan(incl[:, :], reset[:, :], incl[:, :], 0.0, ALU.mult, ALU.add))
                    st.then(dve.tensor_tensor(te(pos), incl[:, :].rearrange("p (e t) -> p t e", t=TILES),
                                              te(pos), ALU.subtract))
                    for g in range(EB):
                        cut = slice(g * TPBANK * E, (g + 1) * TPBANK * E)
                        st.then(dve.tensor_tensor(pos[:, cut], pos[:, cut], c.banks[g][:, 0:TPBANK * E], ALU.add))
                    whole = lambda a, n: a.rearrange("p (o e) -> p o e", o=1).to_broadcast([a.shape[0], n, E])
                    if cap is None:
                        st.then(dve.tensor_copy(cnt[:, :], et(incl)[:, :, TILES - 1]))
                        st.then(dve.tensor_tensor(et(over), cnt[:, :].rearrange("p (e o) -> p e o", o=1)
                                                  .to_broadcast([P, E, TILES]), et(steps16), ALU.is_gt))
                        st.then(dve.tensor_reduce(nt[:, :], et(over), AX, ALU.add))
                        st.then(dve.memset(cnt[:, :], 1.0))
                        st.then(dve.tensor_tensor_scan(start[:, :], cnt[:, :], nt[:, :], 0.0, ALU.mult, ALU.add))
                        st.then(dve.tensor_tensor(start[:, :], start[:, :], nt[:, :], ALU.subtract))
                        st.then(dve.tensor_scalar(off[:, :], start[:, :], float(ROWS), None, ALU.mult))
                        st.then(dve.tensor_scalar(before[:, :], start[0:NT, :], tile_id[:, 0:1], None, ALU.is_le))
                        st.then(dve.tensor_reduce(texp[:, :], before[:, :], AX, ALU.add))
                        dve.tensor_scalar(texp[:, :], texp[:, :], -1.0, None, ALU.add).then_inc(placed.sem, 1)
                        dve.wait_ge(placed.sem, placed.at(2))
                        st.then(dve.tensor_copy(tile_expert[:, :], c.banks[7][0:1, 0:NT]))
                        st.then(dve.tensor_tensor(te(pos), te(pos), whole(off[:, :], TILES), ALU.add))
                    else:
                        st.then(dve.tensor_scalar(incl[:, :], pos[:, :], float(cap), FAR, ALU.is_ge, ALU.mult))
                        st.then(dve.tensor_tensor(pos[:, :], pos[:, :], incl[:, :], ALU.add))
                        st.then(dve.tensor_tensor(te(pos), te(pos), whole(off[:, :], TILES), ALU.add))
                    for k in range(K):
                        st.then(dve.tensor_tensor(hot4[:, :, k, :], hot4[:, :, k, :], te(pos), ALU.mult))
                    st.then(dve.tensor_reduce(slotf[:, :], hot3, AX, ALU.add))
                    st.then(dve.tensor_copy(slots[:, :], slotf[:, :]))
                    if cap is not None:
                        st.then(dve.tensor_scalar(slotf[:, :], slotf[:, :], float(NT * ROWS), None, ALU.is_lt))
                        st.then(dve.tensor_tensor(weights[:, :], weights[:, :], slotf[:, :], ALU.mult))
                    moe.own = st.n
            own.counted(moe.own)
            for w, n in ((placed, 2 if cap is None else 0), (made, 4), (pown, 2), (expd, 2), (ranked, 1), (counted_, 1),
                         (bsplit, 5 if which == 0 else 0), (bstored, 96 if which == 0 else 0)):
                w.counted(n)

            with nc.Block() as block:

                @block.gpsimd
                def _(pool):
                    pool.wait_ge(c.filled.sem, 16 * c.fills)
                    for n in range(TK):
                        i = n // K
                        pool.indirect_dma_start(xs, bass.IndirectOffsetOnAxis(ap=slots[:, n:n + 1], axis=0),
                                                xn[:, i * D_MODEL:(i + 1) * D_MODEL], None,
                                                bounds_check=NT * ROWS - 1, oob_is_err=False) \
                            .then_inc(moved.sem, 16)
                    pool.wait_ge(moved.sem, moved.at(16 * TK))
            moved.counted(16 * TK)
        scope.close()
        loaded.counted(16 * len(LOADS))

        experts(c, which, E, I, ROWS, NT, xs, ys, w_gu, w_dn, (b_gu, b_dn) if which == 0 else None, tile_expert,
                (weights_in.sem, weights_in.at(16 * len(WEIGHTS))))
        weights_in.counted(16 * len(WEIGHTS))

        NB = 16
        fetched = [counter(c, f"mo_fetched{i}") for i in range(NB)]
        added = counter(c, "mo_added")
        with ExitStack() as q:
            yb = q.enter_context(nc.sbuf_tensor("mo_yb", [P, NB * D_MODEL], F32, allow_name_mangling=True))
            with nc.Block() as block:

                @block.gpsimd
                def _(pool):
                    if cap is not None:
                        pool.memset(yb[:, :], 0.0).then_inc(pown.sem, 1)
                        pool.wait_ge(pown.sem, pown.at(1))
                    for n in range(TK):
                        u = n % NB
                        if n >= NB:
                            pool.wait_ge(added.sem, added.at(n - NB + 1))
                        pool.indirect_dma_start(yb[:, u * D_MODEL:(u + 1) * D_MODEL], None, ys,
                                                bass.IndirectOffsetOnAxis(ap=slots[:, n:n + 1], axis=0),
                                                bounds_check=NT * ROWS - 1, oob_is_err=False) \
                            .then_inc(fetched[u].sem, 16)

                @block.vector
                def _(dve):
                    for n in range(TK):
                        u, i = n % NB, n // K
                        at = slice(i * D_MODEL, (i + 1) * D_MODEL)
                        dve.wait_ge(fetched[u].sem, fetched[u].at(16 * (n // NB + 1)))
                        if n % K:
                            dve.wait_ge(added.sem, added.at(n))
                        dve.scalar_tensor_tensor(out=c.x[:, at], in0=yb[:, u * D_MODEL:(u + 1) * D_MODEL],
                                                 scalar=weights[:, n:n + 1], in1=c.x[:, at],
                                                 op0=ALU.mult, op1=ALU.add).then_inc(added.sem, 1)
        added.counted(TK)
        if cap is not None:
            pown.counted(1)
        for u in range(NB):
            fetched[u].counted(16 * (TK // NB))


def remap_gate(c, gold, o2n, iota_e, gate, bias):
    nc = c.nc
    E = M1_E
    made, own, mm = counter(c, "rg_made"), counter(c, "rg_own"), counter(c, "rg_mm")
    with ExitStack() as s:
        sb = lambda name, shape, dt=F32: s.enter_context(nc.sbuf_tensor(name, shape, dt, allow_name_mangling=True))
        o2f, m, mb = sb("rg_o2f", [P, 1]), sb("rg_m", [P, E]), sb("rg_mb", [P, E], BF16)
        with nc.Block() as block:

            @block.gpsimd
            def _(pool):
                pool.iota(m[:, :], [[1, E]], 0, 0, allow_small_or_imprecise_dtypes=True).then_inc(made.sem, 1)

            @block.vector
            def _(dve):
                st = Steps(dve, own)
                st.then(dve.tensor_copy(o2f[:, :], o2n[:, :]))
                dve.wait_ge(made.sem, made.at(1))
                st.then(dve.tensor_scalar(m[:, :], m[:, :], o2f[:, 0:1], None, ALU.is_equal))
                st.then(dve.tensor_copy(mb[:, :], m[:, :]))
                dve.wait_ge(mm.sem, mm.at(1))
                for k in range(KC):
                    dve.tensor_copy(gate[:, k * E:(k + 1) * E], c.banks[k][:, 0:E])
                st.then(dve.tensor_scalar(bias[:, :], c.banks[KC][:, 0:E], 0.5, None, ALU.is_lt))
                dve.tensor_scalar(bias[:, :], bias[:, :], NEG, None, ALU.mult)

            @block.tensor
            def _(pe):
                pe.wait_ge(own.sem, own.at(3))
                for k in range(KC):
                    pe.matmul(c.banks[k][:, 0:E], gold[:, k * P:(k + 1) * P], m[:, :], start=True, stop=True)
                pe.matmul(c.banks[KC][:, 0:E], c.ones[:, :], mb[:, :], start=True, stop=True).then_inc(mm.sem, 1)
    made.counted(1)
    own.counted(4)
    mm.counted(1)


def experts(c, which, E, I, ROWS, NT, xs, ys, w_gu, w_dn, biases, tile_expert, weights_in):
    nc = c.nc
    GU = 2 * I
    NR = 4
    rows_in = [counter(c, f"ex_rows_in{u}") for u in range(NR)]
    rows_out = [counter(c, f"ex_rows_out{u}") for u in range(NR)]
    x_turned, x_kept, gate_done, clipped, act_done, gated, hidden_done, h_turned, h_kept, down_done, y_kept = (
        counter(c, "ex_" + n) for n in ("x_turned", "x_kept", "gate_up", "clipped", "act", "gated", "hidden",
                                       "h_turned", "h_kept", "down", "y_kept"))

    def steps(eng, step):
        for i in range(NR):
            step(i, i)
        with eng.Fori(0, NT // NR - 2) as j:
            for v in range(NR):
                step(j * NR + (NR + v), v)
        for i in range(NT - NR, NT + NR):
            step(i, i % NR)

    def exists(i):
        return not isinstance(i, int) or 0 <= i < NT

    with ExitStack() as s:
        sb = lambda name, shape, dt=F32: s.enter_context(nc.sbuf_tensor(name, shape, dt, allow_name_mangling=True))
        xr = [sb(f"ex_xr{u}", [ROWS, D_MODEL]) for u in range(NR)]
        yo = [sb(f"ex_yo{u}", [ROWS, D_MODEL]) for u in range(NR)]
        xT = [sb(f"ex_xT{u}", [P, KC * ROWS]) for u in range(2)]
        g, up, sg, h = ([sb(f"ex_{n}{u}", [ROWS, I]) for u in range(2)] for n in ("g", "up", "sg", "h"))
        hT = [sb(f"ex_hT{u}", [I, ROWS]) for u in range(2)]
        XT, GUB, HT, YB = (c.banks[2 * k:2 * k + 2] for k in range(4))

        with nc.Block() as block:

            @block.sync
            def _(sp):
                def load(i, u):
                    sp.dma_start(xr[u][:, :], xs[bass.ds(i * ROWS, ROWS), :]).then_inc(rows_in[u].sem, 16)

                def store(i, u):
                    sp.wait_ge(y_kept.sem, y_kept.at(i + 1))
                    sp.dma_start(ys[bass.ds(i * ROWS, ROWS), :], yo[u][:, :]).then_inc(rows_out[u].sem, 16)

                def turn(i, u):
                    sp.wait_ge(x_turned.sem, x_turned.at(i + 1))
                    load(i + NR, u)

                for u in range(NR):
                    load(u, u)
                for u in range(NR):
                    turn(u, u)
                with sp.Fori(0, NT // NR - 2) as j:
                    for u in range(NR):
                        turn(j * NR + (u + NR), u)
                        store(j * NR + u, u)
                for i in range(NT - 2 * NR, NT):
                    store(i, i % NR)
                for u in range(NR):
                    sp.wait_ge(rows_out[u].sem, rows_out[u].at(16 * (NT // NR)))

            @block.tensor
            def _(pe):
                def turn_x(i, phase):
                    u, r = phase % 2, phase % NR
                    pe.wait_ge(rows_in[r].sem, rows_in[r].at(i * (16 // NR) + (NR - r) * (16 // NR)))
                    for k in range(KC):
                        last = pe.transpose(XT[u][:, k * ROWS:(k + 1) * ROWS], xr[r][:, k * P:(k + 1) * P],
                                            c.ident[0:ROWS, 0:ROWS])
                    last.then_inc(x_turned.sem, 1)

                def expert_of(i):
                    if tile_expert is None:
                        return i
                    return pe.value_load(tile_expert[0:1, bass.ds(i, 1)], min_val=0, max_val=E - 1)

                def gate_up(i, phase):
                    u, e = phase % 2, expert_of(i)
                    pe.wait_ge(x_kept.sem, x_kept.at(i + 1))
                    for k in range(KC):
                        last = pe.matmul(GUB[u][0:ROWS, 0:GU], xT[u][:, k * ROWS:(k + 1) * ROWS],
                                         w_gu[:, bass.ds(e * (KC * GU) + k * GU, GU)],
                                         start=(k == 0), stop=(k == KC - 1 and biases is None))
                    if biases is not None:
                        last = pe.matmul(GUB[u][0:ROWS, 0:GU], c.ones[0:3, 0:ROWS],
                                         biases[0][:, bass.ds(e * GU, GU)], start=False, stop=True)
                    last.then_inc(gate_done.sem, 1)

                def turn_h(i, phase):
                    u = phase % 2
                    pe.wait_ge(hidden_done.sem, hidden_done.at(i + 1))
                    pe.transpose(HT[u][0:I, 0:ROWS], h[u][:, :], c.ident[0:ROWS, 0:ROWS]) \
                      .then_inc(h_turned.sem, 1)

                def down(i, phase):
                    u, e = phase % 2, expert_of(i)
                    pe.wait_ge(y_kept.sem, y_kept.at(i - 1))
                    pe.wait_ge(h_kept.sem, h_kept.at(i + 1))
                    last = pe.matmul(YB[u][0:ROWS, 0:D_MODEL], hT[u][:, :],
                                     w_dn[:, bass.ds(e * D_MODEL, D_MODEL)], start=True, stop=(biases is None))
                    if biases is not None:
                        last = pe.matmul(YB[u][0:ROWS, 0:D_MODEL], c.ones[0:3, 0:ROWS],
                                         biases[1][:, bass.ds(e * D_MODEL, D_MODEL)], start=False, stop=True)
                    last.then_inc(down_done.sem, 1)

                def step(i, phase):
                    if exists(i + 1):
                        turn_x(i + 1, phase + 1)
                    if exists(i - 2):
                        turn_h(i - 2, phase - 2)
                    if exists(i):
                        gate_up(i, phase)
                    if exists(i - 3):
                        down(i - 3, phase - 3)

                pe.wait_ge(*weights_in)
                turn_x(0, 0)
                steps(pe, step)

            @block.scalar
            def _(act):
                def keep_x(i, phase):
                    u = phase % 2
                    act.wait_ge(x_turned.sem, x_turned.at(i + 1))
                    act.activation(xT[u][:, :], XT[u][:, 0:KC * ROWS], ACT.Copy).then_inc(x_kept.sem, 1)

                def gate_act(i, phase):
                    u = phase % 2
                    if which == 0:
                        act.wait_ge(clipped.sem, clipped.at(i * 2 + 1))
                        act.activation(sg[u][:, :], g[u][:, :], ACT.Sigmoid, scale=1.702).then_inc(act_done.sem, 1)
                    else:
                        act.wait_ge(gate_done.sem, gate_done.at(i + 1))
                        act.activation(sg[u][:, :], GUB[u][0:ROWS, 0:I], ACT.Silu).then_inc(act_done.sem, 1)

                def keep_h(i, phase):
                    u = phase % 2
                    act.wait_ge(h_turned.sem, h_turned.at(i + 1))
                    act.activation(hT[u][:, :], HT[u][0:I, 0:ROWS], ACT.Copy).then_inc(h_kept.sem, 1)

                def step(i, phase):
                    if exists(i + 1):
                        keep_x(i + 1, phase + 1)
                    if exists(i - 2):
                        keep_h(i - 2, phase - 2)
                    if exists(i):
                        gate_act(i, phase)

                keep_x(0, 0)
                steps(act, step)

            @block.vector
            def _(dve):
                def clip(i, phase):
                    u = phase % 2
                    dve.wait_ge(gate_done.sem, gate_done.at(i + 1))
                    dve.tensor_scalar(g[u][:, :], GUB[u][0:ROWS, 0:I], 7.0, None, ALU.min) \
                       .then_inc(clipped.sem, 1)
                    dve.tensor_scalar(up[u][:, :], GUB[u][0:ROWS, I:GU], -7.0, 7.0, ALU.max, ALU.min) \
                       .then_inc(clipped.sem, 1)

                def hidden(i, phase):
                    u = phase % 2
                    if which == 0:
                        dve.wait_ge(clipped.sem, clipped.at(i * 2 + 2))
                        dve.wait_ge(act_done.sem, act_done.at(i + 1))
                        dve.tensor_tensor(g[u][:, :], g[u][:, :], sg[u][:, :], ALU.mult).then_inc(gated.sem, 1)
                        dve.wait_ge(gated.sem, gated.at(i + 1))
                        dve.scalar_tensor_tensor(out=h[u][:, :], in0=up[u][:, :], scalar=1.0, in1=g[u][:, :],
                                                 op0=ALU.add, op1=ALU.mult).then_inc(hidden_done.sem, 1)
                    else:
                        dve.wait_ge(act_done.sem, act_done.at(i + 1))
                        dve.tensor_tensor(h[u][:, :], sg[u][:, :], GUB[u][0:ROWS, I:GU], ALU.mult) \
                           .then_inc(hidden_done.sem, 1)

                def keep_y(i, phase):
                    u, r = phase % 2, phase % NR
                    dve.wait_ge(rows_out[r].sem, rows_out[r].at(i * (16 // NR) - r * (16 // NR)))
                    dve.wait_ge(down_done.sem, down_done.at(i + 1))
                    dve.tensor_copy(yo[r][:, :], YB[u][0:ROWS, 0:D_MODEL]).then_inc(y_kept.sem, 1)

                def step(i, phase):
                    if exists(i) and which == 0:
                        clip(i, phase)
                    if exists(i - 4):
                        keep_y(i - 4, phase)
                    if exists(i):
                        hidden(i, phase)

                steps(dve, step)
    for u in range(NR):
        rows_in[u].counted(16 * (NT // NR))
        rows_out[u].counted(16 * (NT // NR))
    for w in (x_turned, x_kept, gate_done, act_done, hidden_done, h_turned, h_kept, down_done, y_kept):
        w.counted(NT)
    if which == 0:
        clipped.counted(2 * NT)
        gated.counted(NT)


class Heads:

    def __init__(self, name, heads, dim, kv_heads, scale, causal, rot=0, interleaved=False, window=0):
        self.name, self.H, self.D, self.KH, self.scale, self.causal = name, heads, dim, kv_heads, scale, causal
        self.rot, self.interleaved, self.window = rot, interleaved, window
        self.HG = 4
        self.G = heads // self.HG
        self.latent = kv_heads == 1
        self.KT = min(4, kv_heads)


ROTARY = Heads("ra", 16, 16, 16, 0.25, True, rot=8, interleaved=True)
SINKS = Heads("sa", 32, 64, 8, 0.125, False, rot=16, window=64)
LATENT = Heads("la", 16, 128, 1, 1.0 / float(np.sqrt(128.0)), True)


def rotate(st, a, dst, src, n, tile, cos, sin, t1, t2):
    dve, R = st.eng, a.rot
    if a.interleaved:
        v = lambda x: x.rearrange("p (h r s) -> p h s r", h=n, s=2)
    else:
        v = lambda x: x.rearrange("p (h s r) -> p h s r", h=n, s=2)
    small = lambda x: x[:, 0:n * 2 * R].rearrange("p (h s r) -> p h s r", h=n, s=2)
    c_, s_ = (x[:, tile * R:(tile + 1) * R].rearrange("p (h r) -> p h r", h=1).to_broadcast([P, n, R])
              for x in (cos, sin))
    for half in range(2):
        dve.tensor_tensor(small(t1)[:, :, half, :], v(src)[:, :, half, 0:R], c_, ALU.mult)
        op = dve.tensor_tensor(small(t2)[:, :, half, :], v(src)[:, :, 1 - half, 0:R], s_, ALU.mult)
        if half == 0 and R * 2 < a.D:
            dve.tensor_copy(v(dst)[:, :, :, R:], v(src)[:, :, :, R:])
    st.then(op)
    for half in range(2):
        minus = (half == 0) == a.interleaved
        op = dve.tensor_tensor(v(dst)[:, :, half, 0:R], small(t1)[:, :, half, :], small(t2)[:, :, half, :],
                               ALU.subtract if minus else ALU.add)
    return op


def attention(c, a):
    nc, t = c.nc, c.t
    QW = a.HG * a.D
    KW = a.KH * a.D
    HD = a.H * a.D
    OC = HD // P
    UN = TPB * a.HG
    with ExitStack() as s:
        sb = lambda name, shape, dt=F32: s.enter_context(nc.sbuf_tensor(f"{a.name}_{name}", shape, dt))
        sig = {n: counter(c, "at_" + n) for n in (
            "loaded", "made", "xkept", "kvp", "kput", "vput", "kturned", "kkept", "qp", "qput", "qturned", "qkept",
            "scored", "maxed", "negged", "exped", "turned", "kept_d", "kept_a", "summed", "normed", "own_k",
            "own_q", "own_n", "own_o", "yturned", "ykept", "outp", "added")}
        at = lambda n, v: (sig[n].sem, sig[n].at(v))
        inc = lambda n: (sig[n].sem, 1)
        w_q, w_k = sb("w_q", [P, KC * HD]), sb("w_k", [P, KC * KW])
        w_v = None if a.latent else sb("w_v", [P, KC * KW])
        w_o = sb("w_o", [P, OC * D_MODEL])
        fold = lambda w, src: (w[:, :].rearrange("p (k n) -> p k n", k=KC), src.rearrange("(k p) n -> p k n", p=P))
        LOADS = [fold(w_q, t[a.name + "_wq"]), fold(w_k, t[a.name + "_wk"]),
                 (w_o[:, :].rearrange("p (k n) -> p k n", k=OC), t[a.name + "_wo"].rearrange("(k p) n -> p k n", p=P))]
        if not a.latent:
            LOADS.append(fold(w_v, t[a.name + "_wv"]))
        if a.rot:
            cos, sin = sb("cos", [P, TPB * a.rot]), sb("sin", [P, TPB * a.rot])
            for x, n in ((cos, "_cos"), (sin, "_sin")):
                LOADS.append((x[:, :].rearrange("p (t r) -> p t r", t=TPB),
                              t[a.name + n].rearrange("(t p) r -> p t r", p=P)))
        if a.latent:
            b_q, b_k, b_o = sb("b_q", [P, HD]), sb("b_k", [P, KW]), sb("b_o", [P, D_MODEL])
            LOADS += [(b_q[:, :], t["la_bq"].to_broadcast([P, HD])), (b_k[:, :], t["la_bk"].to_broadcast([P, KW])),
                      (b_o[:, :], t["la_bo"].to_broadcast([P, D_MODEL]))]
        if a.window:
            sink = sb("sink", [P, a.H])
            negsink = sb("negsink", [P, a.H])
            LOADS.append((sink[:, :], t["sinks"].to_broadcast([P, a.H])))

        def loads(sp):
            for dst, src in LOADS:
                sp.dma_start(dst, src).then_inc(sig["loaded"].sem, 16)

        xnT = sb("xnT", [P, KC * TOKENS + SEQ])
        layer_norm(c, xnT, loads=loads)

        MW = 2 * P if a.window else P
        mask, identb = sb("mask", [P, MW], BF16), sb("identb", [P, P], BF16)
        xb = sb("xb", [P, KC * SEQ])
        kst = sb("kst", [P, KW])
        kT = sb("kT", [a.D, a.KH * SEQ])
        VW = KW + P - a.D
        vv = sb("v", [P, TPB * VW])
        qst = sb("qst", [P, QW])
        qT = [sb(f"qT{u}", [a.D, a.HG * P]) for u in range(2)]
        pr = [sb(f"p{u}", [P, SEQ]) for u in range(4)]
        pT = [sb(f"pT{u}", [P, SEQ]) for u in range(2)]
        mx, nm, rs = (sb(n, [P, 2 * a.HG]) for n in ("mx", "nm", "rs"))
        es, rinv = (sb(n, [P, 2 * a.HG]) for n in ("es", "rinv"))
        yb = sb("y", [P, TPB * HD])
        yT = [sb(f"yT{u}", [P, min(4, OC) * P]) for u in range(2)]
        t1, t2 = (sb(n, [P, max(a.KH, a.HG) * 2 * a.rot]) if a.rot else None for n in ("t1", "t2"))
        SC, PT, OB, QB, TQ = c.banks[0:2], c.banks[2:4], c.banks[4:6], c.banks[6], c.banks[7]
        keys = lambda qt: (qt + 1) * P if a.causal else SEQ
        KG = a.KH // a.KT
        ROUNDS = -(-OC // 4)
        RW = min(4, OC)
        CONSTS = 6 + (VW > KW) + 1

        def groups(eng, steps):
            steps(0, True, False)
            with eng.Fori(0, a.G - 2) as j:
                steps(j + 1, False, False)
            steps(a.G - 1, False, True)

        def kept(u):
            return "kept_d" if u % 2 == 0 else "kept_a"

        with nc.Block() as block:

            @block.gpsimd
            def _(pool):
                pool.memset(mask[:, :], 0.0).then_inc(*inc("made"))
                pool.memset(identb[:, :], 0.0).then_inc(*inc("made"))
                pool.wait_ge(*at("made", 2))
                pool.affine_select(out=identb[:, :], in_=identb[:, :], compare_op=ALU.not_equal, fill=1.0,
                                   base=0, pattern=[[-1, P]], channel_multiplier=1).then_inc(*inc("made"))
                if a.window:
                    pool.memset(mask[:, :], NEG).then_inc(*inc("made"))
                    pool.wait_ge(*at("made", 4))
                    pool.affine_select(out=mask[:, :], in_=mask[:, :], compare_op=ALU.is_ge, fill=0.0,
                                       base=P, pattern=[[-1, MW]], channel_multiplier=1).then_inc(*inc("made"))
                    pool.wait_ge(*at("made", 5))
                    pool.affine_select(out=mask[:, :], in_=mask[:, :], compare_op=ALU.is_gt, fill=0.0,
                                       base=a.window - P, pattern=[[1, MW]], channel_multiplier=-1) \
                        .then_inc(*inc("made"))
                else:
                    pool.affine_select(out=mask[:, :], in_=mask[:, :], compare_op=ALU.is_ge, fill=NEG,
                                       base=0, pattern=[[-1, P]], channel_multiplier=1).then_inc(sig["made"].sem, 3)
                if VW > KW:
                    pool.memset(vv[:, :].rearrange("p (t n) -> p t n", t=TPB)[:, :, KW:], 0.0) \
                        .then_inc(*inc("made"))
                pool.memset(xnT[:, KC * TOKENS:], 0.0).then_inc(*inc("made"))

            @block.tensor
            def _(pe):
                pe.wait_ge(*at("made", CONSTS))
                pe.wait_ge(*at("loaded", 16 * len(LOADS)))

                def carry_wait(bank):
                    if a.D == 64:
                        pe.matmul(bank[:, 0:1], c.zeros[:, 0:P], c.zeros[:, 0:1], start=True, stop=True)

                with pe.Fori(0, BATCH) as b:

                    def keys_values(i):
                        n = b * TPB + i
                        if i >= 2:
                            pe.wait_ge(*at("kput", n - 1))
                            if not a.latent:
                                pe.wait_ge(*at("vput", n - 1))
                        for w, bank in ((w_k, SC[i % 2]),) + (() if a.latent else ((w_v, OB[i % 2]),)):
                            for k in range(KC):
                                last = pe.matmul(bank[:, 0:KW], xb[:, k * SEQ + i * P:k * SEQ + (i + 1) * P],
                                                 w[:, k * KW:(k + 1) * KW], start=(k == 0), stop=(k == KC - 1))
                        last.then_inc(*inc("kvp"))

                    def turn_keys(i):
                        n = b * TPB + i
                        pe.wait_ge(*at("kput", n + 1))
                        for m in range(KG):
                            pe.wait_ge(*at("kkept", n * KG + max(m - 1, 0)))
                            carry_wait(PT[m % 2])
                            for hh in range(a.KT):
                                h = m * a.KT + hh
                                src = vv[:, i * VW:i * VW + KW] if a.latent else kst[:, h * a.D:(h + 1) * a.D]
                                last = pe.transpose(PT[m % 2][0:a.D, hh * P:(hh + 1) * P], src, c.ident[:, :])
                            last.then_inc(*inc("kturned"))

                    def project(t, g, qt):
                        pe.wait_ge(*at("qput", t))
                        for k in range(KC):
                            last = pe.matmul(QB[:, 0:QW], xb[:, k * SEQ + qt * P:k * SEQ + (qt + 1) * P],
                                             w_q[:, bass.ds(g * QW + k * HD, QW)],
                                             start=(k == 0), stop=(k == KC - 1))
                        last.then_inc(*inc("qp"))

                    def turn_q(t):
                        pe.wait_ge(*at("qput", t + 1))
                        pe.wait_ge(*at("qkept", t))
                        carry_wait(TQ)
                        for hh in range(a.HG):
                            last = pe.transpose(TQ[0:a.D, hh * P:(hh + 1) * P], qst[:, hh * a.D:(hh + 1) * a.D],
                                                c.ident[:, :])
                        last.then_inc(*inc("qturned"))

                    def score(g, u):
                        qt, hh = divmod(u, a.HG)
                        bank = SC[u % 2]
                        if a.latent:
                            key = kT[:, 0:keys(qt)]
                        else:
                            key = kT[:, bass.ds(g * (SEQ * (a.HG if a.KH == a.H else 1))
                                                + (hh * SEQ if a.KH == a.H else 0), keys(qt))]
                        pe.matmul(bank[:, 0:keys(qt)], qT[qt % 2][:, hh * P:(hh + 1) * P], key,
                                  start=True, stop=False)
                        lo = max(qt * P - (MW - P), 0)
                        hi = (qt + 1) * P
                        pe.matmul(bank[:, lo:hi], identb[:, :], mask[:, MW - (hi - lo):MW],
                                  start=False, stop=True).then_inc(*inc("scored"))

                    def turn_p(I, u, before, earliest):
                        qt, n = u // a.HG, I * UN + (u - before)
                        pe.wait_ge(*at("exped", n + 1))
                        if not earliest:
                            pe.wait_ge(*at(kept(u), I * (UN // 2) + (u - before) // 2))
                        for kb in range(keys(qt) // P):
                            last = pe.transpose(PT[u % 2][:, kb * P:(kb + 1) * P],
                                                pr[u % 4][:, kb * P:(kb + 1) * P], c.ident[:, :])
                        last.then_inc(*inc("turned"))

                    def values(I, g, u, before, earliest):
                        qt, hh = divmod(u, a.HG)
                        pe.wait_ge(*at(kept(u), I * (UN // 2) + ((u - before) // 2 + 1)))
                        if hh == 0 and not earliest:
                            pe.wait_ge(*at("normed", I * TPB + ((u - before) // a.HG - 1)))
                        nb = keys(qt) // P
                        for kb in range(nb):
                            if a.latent:
                                v = vv[:, kb * VW:kb * VW + P]
                            elif a.KH == a.H:
                                v = vv[:, bass.ds(g * (a.HG * a.D) + (kb * VW + hh * a.D
                                                                      - before // UN * a.HG * a.D), P)]
                            else:
                                v = vv[:, bass.ds(g * a.D + (kb * VW - before // UN * a.D), P)]
                            last = pe.matmul(OB[qt % 2][:, hh * P:(hh + 1) * P],
                                             pT[u % 2][:, kb * P:(kb + 1) * P], v,
                                             start=(kb == 0), stop=(kb == nb - 1))
                        last.then_inc(*inc("summed"))

                    def steps(g, first, last):
                        I = b * a.G + g
                        t0 = I * TPB
                        for u in range(UN):
                            qt = u // a.HG + 1
                            if qt < TPB or not last:
                                ahead = (g, qt) if qt < TPB else (g + 1, 0)
                                if u % a.HG == 0:
                                    project(t0 + qt, *ahead)
                                if u % a.HG == 2:
                                    turn_q(t0 + qt)
                            if u >= 2:
                                turn_p(I, u - 2, 0, first and u < 4)
                            elif not first:
                                turn_p(I, u - 2 + UN, UN, False)
                            score(g, u)
                            if u >= 3:
                                values(I, g, u - 3, 0, first and u < 3 + 2 * a.HG)
                            elif not first:
                                values(I, g, u - 3 + UN, UN, False)
                        if last:
                            turn_p(I, UN - 2, 0, False)
                            values(I, g, UN - 3, 0, False)
                            turn_p(I, UN - 1, 0, False)
                            values(I, g, UN - 2, 0, False)
                            values(I, g, UN - 1, 0, False)

                    pe.wait_ge(*at("xkept", b + 1))
                    for i in range(TPB):
                        keys_values(i)
                        if i >= 1:
                            turn_keys(i - 1)
                        if i == 1:
                            pe.wait_ge(*at("added", b * TPB))
                            project(b * (a.G * TPB), 0, 0)
                    turn_keys(TPB - 1)
                    turn_q(b * (a.G * TPB))
                    pe.wait_ge(*at("kkept", (b + 1) * (TPB * KG)))
                    pe.wait_ge(*at("vput", 0 if a.latent else (b + 1) * TPB))
                    pe.wait_ge(*at("qkept", b * (a.G * TPB) + 1))
                    groups(pe, steps)

                    OUT = (QB, TQ)

                    def turn_y(r):
                        qt, m = divmod(r, ROUNDS)
                        if m == 0:
                            pe.wait_ge(*at("normed", (b + 1) * (a.G * TPB) - (TPB - 1 - qt)))
                        if r >= 2:
                            pe.wait_ge(*at("ykept", b * (TPB * ROUNDS) + (r - 1)))
                        for k in range(RW):
                            ch = qt * HD + (m * RW + k) * P
                            last = pe.transpose(PT[r % 2][:, k * P:(k + 1) * P], yb[:, ch:ch + P], c.ident[:, :])
                        last.then_inc(*inc("yturned"))

                    def product(r):
                        qt, m = divmod(r, ROUNDS)
                        pe.wait_ge(*at("ykept", b * (TPB * ROUNDS) + (r + 1)))
                        if m == 0 and qt >= 2:
                            pe.wait_ge(*at("added", b * TPB + (qt - 1)))
                        for k in range(RW):
                            last = pe.matmul(OUT[qt % 2][:, 0:D_MODEL], yT[r % 2][:, k * P:(k + 1) * P],
                                             w_o[:, (m * RW + k) * D_MODEL:(m * RW + k + 1) * D_MODEL],
                                             start=(m == 0 and k == 0), stop=(m == ROUNDS - 1 and k == RW - 1))
                        if m == ROUNDS - 1:
                            last.then_inc(*inc("outp"))

                    for r in range(TPB * ROUNDS):
                        turn_y(r)
                        if r:
                            product(r - 1)
                    product(TPB * ROUNDS - 1)

            @block.scalar
            def _(act):
                def keep_x(b):
                    for k in range(KC):
                        last = act.activation(xb[:, k * SEQ:(k + 1) * SEQ],
                                              xnT[:, bass.ds(b * SEQ + k * TOKENS, SEQ)], ACT.Copy)
                    last.then_inc(*inc("xkept"))

                act.wait_ge(*at("made", CONSTS))
                keep_x(0)
                with act.Fori(0, BATCH) as b:

                    def keep_keys(i):
                        n = b * TPB + i
                        for m in range(KG):
                            act.wait_ge(*at("kturned", n * KG + m + 1))
                            act.activation(kT[:, :].rearrange("p (h n) -> p h n", h=a.KH)
                                           [:, m * a.KT:(m + 1) * a.KT, i * P:(i + 1) * P],
                                           PT[m % 2][0:a.D, 0:a.KT * P].rearrange("p (h n) -> p h n", h=a.KT),
                                           ACT.Copy).then_inc(*inc("kkept"))

                    def keep_q(t, qt):
                        act.wait_ge(*at("qturned", t + 1))
                        act.activation(qT[qt % 2][:, :], TQ[0:a.D, :], ACT.Copy).then_inc(*inc("qkept"))

                    def expo(I, u, earliest):
                        qt, hh = divmod(u, a.HG)
                        col, n = (qt % 2) * a.HG + hh, I * UN + u
                        act.wait_ge(*at("negged", n + 1))
                        if not earliest:
                            act.wait_ge(*at("turned", I * UN + (u - 3)))
                        act.activation(pr[u % 4][:, 0:keys(qt)], SC[u % 2][:, 0:keys(qt)], ACT.Exp,
                                       bias=nm[:, col:col + 1], scale=a.scale,
                                       accum_out=rs[:, col:col + 1]).then_inc(*inc("exped"))

                    def keep_p(I, u, before):
                        if kept(u) != "kept_a":
                            return
                        w = keys(u // a.HG)
                        act.wait_ge(*at("turned", I * UN + (u - before + 1)))
                        act.wait_ge(*at("summed", I * UN + (u - before - 1)))
                        act.activation(pT[u % 2][:, 0:w], PT[u % 2][:, 0:w], ACT.Copy).then_inc(*inc("kept_a"))

                    def steps(g, first, last):
                        I = b * a.G + g
                        for u in range(UN):
                            qt = u // a.HG + 1
                            if u % a.HG == 2 and (qt < TPB or not last):
                                act.wait_ge(*at("scored", I * UN + (qt - 1) * a.HG))
                                keep_q(I * TPB + qt, qt)
                            if u >= 2:
                                keep_p(I, u - 2, 0)
                            elif not first:
                                keep_p(I, u - 2 + UN, UN)
                            expo(I, u, first and u < 4)
                            if a.window and u % a.HG == a.HG - 1:
                                cut = slice((qt - 1) % 2 * a.HG, ((qt - 1) % 2 + 1) * a.HG)
                                act.wait_ge(*at("own_n", (I * TPB + (qt - 1)) * 3 + 1))
                                act.activation(es[:, cut], es[:, cut], ACT.Exp).then_inc(*inc("maxed"))
                        if last:
                            keep_p(I, UN - 2, 0)
                            keep_p(I, UN - 1, 0)

                    for i in range(TPB):
                        if not a.latent:
                            act.wait_ge(*at("kvp", b * TPB + i + 1))
                            act.activation(vv[:, i * VW:i * VW + KW], OB[i % 2][:, 0:KW],
                                           ACT.Copy).then_inc(*inc("vput"))
                        if i >= 1:
                            keep_keys(i - 1)
                    keep_keys(TPB - 1)
                    keep_q(b * (a.G * TPB), 0)
                    groups(act, steps)
                    act.wait_ge(*at("qp", (b + 1) * (a.G * TPB)))
                    keep_x(b + 1)
                    for r in range(TPB * ROUNDS):
                        act.wait_ge(*at("yturned", b * (TPB * ROUNDS) + (r + 1)))
                        act.activation(yT[r % 2][:, :], PT[r % 2][:, 0:RW * P], ACT.Copy).then_inc(*inc("ykept"))

            @block.vector
            def _(dve):
                dve.wait_ge(*at("loaded", 16 * len(LOADS)))
                if a.window:
                    dve.tensor_scalar(negsink[:, :], sink[:, :], -1.0, None, ALU.mult).then_inc(*inc("own_o"))
                    dve.wait_ge(*at("own_o", 1))
                with dve.Fori(0, BATCH) as b:

                    def put_keys(i):
                        n = b * TPB + i
                        dve.wait_ge(*at("kvp", n + 1))
                        if a.latent:
                            dve.tensor_tensor(vv[:, i * VW:i * VW + KW], SC[i % 2][:, 0:KW], b_k[:, :], ALU.add) \
                               .then_inc(*inc("kput"))
                        else:
                            dve.wait_ge(*at("kturned", n * KG))
                            st = Steps(dve, sig["own_k"])
                            st.loop = n
                            rotate(st, a, kst[:, :], SC[i % 2][:, 0:KW], a.KH, i, cos, sin, t1, t2) \
                                .then_inc(*inc("kput"))

                    def put_q(t, g, qt):
                        dve.wait_ge(*at("qp", t + 1))
                        dve.wait_ge(*at("qturned", t))
                        if a.latent:
                            dve.tensor_tensor(qst[:, :], QB[:, :], b_q[:, bass.ds(g * QW, QW)], ALU.add) \
                               .then_inc(*inc("qput"))
                        else:
                            st = Steps(dve, sig["own_q"])
                            st.loop = t
                            rotate(st, a, qst[:, :], QB[:, 0:QW], a.HG, qt, cos, sin, t1, t2) \
                                .then_inc(*inc("qput"))

                    def maximum(I, g, u):
                        qt, hh = divmod(u, a.HG)
                        col = (qt % 2) * a.HG + hh
                        dve.wait_ge(*at("scored", I * UN + (u + 1)))
                        dve.reduce_max(mx[:, col:col + 1], SC[u % 2][:, 0:keys(qt)], AX) \
                           .then_inc(*inc("own_o"))
                        dve.wait_ge(*at("own_o", I * UN + (u + 1 + bool(a.window))))
                        if a.window:
                            dve.scalar_tensor_tensor(out=nm[:, col:col + 1], in0=mx[:, col:col + 1],
                                                     scalar=-a.scale, in1=negsink[:, bass.ds(g * a.HG + hh, 1)],
                                                     op0=ALU.mult, op1=ALU.min).then_inc(*inc("negged"))
                        else:
                            dve.tensor_scalar(nm[:, col:col + 1], mx[:, col:col + 1], -a.scale, None,
                                              ALU.mult).then_inc(*inc("negged"))

                    def keep_p(I, u, before, earliest):
                        if kept(u) != "kept_d":
                            return
                        w = keys(u // a.HG)
                        dve.wait_ge(*at("turned", I * UN + (u - before + 1)))
                        if not earliest:
                            dve.wait_ge(*at("summed", I * UN + (u - before - 1)))
                        dve.tensor_copy(pT[u % 2][:, 0:w], PT[u % 2][:, 0:w]).then_inc(*inc("kept_d"))

                    def sink_minus_max(I, g, qt):
                        cut = slice((qt % 2) * a.HG, (qt % 2 + 1) * a.HG)
                        dve.wait_ge(*at("negged", I * UN + (qt + 1) * a.HG))
                        dve.tensor_tensor(es[:, cut], nm[:, cut], sink[:, bass.ds(g * a.HG, a.HG)],
                                          ALU.add).then_inc(*inc("own_n"))

                    def normalize(I, g, qt, before):
                        cut = slice((qt % 2) * a.HG, (qt % 2 + 1) * a.HG)
                        t = I * TPB + (qt - before * TPB)
                        dve.wait_ge(*at("summed", I * UN + ((qt + 1) * a.HG - before * UN)))
                        if a.window:
                            dve.wait_ge(*at("maxed", t + 1))
                            dve.tensor_tensor(rs[:, cut], rs[:, cut], es[:, cut], ALU.add) \
                               .then_inc(*inc("own_n"))
                            dve.wait_ge(*at("own_n", t * 3 + 2))
                            dve.reciprocal(rinv[:, cut], rs[:, cut]).then_inc(*inc("own_n"))
                            dve.wait_ge(*at("own_n", t * 3 + 3))
                        else:
                            dve.reciprocal(rinv[:, cut], rs[:, cut]).then_inc(*inc("own_n"))
                            dve.wait_ge(*at("own_n", t + 1))
                        dve.tensor_tensor(
                            yb[:, bass.ds(g * QW + (qt * HD - before * QW), QW)]
                            .rearrange("p (h d) -> p h d", h=a.HG),
                            OB[qt % 2][:, :].rearrange("p (h d) -> p h d", h=a.HG)[:, :, 0:a.D],
                            rinv[:, cut].rearrange("p (h o) -> p h o", o=1).to_broadcast([P, a.HG, a.D]),
                            ALU.mult).then_inc(*inc("normed"))

                    def steps(g, first, last):
                        I = b * a.G + g
                        for u in range(UN):
                            qt = u // a.HG + 1
                            maximum(I, g, u)
                            if a.window and u % a.HG == a.HG - 1:
                                sink_minus_max(I, g, qt - 1)
                            if u % a.HG == 0 and (qt < TPB or not last):
                                ahead = (g, qt) if qt < TPB else (g + 1, 0)
                                put_q(I * TPB + qt, *ahead)
                            if u >= 2:
                                keep_p(I, u - 2, 0, first and u == 2)
                            elif not first:
                                keep_p(I, u - 2 + UN, UN, False)
                            if u % a.HG == 2:
                                if u >= 3:
                                    normalize(I, g, qt - 2, 0)
                                elif not first:
                                    normalize(I, g, TPB - 1, 1)
                        if last:
                            keep_p(I, UN - 2, 0, False)
                            normalize(I, g, TPB - 1, 0)

                    for i in range(TPB):
                        put_keys(i)
                        if i == 1:
                            dve.wait_ge(*at("kput", b * TPB + 2))
                            put_q(b * (a.G * TPB), 0, 0)
                            dve.wait_ge(*at("qput", b * (a.G * TPB) + 1))
                    groups(dve, steps)
                    for qt in range(TPB):
                        n = b * TPB + qt
                        at_x = c.x[:, bass.ds(b * (TPB * D_MODEL) + qt * D_MODEL, D_MODEL)]
                        if a.latent:
                            dve.tensor_tensor(at_x, at_x, b_o[:, :], ALU.add).then_inc(*inc("own_k"))
                            dve.wait_ge(*at("own_k", n + 1))
                        dve.wait_ge(*at("outp", n + 1))
                        dve.tensor_tensor(at_x, at_x, (QB, TQ)[qt % 2][:, 0:D_MODEL], ALU.add) \
                           .then_inc(*inc("added"))
        NI = BATCH * a.G
        for n, v in dict(
                loaded=16 * len(LOADS), made=CONSTS, xkept=BATCH + 1, kvp=TILES, kput=TILES, vput=0 if a.latent else TILES,
                kturned=TILES * KG, kkept=TILES * KG, qp=NI * TPB, qput=NI * TPB, qturned=NI * TPB, qkept=NI * TPB,
                scored=NI * UN, negged=NI * UN, exped=NI * UN, turned=NI * UN, kept_d=NI * UN // 2,
                kept_a=NI * UN // 2, summed=NI * UN, normed=NI * TPB, maxed=NI * TPB if a.window else 0,
                own_k=TILES, own_q=0 if a.latent else NI * TPB,
                own_n=NI * TPB * (3 if a.window else 1), own_o=NI * UN + bool(a.window),
                yturned=TILES * ROUNDS, ykept=TILES * ROUNDS, outp=TILES, added=TILES).items():
            sig[n].counted(v)


LAYERS = ["mamba", "moe0", "rotary", "moe0", "sinks", "moe1", "latent", "moe1"]
STAGES = {"mamba": mamba, "moe0": lambda c: moe(c, 0), "moe1": lambda c: moe(c, 1),
          "rotary": lambda c: attention(c, ROTARY), "sinks": lambda c: attention(c, SINKS),
          "latent": lambda c: attention(c, LATENT)}


def build_program(nc, t, layers=LAYERS):
    with ExitStack() as ctx:
        c = setup(nc, ctx, t)
        load_residual(c)
        for name in layers:
            STAGES[name](c)
        store_residual(c)


def host_layout(inputs):
    f = lambda name: np.asarray(inputs[name])
    cols = lambda a: np.ascontiguousarray(a.reshape(-1, P).T)
    gu0 = np.concatenate([f("L0_ffn_w_gate"), f("L0_ffn_w_up")], axis=2)
    gu1 = f("L1_ffn_gate_up_proj").transpose(0, 2, 1)
    pack = lambda w: w.reshape(w.shape[0], KC, P, w.shape[2]).transpose(2, 0, 1, 3).reshape(P, -1)
    rq, rk, rv = np.split(f("L0_attn_b_w_atten").T, 3, axis=1)
    sq, sk, sv = np.split(f("L1_attn_a_W_qkv"), (SINKS.H * SINKS.D, (SINKS.H + SINKS.KH) * SINKS.D), axis=1)
    position = np.arange(SEQ, dtype=np.float32)
    theta_r = np.outer(position, 1.0 / np.float32(10000.0) ** (np.arange(0, 16, 2, dtype=np.float32) / 16))
    theta_s = np.outer(position, np.float32(1.0 / 1024.0) ** np.linspace(0.0, 1.0, 16, dtype=np.float32))
    return {
        "ra_wq": rq, "ra_wk": rk, "ra_wv": rv, "ra_wo": f("L0_attn_b_w_proj").T,
        "ra_cos": np.cos(theta_r).astype(np.float32), "ra_sin": np.sin(theta_r).astype(np.float32),
        "sa_wq": sq, "sa_wk": sk, "sa_wv": sv, "sa_wo": f("L1_attn_a_W_out"),
        "sa_cos": np.cos(theta_s).astype(np.float32), "sa_sin": np.sin(theta_s).astype(np.float32),
        "sinks": f("L1_attn_a_s").reshape(1, -1),
        "la_wq": f("L1_attn_b_W_d"), "la_wk": f("L1_attn_b_W_lat"), "la_wo": f("L1_attn_b_W_proj"),
        "la_bq": f("L1_attn_b_b_d")[None, :], "la_bk": f("L1_attn_b_b_lat")[None, :],
        "la_bo": f("L1_attn_b_b_proj")[None, :],
        "w_gu0": pack(gu0), "w_gu1": pack(gu1),
        "w_dn0": f("L0_ffn_w_down").transpose(1, 0, 2).reshape(M0_I, -1),
        "w_dn1": f("L1_ffn_down_proj").transpose(2, 0, 1).reshape(M1_I, -1),
        "gate0T": f("L0_ffn_gate_w").T, "gate_b": f("L0_ffn_gate_b")[None, :],
        "b_all": np.concatenate([f("L0_ffn_b_gate"), f("L0_ffn_b_up"), f("L0_ffn_b_down")], axis=1),
        "gate1": f("L1_ffn_gate_weight"), "o2n": f("L1_ffn_old_to_new")[:, None],
        "x": f("L0_attn_a_hidden_states"),
        "in_wT": f("L0_attn_a_in_proj_w").T, "conv_w": f("L0_attn_a_conv_w"),
        "conv_b": cols(f("L0_attn_a_conv_b")), "D": cols(f("L0_attn_a_D")), "dt_b": cols(f("L0_attn_a_dt_proj_b")),
        "A_log": f("L0_attn_a_A_log"), "x_wT": f("L0_attn_a_x_proj_w").T,
        "dt_wT": f("L0_attn_a_dt_proj_w").T, "out_wT": f("L0_attn_a_out_proj_w").T,
    }


SCRATCH = {"scratch_bc": (2 * D_STATE, TOKENS)}
for _which, _rows in ((0, M0_TILES * P), (1, M1_E * M1_CAP)):
    SCRATCH[f"scratch_xs{_which}"] = SCRATCH[f"scratch_ys{_which}"] = (_rows, D_MODEL)


def make(nc, arrays, layers=LAYERS):
    t = {n: nc.dram_tensor(f"in_{n}", a.shape, mybir.dt.from_np(a.dtype), kind="ExternalInput").ap()
         for n, a in arrays.items()}
    for n, shape in SCRATCH.items():
        t[n] = nc.dram_tensor(n, shape, F32, kind="Internal").ap()
    t["out"] = nc.dram_tensor("out", (BATCH, SEQ, D_MODEL), F32, kind="ExternalOutput").ap()
    build_program(nc, t, layers)


def kernel(**inputs):
    import concourse.bacc as bacc
    from concourse.bass_utils import run_bass_kernel_spmd

    nc = bacc.Bacc("TRN2", target_bir_lowering=False, num_devices=1)
    arrays = {n: np.ascontiguousarray(a) for n, a in host_layout(inputs).items()}
    make(nc, arrays)
    got = run_bass_kernel_spmd(nc, [{f"in_{n}": a for n, a in arrays.items()}], core_ids=[0])
    return got.results[0]["out"]
```

```python
from contextlib import ExitStack

import numpy as np

import concourse.bass as bass
from concourse import mybir
from concourse.alu_op_type import AluOpType as ALU

F32 = mybir.dt.float32
F32R = mybir.dt.float32r
BF16 = mybir.dt.bfloat16
I32 = mybir.dt.int32
U32 = mybir.dt.uint32
ACT = mybir.ActivationFunctionType
AX = mybir.AxisListType.X

P = 128
BATCH, SEQ, D_MODEL = 4, 512, 256
TOKENS = BATCH * SEQ
TILES = TOKENS // P
TPB = SEQ // P
KC = D_MODEL // P
LN_EPS = 1e-5
NEG = -1.0e30

D_INNER, D_STATE, D_CONV, DT_RANK = 512, 16, 4, 16
BLK = D_INNER // P
HALF = TOKENS // 2

M0_E, M0_K, M0_I = 32, 4, 128
M0_TILES = TOKENS * M0_K // P + M0_E
M1_E, M1_K, M1_I, M1_CAP, M1_OLD = 48, 8, 96, 96, 128
FAR = 1.0e6


class Counter:

    def __init__(self, ctx, nc, name, base=0):
        self.sem = ctx.enter_context(nc.semaphore(name))
        self.base = base

    def at(self, n):
        return self.base + n

    def counted(self, n):
        self.base += n


FROM_ONE = ("mb_fetched", "mb_gated", "mb_conved", "mb_acted", "sc_scanned", "sc_out",
            "ex_rows_out0", "ex_rows_out1", "ex_rows_out2", "ex_rows_out3", "ex_y_kept") + tuple(
                "at_" + n for n in (
                "kput", "qraw", "vput", "kturned", "kkept", "qput", "qturned", "qkept", "scored", "exped", "turned",
                "kept_d", "kept_a", "summed", "normed", "ykept", "outp", "added", "klow", "qlow"))


class Steps:

    def __init__(self, eng, counter):
        self.eng, self.counter, self.n, self.loop = eng, counter, 0, 0

    def then(self, instruction):
        self.n += 1
        instruction.then_inc(self.counter.sem, 1)
        self.eng.wait_ge(self.counter.sem, self.counter.at(self.loop + self.n))


class Core:
    pass


def setup(nc, ctx, t):
    c = Core()
    c.nc, c.t, c.ctx = nc, t, ctx
    c.counters = {n: Counter(ctx, nc, n, 1) for n in FROM_ONE}
    c.x = ctx.enter_context(nc.sbuf_tensor("residual", [P, TILES * D_MODEL], F32))
    c.ident = ctx.enter_context(nc.sbuf_tensor("ident", [P, P], F32))
    c.banks = [ctx.enter_context(nc.psum_tensor(f"bank{i}", [P, 512], F32)) for i in range(8)]
    c.zeros = ctx.enter_context(nc.sbuf_tensor("zeros", [P, 512], BF16))
    c.ones = ctx.enter_context(nc.sbuf_tensor("ones", [P, P], BF16))
    return c


def counter(c, name):
    if name not in c.counters:
        c.counters[name] = Counter(c.ctx, c.nc, name)
    return c.counters[name]


def load_residual(c):
    nc = c.nc
    loaded, made = counter(c, "x_loaded"), counter(c, "const_made")
    with nc.Block() as block:

        @block.sync
        def _(sp):
            sp.dma_start(c.x[:, :].rearrange("p (t d) -> p t d", d=D_MODEL),
                         c.t["x"].rearrange("b (t p) d -> p (b t) d", p=P)).then_inc(loaded.sem, 16)
            sp.wait_ge(loaded.sem, 16)

        @block.vector
        def _(dve):
            for name in FROM_ONE:
                dve.sem_inc(c.counters[name].sem, 1)

        @block.gpsimd
        def _(pool):
            pool.memset(c.ident[:, :], 0.0).then_inc(made.sem, 1)
            pool.memset(c.zeros[:, :], 0.0)
            pool.memset(c.ones[:, :], 1.0)
            pool.wait_ge(made.sem, 1)
            pool.affine_select(out=c.ident[:, :], in_=c.ident[:, :], compare_op=ALU.not_equal, fill=1.0,
                               base=0, pattern=[[-1, P]], channel_multiplier=1)
    loaded.counted(16)
    made.counted(1)
    c.filled, c.fills = counter(c, "filled"), 0


def zero_scratch(c, sp):
    blank = c.zeros[:, :].bitcast(F32)
    for name in ("scratch_xs0", "scratch_xs1"):
        rows = c.t[name].shape[0]
        sp.dma_start(c.t[name].rearrange("(p n) d -> p n d", p=P),
                     blank.rearrange("p (n d) -> p n d", n=1).to_broadcast([P, rows // P, D_MODEL])) \
          .then_inc(c.filled.sem, 16)
        c.fills += 1


def store_residual(c):
    nc = c.nc
    stored = counter(c, "x_stored")
    with nc.Block() as block:

        @block.sync
        def _(sp):
            sp.dma_start(c.t["out"].rearrange("b (t p) d -> p (b t) d", p=P),
                         c.x[:, :].rearrange("p (t d) -> p t d", d=D_MODEL)).then_inc(stored.sem, 16)
            sp.wait_ge(stored.sem, 16)


def layer_norm(c, xnT, xn=None, loads=None, products=None, last_step=None):
    nc = c.nc
    own, root, stat = counter(c, "ln_own"), counter(c, "ln_root"), counter(c, "ln_stat")
    normed, turned, kept = counter(c, "ln_normed"), counter(c, "ln_turned"), counter(c, "ln_kept")
    with ExitStack() as s:
        sb = lambda name, shape: s.enter_context(nc.sbuf_tensor(name, shape, F32, allow_name_mangling=True))
        bn = sb("ln_bn", [P, TILES * 6])
        mean, var, tmp, rstd = (sb(n, [P, TILES]) for n in ("ln_mean", "ln_var", "ln_tmp", "ln_rstd"))
        stage = sb("ln_stage", [P, 2 * D_MODEL]) if xn is None else None
        bnv = bn[:, :].rearrange("p (t s) -> p t s", s=6)

        def normal(tile, u):
            if xn is None:
                return stage[:, u * D_MODEL:(u + 1) * D_MODEL]
            return xn[:, tile * D_MODEL:(tile + 1) * D_MODEL]

        with nc.Block() as block:
            if loads is not None:
                @block.sync
                def _(sp):
                    loads(sp)
                    if not c.fills:
                        zero_scratch(c, sp)

            @block.vector
            def _(dve):
                st = Steps(dve, own)
                with dve.Fori(0, TILES) as i:
                    dve.bn_stats(bn[:, bass.ds(i * 6, 6)], c.x[:, bass.ds(i * D_MODEL, D_MODEL)]) \
                       .then_inc(stat.sem, 1)
                dve.wait_ge(stat.sem, stat.at(TILES))
                st.then(dve.tensor_tensor(mean[:, :], bnv[:, :, 1], bnv[:, :, 4], ALU.add))
                st.then(dve.tensor_tensor(tmp[:, :], bnv[:, :, 1], bnv[:, :, 4], ALU.subtract))
                st.then(dve.tensor_tensor(var[:, :], bnv[:, :, 2], bnv[:, :, 5], ALU.add))
                st.then(dve.tensor_tensor(tmp[:, :], tmp[:, :], tmp[:, :], ALU.mult))
                st.then(dve.tensor_scalar(var[:, :], var[:, :], 1.0 / D_MODEL, LN_EPS, ALU.mult, ALU.add))
                st.then(dve.tensor_scalar(mean[:, :], mean[:, :], 0.5, None, ALU.mult))
                st.then(dve.scalar_tensor_tensor(out=var[:, :], in0=tmp[:, :], scalar=0.25, in1=var[:, :],
                                                 op0=ALU.mult, op1=ALU.add))
                dve.wait_ge(root.sem, root.at(1))
                st.then(dve.reciprocal(rstd[:, :], tmp[:, :]))
                for i in range(TILES):
                    if i >= 2 and xn is None:
                        dve.wait_ge(turned.sem, turned.at(i - 1))
                    dve.tensor_scalar(normal(i, i % 2), c.x[:, i * D_MODEL:(i + 1) * D_MODEL],
                                      mean[:, i:i + 1], rstd[:, i:i + 1], ALU.subtract, ALU.mult) \
                       .then_inc(normed.sem, 1)
                if last_step is not None:
                    last_step(dve)

            @block.scalar
            def _(act):
                act.wait_ge(own.sem, own.at(7))
                act.activation(tmp[:, :], var[:, :], ACT.Sqrt).then_inc(root.sem, 1)
                for i in range(TILES):
                    act.wait_ge(turned.sem, turned.at(i + 1))
                    act.activation(xnT[:, 0:KC * TOKENS].rearrange("p (k n) -> p k n", k=KC)[:, :, i * P:(i + 1) * P],
                                   c.banks[i % 2][:, 0:KC * P].rearrange("p (k n) -> p k n", k=KC),
                                   ACT.Copy).then_inc(kept.sem, 1)

            @block.tensor
            def _(pe):
                for i in range(TILES):
                    pe.wait_ge(normed.sem, normed.at(i + 1))
                    if i >= 2:
                        pe.wait_ge(kept.sem, kept.at(i - 1))
                    src = normal(i, i % 2)
                    for k in range(KC):
                        last = pe.transpose(c.banks[i % 2][:, k * P:(k + 1) * P],
                                            src[:, k * P:(k + 1) * P], c.ident[:, :])
                    last.then_inc(turned.sem, 1)
                    if products is not None and i >= 1:
                        pe.wait_ge(kept.sem, kept.at(i))
                        products(pe, i - 1)
                if products is not None:
                    pe.wait_ge(kept.sem, kept.at(TILES))
                    products(pe, TILES - 1)
    own.counted(8)
    root.counted(1)
    stat.counted(TILES)
    for q in (normed, turned, kept):
        q.counted(TILES)


def mamba(c):
    nc, t = c.nc, c.t
    with ExitStack() as s:
        sb = lambda name, shape, dt=F32: s.enter_context(nc.sbuf_tensor(name, shape, dt))
        xact = sb("mb_xact", [P, BLK * TOKENS])
        zgate = sb("mb_zgate", [P, BLK * TOKENS])
        cw, cb = sb("mb_conv_w", [P, BLK * D_CONV]), sb("mb_conv_b", [P, BLK])
        a_coef = sb("mb_a", [P, BLK * D_STATE])
        dskip, dtb = sb("mb_d", [P, BLK]), sb("mb_dt_b", [P, BLK])
        w_x = sb("mb_w_x", [P, BLK * 48])
        w_dt = sb("mb_w_dt", [DT_RANK, D_INNER])
        w_out = sb("mb_w_out", [P, BLK * D_MODEL])
        loaded = counter(c, "mb_loaded")
        inner = s.enter_context(ExitStack())
        xnT = inner.enter_context(nc.sbuf_tensor("mb_xnT", [P, KC * TOKENS], F32))
        w_in = inner.enter_context(nc.sbuf_tensor("mb_w_in", [P, KC * 2 * D_INNER], F32))
        LOADS = [
            (w_in[:, :].rearrange("p (k e) -> p k e", k=KC), t["in_wT"].rearrange("(k p) e -> p k e", p=P)),
            (cw[:, :].rearrange("p (b k) -> p b k", b=BLK), t["conv_w"].rearrange("(b p) k -> p b k", p=P)),
            (cb[:, :], t["conv_b"]), (dskip[:, :], t["D"]), (dtb[:, :], t["dt_b"]),
            (a_coef[:, :].rearrange("p (b n) -> p b n", b=BLK), t["A_log"].rearrange("(b p) n -> p b n", p=P)),
            (w_x[:, :].rearrange("p (b e) -> p b e", b=BLK), t["x_wT"].rearrange("(b p) e -> p b e", p=P)),
            (w_dt[:, :], t["dt_wT"]),
            (w_out[:, :].rearrange("p (b e) -> p b e", b=BLK), t["out_wT"].rearrange("(b p) e -> p b e", p=P)),
        ]

        def loads(sp):
            for dst, src in LOADS:
                sp.dma_start(dst, src).then_inc(loaded.sem, 16)

        layer_norm(c, xnT, loads=loads)

        proj, fetched, padded = counter(c, "mb_proj"), counter(c, "mb_fetched"), counter(c, "mb_padded")
        zproj, gated = counter(c, "mb_zproj"), counter(c, "mb_gated")
        own, conved, acted = counter(c, "mb_own"), counter(c, "mb_conved"), counter(c, "mb_acted")
        LEAD = D_CONV - 1
        WP = LEAD + SEQ
        with ExitStack() as q:
            xp = q.enter_context(nc.sbuf_tensor("mb_xpad", [P, 2 * WP], F32))
            cv = q.enter_context(nc.sbuf_tensor("mb_cv", [P, 2 * SEQ], F32))
            with nc.Block() as block:

                @block.tensor
                def _(pe):
                    pe.wait_ge(loaded.sem, loaded.at(16 * len(LOADS)))
                    for eb in range(BLK):
                        with pe.Fori(0, BATCH // 2) as j:
                            for u in range(2):
                                n = eb * BATCH + j * 2 + u
                                for gate, read, done in ((0, fetched, proj), (1, gated, zproj)):
                                    pe.wait_ge(read.sem, read.at(n - 1 if eb > 0 else j * 2))
                                    for k in range(KC):
                                        at = (k * 2 + gate) * D_INNER + eb * P
                                        last = pe.matmul(c.banks[2 * gate + u][:, :], w_in[:, at:at + P],
                                                         xnT[:, bass.ds(j * (2 * SEQ) + (k * TOKENS + u * SEQ), SEQ)],
                                                         start=(k == 0), stop=(k == KC - 1))
                                    last.then_inc(done.sem, 1)

                @block.scalar
                def _(act):
                    for b in range(BLK):
                        with act.Fori(0, BATCH // 2) as j:
                            for u in range(2):
                                n = b * BATCH + j * 2 + u
                                act.wait_ge(proj.sem, proj.at(n + 1))
                                act.wait_ge(conved.sem, conved.at(n - 1 if b else j * 2))
                                act.activation(xp[:, u * WP + LEAD:(u + 1) * WP], c.banks[u][:, :],
                                               ACT.Copy).then_inc(fetched.sem, 1)
                            for u in range(2):
                                n = b * BATCH + j * 2 + u
                                act.wait_ge(zproj.sem, zproj.at(n + 1))
                                act.activation(zgate[:, bass.ds(j * (2 * SEQ) + (b * TOKENS + u * SEQ), SEQ)],
                                               c.banks[2 + u][:, :], ACT.Silu).then_inc(gated.sem, 1)
                                act.wait_ge(conved.sem, conved.at(n + 1))
                                act.activation(xact[:, bass.ds(j * (2 * SEQ) + (b * TOKENS + u * SEQ), SEQ)],
                                               cv[:, u * SEQ:(u + 1) * SEQ], ACT.Silu).then_inc(acted.sem, 1)

                @block.vector
                def _(dve):
                    dve.wait_ge(loaded.sem, loaded.at(16 * len(LOADS)))
                    for u in range(2):
                        dve.memset(xp[:, u * WP:u * WP + LEAD], 0.0).then_inc(padded.sem, 1)
                    dve.wait_ge(padded.sem, padded.at(2))
                    for b in range(BLK):
                        with dve.Fori(0, BATCH // 2) as j:
                            for u in range(2):
                                n = b * BATCH + j * 2 + u
                                st = Steps(dve, own)
                                st.loop = n * (D_CONV - 1)
                                dst = cv[:, u * SEQ:(u + 1) * SEQ]
                                tap = lambda k: cw[:, b * D_CONV + k:b * D_CONV + k + 1]
                                dve.wait_ge(fetched.sem, fetched.at(n + 1))
                                if b == 0:
                                    dve.wait_ge(acted.sem, acted.at(j * 2))
                                else:
                                    dve.wait_ge(acted.sem, acted.at(n - 1))
                                st.then(dve.tensor_scalar(dst, xp[:, u * WP + LEAD:(u + 1) * WP], tap(LEAD),
                                                          cb[:, b:b + 1], ALU.mult, ALU.add))
                                for k in reversed(range(LEAD)):
                                    op = dve.scalar_tensor_tensor(
                                        out=dst, in0=xp[:, u * WP + k:u * WP + k + SEQ], scalar=tap(k),
                                        in1=dst, op0=ALU.mult, op1=ALU.add)
                                    if k:
                                        st.then(op)
                                    else:
                                        op.then_inc(conved.sem, 1)
        for q in (proj, zproj, fetched, gated):
            q.counted(BLK * BATCH)
        padded.counted(2)
        own.counted(BLK * BATCH * (D_CONV - 1))
        conved.counted(BLK * BATCH)
        acted.counted(BLK * BATCH)
        inner.close()

        dt = sb("mb_dt", [P, BLK * TOKENS])
        ux = sb("mb_ux", [P, BLK * TOKENS])
        bcT = t["scratch_bc"]
        xdbl, xkept, stored = counter(c, "mb_xdbl"), counter(c, "mb_xkept"), counter(c, "mb_bc_stored")
        dtp, dtr = counter(c, "mb_dtp"), counter(c, "mb_dtr")
        soft, summed = counter(c, "mb_soft"), counter(c, "mb_summed")
        with ExitStack() as q:
            dbl = q.enter_context(nc.sbuf_tensor("mb_dbl", [48, TOKENS], F32))
            with nc.Block() as block:

                @block.tensor
                def _(pe):
                    for b in range(BATCH):
                        if b >= 2:
                            pe.wait_ge(xkept.sem, xkept.at(b - 1))
                        for k in range(BLK):
                            last = pe.matmul(c.banks[b % 2][0:48, :], w_x[:, k * 48:(k + 1) * 48],
                                             xact[:, k * TOKENS + b * SEQ:k * TOKENS + (b + 1) * SEQ],
                                             start=(k == 0), stop=(k == BLK - 1))
                        last.then_inc(xdbl.sem, 1)
                    pe.wait_ge(xkept.sem, xkept.at(BATCH))
                    for n in range(BLK * BATCH):
                        k, b = divmod(n, BATCH)
                        if n >= 2:
                            pe.wait_ge(dtr.sem, dtr.at(2 * (n - 1)))
                        pe.matmul(c.banks[2 + n % 2][:, :], w_dt[:, k * P:(k + 1) * P],
                                  dbl[0:DT_RANK, b * SEQ:(b + 1) * SEQ], start=True, stop=True) \
                          .then_inc(dtp.sem, 1)

                @block.vector
                def _(dve):
                    for n in range(BLK * BATCH):
                        k = n // BATCH
                        at = slice(n * SEQ, (n + 1) * SEQ)
                        dve.wait_ge(dtp.sem, dtp.at(n + 1))
                        dve.tensor_scalar(ux[:, at], c.banks[2 + n % 2][:, :], dtb[:, k:k + 1], 0.0,
                                          ALU.add, ALU.max).then_inc(dtr.sem, 1)
                        dve.wait_ge(dtr.sem, dtr.at(2 * n + 1))
                        dve.scalar_tensor_tensor(out=dt[:, at], in0=ux[:, at], scalar=-2.0,
                                                 in1=c.banks[2 + n % 2][:, :], op0=ALU.mult, op1=ALU.add) \
                           .then_inc(dtr.sem, 1)
                    for k in range(BLK):
                        at = slice(k * TOKENS, (k + 1) * TOKENS)
                        dve.wait_ge(soft.sem, soft.at(2 + BLK + k + 1))
                        dve.tensor_tensor(dt[:, at], dt[:, at], ux[:, at], ALU.add).then_inc(summed.sem, 1)
                        dve.wait_ge(summed.sem, summed.at(k + 1))
                        dve.tensor_tensor(ux[:, at], dt[:, at], xact[:, at], ALU.mult)

                @block.scalar
                def _(act):
                    for b in range(BATCH):
                        act.wait_ge(xdbl.sem, xdbl.at(b + 1))
                        act.activation(dbl[:, b * SEQ:(b + 1) * SEQ], c.banks[b % 2][0:48, :],
                                       ACT.Copy).then_inc(xkept.sem, 1)
                    act.activation(a_coef[:, :], a_coef[:, :], ACT.Exp).then_inc(soft.sem, 1)
                    act.wait_ge(soft.sem, soft.at(1))
                    act.activation(a_coef[:, :], a_coef[:, :], ACT.Copy, scale=-1.0).then_inc(soft.sem, 1)
                    for k in range(BLK):
                        at = slice(k * TOKENS, (k + 1) * TOKENS)
                        act.wait_ge(dtr.sem, dtr.at(2 * (k + 1) * BATCH))
                        act.activation(dt[:, at], dt[:, at], ACT.Exp, bias=dtb[:, k:k + 1]).then_inc(soft.sem, 1)
                    for k in range(BLK):
                        at = slice(k * TOKENS, (k + 1) * TOKENS)
                        act.wait_ge(soft.sem, soft.at(2 + k + 1))
                        act.activation(dt[:, at], dt[:, at], ACT.Ln, bias=1.0).then_inc(soft.sem, 1)

                @block.sync
                def _(sp):
                    sp.wait_ge(xkept.sem, xkept.at(BATCH))
                    sp.dma_start(bcT, dbl[DT_RANK:48, :]).then_inc(stored.sem, 16)
                    sp.wait_ge(stored.sem, stored.at(16))
        for q, n in ((xdbl, BATCH), (xkept, BATCH), (stored, 16), (dtp, BLK * BATCH),
                     (dtr, 2 * BLK * BATCH), (soft, 2 + 2 * BLK), (summed, BLK)):
            q.counted(n)

        mamba_scan(c, xact, zgate, dt, ux, a_coef, dskip, bcT)

        outp, added = counter(c, "mb_outp"), counter(c, "mb_added")
        with nc.Block() as block:

            @block.tensor
            def _(pe):
                for i in range(TILES):
                    if i >= 2:
                        pe.wait_ge(added.sem, added.at(i - 1))
                    for k in range(BLK):
                        last = pe.matmul(c.banks[i % 2][:, 0:D_MODEL],
                                         xact[:, k * TOKENS + i * P:k * TOKENS + (i + 1) * P],
                                         w_out[:, k * D_MODEL:(k + 1) * D_MODEL],
                                         start=(k == 0), stop=(k == BLK - 1))
                    last.then_inc(outp.sem, 1)

            @block.vector
            def _(dve):
                for i in range(TILES):
                    at = slice(i * D_MODEL, (i + 1) * D_MODEL)
                    dve.wait_ge(outp.sem, outp.at(i + 1))
                    dve.tensor_tensor(c.x[:, at], c.x[:, at], c.banks[i % 2][:, 0:D_MODEL],
                                      ALU.add).then_inc(added.sem, 1)
        outp.counted(TILES)
        added.counted(TILES)


def mamba_scan(c, xact, zgate, dt, ux, a_coef, dskip, bcT):
    nc = c.nc
    ST = BLK * D_STATE
    TURNS = D_STATE // 2
    rows = [counter(c, f"sc_rows{u}") for u in range(2)]
    decay, scanned = counter(c, "sc_decay"), counter(c, "sc_scanned")
    used, out, edge = (counter(c, n) for n in ("sc_used", "sc_out", "sc_edge"))
    summed, gated, own = counter(c, "sc_summed"), counter(c, "sc_gated"), counter(c, "sc_own")
    with ExitStack() as s:
        sb = lambda name, shape, dt=F32: s.enter_context(nc.sbuf_tensor(name, shape, dt))
        da = sb("sc_da", [P, 2 * HALF])
        hb = sb("sc_h", [P, 4 * HALF])
        bc = sb("sc_bc", [P, 4 * HALF])
        DA = [da[:, u * HALF:(u + 1) * HALF] for u in range(2)]
        H = [hb[:, u * HALF:(u + 1) * HALF] for u in range(4)]
        B = [bc[:, u * 2 * HALF:u * 2 * HALF + HALF] for u in range(2)]
        C = [bc[:, u * 2 * HALF + HALF:(u + 1) * 2 * HALF] for u in range(2)]
        for half in range(2):
            lo = half * HALF
            with nc.Block() as block:

                @block.sync
                def _(sp):
                    def fetch(n, u):
                        for dst, row in ((B[u], n), (C[u], n + D_STATE)):
                            sp.dma_start(dst, bcT[bass.ds(row, 1), lo:lo + HALF].to_broadcast([P, HALF])) \
                              .then_inc(rows[u].sem, 16)

                    for u in range(2):
                        fetch(u, u)
                    with sp.Fori(0, D_STATE // 2 - 1) as j:
                        for u in range(2):
                            sp.wait_ge(used.sem, used.at(j * (2 * BLK) + (u + 1) * BLK))
                            fetch(j * 2 + (u + 2), u)

                @block.scalar
                def _(act):
                    act.wait_ge(edge.sem, edge.at(2))

                    def turn(j):
                        for v in range(2 * BLK):
                            n, b = divmod(v, BLK)
                            if not (isinstance(j, int) and j == 0 and v < 2):
                                act.wait_ge(scanned.sem, scanned.at(j * (2 * BLK) + (v - 1)))
                            act.activation(
                                DA[v % 2].rearrange("p (b t) -> p b t", b=2)[:, :, 1:SEQ],
                                dt[:, b * TOKENS + lo:b * TOKENS + lo + HALF]
                                .rearrange("p (b t) -> p b t", b=2)[:, :, 1:SEQ],
                                ACT.Exp, scale=a_coef[:, bass.ds(j * 2 + (b * D_STATE + n), 1)]) \
                               .then_inc(decay.sem, 1)

                    turn(0)
                    with act.Fori(0, TURNS - 1) as j:
                        turn(j + 1)

                @block.gpsimd
                def _(pool):
                    with pool.Fori(0, D_STATE // 2) as j:
                        for v in range(2 * BLK):
                            n, b = divmod(v, BLK)
                            step = j * (2 * BLK) + v
                            if b == 0:
                                pool.wait_ge(rows[n].sem, rows[n].at(j * 32 + 32))
                            pool.wait_ge(scanned.sem, scanned.at(step + 1))
                            pool.tensor_tensor(H[v % 4], H[v % 4], C[n], ALU.mult).then_inc(used.sem, 1)

                @block.vector
                def _(dve):
                    for u in range(2):
                        dve.memset(DA[u].rearrange("p (b t) -> p b t", b=2)[:, :, 0:1], 0.0) \
                           .then_inc(edge.sem, 1)
                    dve.wait_ge(edge.sem, edge.at(2))

                    def input_of(j, v):
                        n, b = divmod(v, BLK)
                        if b == 0:
                            dve.wait_ge(rows[n].sem, rows[n].at(j * 32 + 32))
                        if not (isinstance(j, int) and j == 0 and v < 4):
                            dve.wait_ge(out.sem, out.at(j * (2 * BLK) + (v - 3)))
                        dve.tensor_tensor(H[v % 4], ux[:, b * TOKENS + lo:b * TOKENS + lo + HALF],
                                          B[n], ALU.mult).then_inc(own.sem, 1)

                    def turn(j):
                        for v in range(2 * BLK):
                            step = j * (2 * BLK) + v
                            if v + 1 < 2 * BLK:
                                input_of(j, v + 1)
                            elif not (isinstance(j, int) and j == TURNS - 1):
                                input_of(j + 1, 0)
                            dve.wait_ge(own.sem, own.at(step + 1))
                            dve.wait_ge(decay.sem, decay.at(step + 1))
                            dve.tensor_tensor_scan(H[v % 4], DA[v % 2], H[v % 4], 0.0, ALU.mult, ALU.add) \
                               .then_inc(scanned.sem, 1)

                    input_of(0, 0)
                    turn(0)
                    with dve.Fori(0, TURNS - 2) as j:
                        turn(j + 1)
                    turn(TURNS - 1)
                    for b in range(BLK):
                        at = slice(b * TOKENS + lo, b * TOKENS + lo + HALF)
                        for q in range(2):
                            cut = slice(b * TOKENS + lo + q * SEQ, b * TOKENS + lo + (q + 1) * SEQ)
                            dve.wait_ge(summed.sem, summed.at(1))
                            dve.scalar_tensor_tensor(out=xact[:, cut], in0=xact[:, cut],
                                                     scalar=dskip[:, b:b + 1], in1=c.banks[2 * b + q][:, :],
                                                     op0=ALU.mult, op1=ALU.add).then_inc(gated.sem, 1)
                    dve.wait_ge(gated.sem, gated.at(2 * BLK))
                    for b in range(BLK):
                        at = slice(b * TOKENS + lo, b * TOKENS + lo + HALF)
                        dve.tensor_tensor(xact[:, at], xact[:, at], zgate[:, at], ALU.mult)

                @block.tensor
                def _(pe):
                    for k in range(8):
                        pe.matmul(c.banks[k][:, :], c.zeros[:, 0:P], c.zeros[:, :], start=True, stop=False)
                    with pe.Fori(0, D_STATE // 2) as j:
                        for v in range(2 * BLK):
                            b = v % BLK
                            pe.wait_ge(used.sem, used.at(j * (2 * BLK) + v + 1))
                            for q in range(2):
                                last = pe.matmul(c.banks[2 * b + q][:, :], c.ident[:, :],
                                                 H[v % 4][:, q * SEQ:(q + 1) * SEQ], start=False, stop=False)
                            last.then_inc(out.sem, 1)
                    for k in range(8):
                        last = pe.matmul(c.banks[k][:, :], c.zeros[:, 0:P], c.zeros[:, :], start=False, stop=True)
                    last.then_inc(summed.sem, 1)
            for q, n in ((rows[0], 16 * D_STATE), (rows[1], 16 * D_STATE), (decay, ST), (scanned, ST),
                         (used, ST), (out, ST), (edge, 2),
                         (own, ST),
                         (summed, 1), (gated, 2 * BLK)):
                q.counted(n)


def moe(c, which):
    nc, t = c.nc, c.t
    if which == 0:
        E, K, I, ROWS, NT, cap = M0_E, M0_K, M0_I, P, M0_TILES, None
    else:
        E, K, I, ROWS, NT, cap = M1_E, M1_K, M1_I, M1_CAP, M1_E, M1_CAP
    xs, ys = t[f"scratch_xs{which}"], t[f"scratch_ys{which}"]
    GU = 2 * I
    TK = TILES * K
    EB = -(-E * TILES // 512)
    TPBANK = TILES // EB
    with ExitStack() as s:
        sb = lambda name, shape, dt=F32: s.enter_context(nc.sbuf_tensor(name, shape, dt, allow_name_mangling=True))
        slots = sb("mo_slots", [P, TK], I32)
        weights = sb("mo_weights", [P, TK])
        tile_expert = sb("mo_tile_expert", [1, NT], I32) if cap is None else None
        w_gu = sb("mo_w_gu", [P, E * KC * GU])
        w_dn = sb("mo_w_dn", [I, E * D_MODEL])
        if which == 0:
            b_gu, b_dn = sb("mo_b_gu", [3, E * GU], BF16), sb("mo_b_dn", [3, E * D_MODEL], BF16)
        loaded, weights_in = counter(c, "mo_loaded"), counter(c, "mo_weights_in")
        scope = s.enter_context(ExitStack())
        sc = lambda name, shape, dt=F32: scope.enter_context(nc.sbuf_tensor(name, shape, dt, allow_name_mangling=True))
        xn = sc("mo_xn", [P, TILES * D_MODEL])
        gate = sc("mo_gate", [P, KC * E])
        bias = sc("mo_gate_b", [P, E])
        if which == 0:
            braw = sc("mo_braw", [E, GU + D_MODEL])
        else:
            gold, o2n = sc("mo_gold", [M1_OLD, D_MODEL]), sc("mo_o2n", [M1_OLD, 1], I32)
        WEIGHTS = [(w_gu[:, :], t[f"w_gu{which}"]), (w_dn[:, :], t[f"w_dn{which}"])]
        if which == 0:
            LOADS = [(gate[:, :].rearrange("p (k e) -> p k e", k=KC), t["gate0T"].rearrange("(k p) e -> p k e", p=P)),
                      (bias[:, :], t["gate_b"].to_broadcast([P, E])), (braw[:, :], t["b_all"])]
        else:
            LOADS = [(gold[:, :], t["gate1"]), (o2n[:, :], t["o2n"])]

        def loads(sp):
            for dst, src in LOADS:
                sp.dma_start(dst, src).then_inc(loaded.sem, 16)
            for dst, src in WEIGHTS:
                sp.dma_start(dst, src).then_inc(weights_in.sem, 16)

        logit, ldone, own, pown = (counter(c, n) for n in ("mo_logit", "mo_ldone", "mo_own", "mo_pown"))
        made, ranked, expd, counted_, moved, bsplit, bstored = (
            counter(c, "mo_" + n) for n in ("made", "ranked", "expd", "counted", "moved", "bsplit", "bstored"))
        placed, slotted = counter(c, "mo_placed"), counter(c, "mo_slotted")
        CHUNKS = 8
        with ExitStack() as q:
            sq = lambda name, shape, dt=F32: q.enter_context(nc.sbuf_tensor(name, shape, dt, allow_name_mangling=True))
            lg = sq("mo_lg", [P, TILES * E])
            iota_e = sq("mo_iota_e", [P, E])
            with ExitStack() as qq:
                xnT = qq.enter_context(nc.sbuf_tensor("mo_xnT", [P, KC * TOKENS], F32, allow_name_mangling=True))
                LG = c.banks[2:2 + EB]

                def logits(pe, i):
                    if i == 0 and which == 0:
                        pe.wait_ge(loaded.sem, loaded.at(16 * len(LOADS)))
                    for k in range(KC):
                        last = pe.matmul(LG[i // TPBANK][:, (i % TPBANK) * E:(i % TPBANK + 1) * E],
                                         xnT[:, k * TOKENS + i * P:k * TOKENS + (i + 1) * P],
                                         gate[:, k * E:(k + 1) * E], start=(k == 0), stop=(k == KC - 1))
                    if i == TILES - 1:
                        last.then_inc(logit.sem, 1)

                def add_bias(dve):
                    if which == 0:
                        dve.wait_ge(loaded.sem, loaded.at(16 * len(LOADS)))
                    dve.wait_ge(logit.sem, logit.at(1))
                    for g in range(EB):
                        cut = slice(g * TPBANK * E, (g + 1) * TPBANK * E)
                        dve.tensor_tensor(lg[:, cut].rearrange("p (t e) -> p t e", e=E),
                                          LG[g][:, 0:TPBANK * E].rearrange("p (t e) -> p t e", e=E),
                                          bias[:, :].rearrange("p (t e) -> p t e", t=1)
                                          .to_broadcast([P, TPBANK, E]), ALU.add).then_inc(ldone.sem, 1)

                if which == 1:
                    remap_gate(c, gold, o2n, gate, bias, loads, (loaded.sem, loaded.at(16 * len(LOADS))))
                layer_norm(c, xnT, xn=xn, loads=loads if which == 0 else None, products=logits,
                           last_step=add_bias)
            logit.counted(1)
            ldone.counted(EB)
            upper = sq("mo_upper", [P, P], BF16)
            top, topi, topf = sq("mo_top", [P, TILES * 8]), sq("mo_topi", [P, TILES * 8], U32), sq("mo_topf", [P, TK])
            hot = sq("mo_hot", [P, TK * E])
            mask = sq("mo_mask", [P, TILES * E], BF16)
            reset = sq("mo_reset", [P, E * TILES])
            incl = sq("mo_incl", [P, E * TILES])
            pos = sq("mo_pos", [P, TILES * E])
            cnt, nt, start, off = (sq(n, [P, E]) for n in ("mo_cnt", "mo_nt", "mo_start", "mo_off"))
            ssum = sq("mo_ssum", [P, TILES])
            slotf = sq("mo_slotf", [P, TK])
            te = lambda a: a[:, :].rearrange("p (t e) -> p t e", e=E)
            et = lambda a: a[:, :].rearrange("p (e t) -> p e t", t=TILES)
            if cap is None:
                steps16 = sq("mo_steps16", [P, E * TILES])
                over = sq("mo_over", [P, E * TILES])
                tile_id = sq("mo_tile_id", [NT, 1])
                before = sq("mo_before", [NT, E])
                texp = sq("mo_texp", [NT, 1])
                bparts = [sq(f"mo_bpart{i}", [E, GU + D_MODEL], BF16) for i in range(3)]

            with nc.Block() as block:

                @block.gpsimd
                def _(pool):
                    small = dict(allow_small_or_imprecise_dtypes=True)
                    pool.iota(iota_e[:, :], [[1, E]], 0, 0, **small).then_inc(made.sem, 1)
                    pool.memset(reset[:, :], 1.0).then_inc(pown.sem, 1)
                    pool.wait_ge(pown.sem, pown.at(1))
                    pool.memset(et(reset)[:, :, 0:1], 0.0)
                    pool.memset(upper[:, :], 1.0).then_inc(pown.sem, 1)
                    pool.wait_ge(pown.sem, pown.at(2))
                    pool.affine_select(out=upper[:, :], in_=upper[:, :], compare_op=ALU.is_gt, fill=0.0,
                                       base=0, pattern=[[1, P]], channel_multiplier=-1).then_inc(made.sem, 1)
                    if cap is None:
                        pool.iota(steps16[:, :], [[0, E], [ROWS, TILES]], 0, 0, **small).then_inc(made.sem, 1)
                        pool.iota(tile_id[:, :], [[0, 1]], 0, 1, **small).then_inc(made.sem, 1)
                    else:
                        pool.iota(off[:, :], [[ROWS, E]], 0, 0, **small).then_inc(made.sem, 2)
                    pool.wait_ge(c.filled.sem, 16 * c.fills)
                    for n in range(TK):
                        if n % (TK // CHUNKS) == 0:
                            pool.wait_ge(slotted.sem, slotted.at(n // (TK // CHUNKS) + 1))
                        i = n // K
                        pool.indirect_dma_start(xs, bass.IndirectOffsetOnAxis(ap=slots[:, n:n + 1], axis=0),
                                                xn[:, i * D_MODEL:(i + 1) * D_MODEL], None,
                                                bounds_check=NT * ROWS - 1, oob_is_err=False) \
                            .then_inc(moved.sem, 16)
                    pool.wait_ge(moved.sem, moved.at(16 * TK))

                @block.tensor
                def _(pe):
                    pe.wait_ge(ranked.sem, ranked.at(1))
                    pe.wait_ge(made.sem, made.at(4))
                    for g in range(EB):
                        cut = slice(g * TPBANK * E, (g + 1) * TPBANK * E)
                        pe.matmul(c.banks[g][:, 0:TPBANK * E], upper[:, :], mask[:, cut], start=True, stop=True)
                        last = pe.matmul(c.banks[EB + g][:, 0:TPBANK * E], c.ones[:, :], mask[:, cut],
                                         start=True, stop=True)
                    last.then_inc(counted_.sem, 1)
                    if cap is None:
                        pe.wait_ge(placed.sem, placed.at(1))
                        pe.matmul(c.banks[7][0:1, 0:NT], texp[:, :], c.ident[0:NT, 0:NT], start=True, stop=True) \
                          .then_inc(placed.sem, 1)

                @block.scalar
                def _(act):
                    act.wait_ge(expd.sem, expd.at(1))
                    act.activation(weights[:, :], weights[:, :], ACT.Exp).then_inc(expd.sem, 1)

                if which == 0:
                    @block.sync
                    def _(sp):
                        sp.wait_ge(bsplit.sem, bsplit.at(5))
                        for i in range(3):
                            sp.dma_start(b_gu[i:i + 1, :].rearrange("a (e n) -> a e n", e=E),
                                         bparts[i][:, 0:GU]) \
                              .then_inc(bstored.sem, 16)
                            sp.dma_start(b_dn[i:i + 1, :].rearrange("a (e n) -> a e n", e=E),
                                         bparts[i][:, GU:]) \
                              .then_inc(bstored.sem, 16)
                        sp.wait_ge(bstored.sem, bstored.at(96))

                @block.vector
                def _(dve):
                    st = Steps(dve, own)
                    if which == 0:
                        sp_ = Steps(dve, bsplit)
                        sp_.then(dve.tensor_copy(bparts[0][:, :], braw[:, :]))
                        sp_.then(dve.tensor_tensor(braw[:, :], braw[:, :], bparts[0][:, :], ALU.subtract))
                        sp_.then(dve.tensor_copy(bparts[1][:, :], braw[:, :]))
                        sp_.then(dve.tensor_tensor(braw[:, :], braw[:, :], bparts[1][:, :], ALU.subtract))
                        sp_.then(dve.tensor_copy(bparts[2][:, :], braw[:, :]))
                    for i in range(TILES):
                        dve.max(top[:, i * 8:(i + 1) * 8], lg[:, i * E:(i + 1) * E]).then_inc(own.sem, 1)
                    dve.wait_ge(own.sem, own.at(TILES))
                    for i in range(TILES):
                        dve.max_index(topi[:, i * 8:(i + 1) * 8], top[:, i * 8:(i + 1) * 8],
                                      lg[:, i * E:(i + 1) * E]).then_inc(own.sem, 1)
                    dve.wait_ge(own.sem, own.at(2 * TILES))
                    st.n = 2 * TILES
                    top3 = top[:, :].rearrange("p (t k) -> p t k", k=8)
                    wk = weights[:, :].rearrange("p (t k) -> p t k", k=K)
                    st.then(dve.tensor_copy(topf[:, :].rearrange("p (t k) -> p t k", k=K),
                                            topi[:, :].rearrange("p (t k) -> p t k", k=8)[:, :, 0:K]))
                    dve.tensor_tensor(wk, top3[:, :, 0:K], top3[:, :, 0:1].to_broadcast([P, TILES, K]),
                                      ALU.subtract).then_inc(expd.sem, 1)
                    dve.wait_ge(made.sem, made.at(1))
                    hot3 = hot[:, :].rearrange("p (n e) -> p n e", e=E)
                    st.then(dve.tensor_tensor(
                        hot3, topf[:, :].rearrange("p (n o) -> p n o", o=1).to_broadcast([P, TK, E]),
                        iota_e[:, :].rearrange("p (o e) -> p o e", o=1).to_broadcast([P, TK, E]), ALU.is_equal))
                    hot4 = hot[:, :].rearrange("p (t k e) -> p t k e", k=K, e=E)
                    for k in range(1, K):
                        if k == 1:
                            st.then(dve.tensor_tensor(te(mask), hot4[:, :, 0, :], hot4[:, :, 1, :], ALU.add))
                        else:
                            op = dve.tensor_tensor(te(mask), te(mask), hot4[:, :, k, :], ALU.add)
                            if k < K - 1:
                                st.then(op)
                            else:
                                op.then_inc(ranked.sem, 1)
                    dve.wait_ge(expd.sem, expd.at(2))
                    st.then(dve.tensor_reduce(ssum[:, :], wk, AX, ALU.add))
                    st.then(dve.reciprocal(ssum[:, :], ssum[:, :]))
                    st.then(dve.tensor_tensor(wk, wk, ssum[:, :].rearrange("p (t o) -> p t o", o=1)
                                              .to_broadcast([P, TILES, K]), ALU.mult))
                    dve.wait_ge(made.sem, made.at(4))
                    dve.wait_ge(counted_.sem, counted_.at(1))
                    for g in range(EB):
                        st.then(dve.tensor_copy(
                            et(incl)[:, :, g * TPBANK:(g + 1) * TPBANK],
                            c.banks[EB + g][:, 0:TPBANK * E].rearrange("p (t e) -> p e t", e=E)))
                    st.then(dve.tensor_copy(pos[:, :].rearrange("p (t e) -> p e t", e=E), et(incl)))
                    st.then(dve.tensor_tensor_scan(incl[:, :], reset[:, :], incl[:, :], 0.0, ALU.mult, ALU.add))
                    st.then(dve.tensor_tensor(te(pos), incl[:, :].rearrange("p (e t) -> p t e", t=TILES),
                                              te(pos), ALU.subtract))
                    for g in range(EB):
                        cut = slice(g * TPBANK * E, (g + 1) * TPBANK * E)
                        st.then(dve.tensor_tensor(pos[:, cut], pos[:, cut], c.banks[g][:, 0:TPBANK * E], ALU.add))
                    whole = lambda a, n: a.rearrange("p (o e) -> p o e", o=1).to_broadcast([a.shape[0], n, E])
                    if cap is None:
                        st.then(dve.tensor_copy(cnt[:, :], et(incl)[:, :, TILES - 1]))
                        st.then(dve.tensor_tensor(et(over), cnt[:, :].rearrange("p (e o) -> p e o", o=1)
                                                  .to_broadcast([P, E, TILES]), et(steps16), ALU.is_gt))
                        st.then(dve.tensor_reduce(nt[:, :], et(over), AX, ALU.add))
                        st.then(dve.memset(cnt[:, :], 1.0))
                        st.then(dve.tensor_tensor_scan(start[:, :], cnt[:, :], nt[:, :], 0.0, ALU.mult, ALU.add))
                        st.then(dve.tensor_tensor(start[:, :], start[:, :], nt[:, :], ALU.subtract))
                        st.then(dve.tensor_scalar(off[:, :], start[:, :], float(ROWS), None, ALU.mult))
                        st.then(dve.tensor_scalar(before[:, :], start[0:NT, :], tile_id[:, 0:1], None, ALU.is_le))
                        st.then(dve.tensor_reduce(texp[:, :], before[:, :], AX, ALU.add))
                        dve.tensor_scalar(texp[:, :], texp[:, :], -1.0, None, ALU.add).then_inc(placed.sem, 1)
                        dve.wait_ge(placed.sem, placed.at(2))
                        st.then(dve.tensor_copy(tile_expert[:, :], c.banks[7][0:1, 0:NT]))
                        st.then(dve.tensor_tensor(te(pos), te(pos), whole(off[:, :], TILES), ALU.add))
                    else:
                        st.then(dve.tensor_scalar(incl[:, :], pos[:, :], float(cap), FAR, ALU.is_ge, ALU.mult))
                        st.then(dve.tensor_tensor(pos[:, :], pos[:, :], incl[:, :], ALU.add))
                        st.then(dve.tensor_tensor(te(pos), te(pos), whole(off[:, :], TILES), ALU.add))
                    for ch in range(CHUNKS):
                        ts, ns = (slice(ch * n // CHUNKS, (ch + 1) * n // CHUNKS) for n in (TILES, TK))
                        st.then(dve.tensor_tensor(
                            hot4[:, ts], hot4[:, ts],
                            pos[:, :].rearrange("p (t o e) -> p t o e", o=1, e=E)[:, ts]
                            .to_broadcast([P, TILES // CHUNKS, K, E]), ALU.mult))
                        st.then(dve.tensor_reduce(slotf[:, ns], hot3[:, ns], AX, ALU.add))
                        dve.tensor_copy(slots[:, ns], slotf[:, ns]).then_inc(slotted.sem, 1)
                    if cap is not None:
                        dve.wait_ge(slotted.sem, slotted.at(CHUNKS))
                        st.then(dve.tensor_scalar(slotf[:, :], slotf[:, :], float(NT * ROWS), None, ALU.is_lt))
                        st.then(dve.tensor_tensor(weights[:, :], weights[:, :], slotf[:, :], ALU.mult))
                    moe.own = st.n
            own.counted(moe.own)
            for w, n in ((slotted, CHUNKS), (placed, 2 if cap is None else 0), (made, 4), (pown, 2),
                         (expd, 2), (ranked, 1), (counted_, 1),
                         (bsplit, 5 if which == 0 else 0), (bstored, 96 if which == 0 else 0)):
                w.counted(n)
            moved.counted(16 * TK)
        scope.close()
        loaded.counted(16 * len(LOADS))

        experts(c, which, E, I, ROWS, NT, xs, ys, w_gu, w_dn, (b_gu, b_dn) if which == 0 else None, tile_expert,
                (weights_in.sem, weights_in.at(16 * len(WEIGHTS))))
        weights_in.counted(16 * len(WEIGHTS))

        NB = 16
        fetched = [counter(c, f"mo_fetched{i}") for i in range(NB)]
        added = counter(c, "mo_added")
        with ExitStack() as q:
            yb = q.enter_context(nc.sbuf_tensor("mo_yb", [P, NB * D_MODEL], F32, allow_name_mangling=True))
            with nc.Block() as block:

                @block.gpsimd
                def _(pool):
                    if cap is not None:
                        pool.memset(yb[:, :], 0.0).then_inc(pown.sem, 1)
                        pool.wait_ge(pown.sem, pown.at(1))
                    for n in range(TK):
                        u = n % NB
                        if n >= NB:
                            pool.wait_ge(added.sem, added.at(n - NB + 1))
                        pool.indirect_dma_start(yb[:, u * D_MODEL:(u + 1) * D_MODEL], None, ys,
                                                bass.IndirectOffsetOnAxis(ap=slots[:, n:n + 1], axis=0),
                                                bounds_check=NT * ROWS - 1, oob_is_err=False) \
                            .then_inc(fetched[u].sem, 16)

                @block.vector
                def _(dve):
                    for n in range(TK):
                        u, i = n % NB, n // K
                        at = slice(i * D_MODEL, (i + 1) * D_MODEL)
                        dve.wait_ge(fetched[u].sem, fetched[u].at(16 * (n // NB + 1)))
                        if n % K:
                            dve.wait_ge(added.sem, added.at(n))
                        dve.scalar_tensor_tensor(out=c.x[:, at], in0=yb[:, u * D_MODEL:(u + 1) * D_MODEL],
                                                 scalar=weights[:, n:n + 1], in1=c.x[:, at],
                                                 op0=ALU.mult, op1=ALU.add).then_inc(added.sem, 1)
        added.counted(TK)
        if cap is not None:
            pown.counted(1)
        for u in range(NB):
            fetched[u].counted(16 * (TK // NB))


def remap_gate(c, gold, o2n, gate, bias, loads, loaded):
    nc = c.nc
    E = M1_E
    made, own, mm = counter(c, "rg_made"), counter(c, "rg_own"), counter(c, "rg_mm")
    with ExitStack() as s:
        sb = lambda name, shape, dt=F32: s.enter_context(nc.sbuf_tensor(name, shape, dt, allow_name_mangling=True))
        o2f, m, mb = sb("rg_o2f", [P, 1]), sb("rg_m", [P, E]), sb("rg_mb", [P, E], BF16)
        with nc.Block() as block:

            @block.sync
            def _(sp):
                loads(sp)

            @block.gpsimd
            def _(pool):
                pool.iota(m[:, :], [[1, E]], 0, 0, allow_small_or_imprecise_dtypes=True).then_inc(made.sem, 1)

            @block.vector
            def _(dve):
                st = Steps(dve, own)
                dve.wait_ge(*loaded)
                st.then(dve.tensor_copy(o2f[:, :], o2n[:, :]))
                dve.wait_ge(made.sem, made.at(1))
                st.then(dve.tensor_scalar(m[:, :], m[:, :], o2f[:, 0:1], None, ALU.is_equal))
                st.then(dve.tensor_copy(mb[:, :], m[:, :]))
                dve.wait_ge(mm.sem, mm.at(1))
                for k in range(KC):
                    dve.tensor_copy(gate[:, k * E:(k + 1) * E], c.banks[k][:, 0:E])
                st.then(dve.tensor_scalar(bias[:, :], c.banks[KC][:, 0:E], 0.5, None, ALU.is_lt))
                dve.tensor_scalar(bias[:, :], bias[:, :], NEG, None, ALU.mult)

            @block.tensor
            def _(pe):
                pe.wait_ge(own.sem, own.at(3))
                pe.wait_ge(*loaded)
                for k in range(KC):
                    pe.matmul(c.banks[k][:, 0:E], gold[:, k * P:(k + 1) * P], m[:, :], start=True, stop=True)
                pe.matmul(c.banks[KC][:, 0:E], c.ones[:, :], mb[:, :], start=True, stop=True).then_inc(mm.sem, 1)
    made.counted(1)
    own.counted(4)
    mm.counted(1)


def experts(c, which, E, I, ROWS, NT, xs, ys, w_gu, w_dn, biases, tile_expert, weights_in):
    nc = c.nc
    GU = 2 * I
    NR = 4
    BODY = 2 * NR
    rows_in = [counter(c, f"ex_rows_in{u}") for u in range(NR)]
    rows_out = [counter(c, f"ex_rows_out{u}") for u in range(NR)]
    x_turned, x_kept, gate_done, clipped, act_done, gated, hidden_done, h_turned, h_kept, down_done, y_kept = (
        counter(c, "ex_" + n) for n in ("x_turned", "x_kept", "gate_up", "clipped", "act", "gated", "hidden",
                                       "h_turned", "h_kept", "down", "y_kept"))

    def steps(eng, step):
        for i in range(NR):
            step(i, i)
        with eng.Fori(0, NT // BODY - 1) as j:
            for v in range(BODY):
                step(j * BODY + (NR + v), v)
        for i in range(NT - NR, NT + NR):
            step(i, BODY + i % NR)

    def exists(i):
        return not isinstance(i, int) or 0 <= i < NT

    with ExitStack() as s:
        sb = lambda name, shape, dt=F32: s.enter_context(nc.sbuf_tensor(name, shape, dt, allow_name_mangling=True))
        xr = [sb(f"ex_xr{u}", [ROWS, D_MODEL]) for u in range(NR)]
        yo = [sb(f"ex_yo{u}", [ROWS, D_MODEL]) for u in range(NR)]
        xT = [sb(f"ex_xT{u}", [P, KC * ROWS]) for u in range(2)]
        g, up, sg, h = ([sb(f"ex_{n}{u}", [ROWS, I]) for u in range(2)] for n in ("g", "up", "sg", "h"))
        hT = [sb(f"ex_hT{u}", [I, ROWS]) for u in range(2)]
        XT, GUB, HT, YB = (c.banks[2 * k:2 * k + 2] for k in range(4))

        with nc.Block() as block:

            @block.sync
            def _(sp):
                def load(i, u):
                    sp.dma_start(xr[u][:, :], xs[bass.ds(i * ROWS, ROWS), :]).then_inc(rows_in[u].sem, 16)

                def store(i, u):
                    sp.wait_ge(y_kept.sem, y_kept.at(i + 1))
                    sp.dma_start(ys[bass.ds(i * ROWS, ROWS), :], yo[u][:, :]).then_inc(rows_out[u].sem, 16)

                def turn(i, u):
                    sp.wait_ge(x_turned.sem, x_turned.at(i + 1))
                    load(i + NR, u)

                for u in range(NR):
                    load(u, u)
                for u in range(NR):
                    turn(u, u)
                with sp.Fori(0, NT // NR - 2) as j:
                    for u in range(NR):
                        turn(j * NR + (u + NR), u)
                        store(j * NR + u, u)
                for i in range(NT - 2 * NR, NT):
                    store(i, i % NR)
                for u in range(NR):
                    sp.wait_ge(rows_out[u].sem, rows_out[u].at(16 * (NT // NR)))

            @block.tensor
            def _(pe):
                def turn_x(i, phase):
                    u, r = phase % 2, phase % NR
                    pe.wait_ge(rows_in[r].sem, rows_in[r].at(i * (16 // NR) + (NR - r) * (16 // NR)))
                    for k in range(KC):
                        last = pe.transpose(XT[u][:, k * ROWS:(k + 1) * ROWS], xr[r][:, k * P:(k + 1) * P],
                                            c.ident[0:ROWS, 0:ROWS])
                    last.then_inc(x_turned.sem, 1)

                experts_known = {}

                def expert_of(i, place):
                    if tile_expert is None:
                        return i
                    if place not in experts_known:
                        experts_known[place] = pe.value_load(tile_expert[0:1, bass.ds(i, 1)],
                                                             min_val=0, max_val=E - 1)
                    return experts_known[place]

                def gate_up(i, phase):
                    u, e = phase % 2, expert_of(i, phase)
                    pe.wait_ge(x_kept.sem, x_kept.at(i + 1))
                    for k in range(KC):
                        last = pe.matmul(GUB[u][0:ROWS, 0:GU], xT[u][:, k * ROWS:(k + 1) * ROWS],
                                         w_gu[:, bass.ds(e * (KC * GU) + k * GU, GU)],
                                         start=(k == 0), stop=(k == KC - 1 and biases is None))
                    if biases is not None:
                        last = pe.matmul(GUB[u][0:ROWS, 0:GU], c.ones[0:3, 0:ROWS],
                                         biases[0][:, bass.ds(e * GU, GU)], start=False, stop=True)
                    last.then_inc(gate_done.sem, 1)

                def turn_h(i, phase):
                    u = phase % 2
                    pe.wait_ge(hidden_done.sem, hidden_done.at(i + 1))
                    pe.transpose(HT[u][0:I, 0:ROWS], h[u][:, :], c.ident[0:ROWS, 0:ROWS]) \
                      .then_inc(h_turned.sem, 1)

                def down(i, phase):
                    u, e = phase % 2, expert_of(i, phase)
                    pe.wait_ge(y_kept.sem, y_kept.at(i - 1))
                    pe.wait_ge(h_kept.sem, h_kept.at(i + 1))
                    last = pe.matmul(YB[u][0:ROWS, 0:D_MODEL], hT[u][:, :],
                                     w_dn[:, bass.ds(e * D_MODEL, D_MODEL)], start=True, stop=(biases is None))
                    if biases is not None:
                        last = pe.matmul(YB[u][0:ROWS, 0:D_MODEL], c.ones[0:3, 0:ROWS],
                                         biases[1][:, bass.ds(e * D_MODEL, D_MODEL)], start=False, stop=True)
                    last.then_inc(down_done.sem, 1)

                def step(i, phase):
                    if phase in (0, BODY):
                        experts_known.clear()
                    if exists(i + 1):
                        turn_x(i + 1, phase + 1)
                    if exists(i - 2):
                        turn_h(i - 2, phase - 2)
                    if exists(i):
                        gate_up(i, phase)
                    if exists(i - 3):
                        down(i - 3, phase - 3)

                pe.wait_ge(*weights_in)
                turn_x(0, 0)
                steps(pe, step)

            @block.scalar
            def _(act):
                def keep_x(i, phase):
                    u = phase % 2
                    act.wait_ge(x_turned.sem, x_turned.at(i + 1))
                    act.activation(xT[u][:, :], XT[u][:, 0:KC * ROWS], ACT.Copy).then_inc(x_kept.sem, 1)

                def gate_act(i, phase):
                    u = phase % 2
                    if which == 0:
                        act.wait_ge(clipped.sem, clipped.at(i * 2 + 1))
                        act.activation(sg[u][:, :], g[u][:, :], ACT.Sigmoid, scale=1.702).then_inc(act_done.sem, 1)
                    else:
                        act.wait_ge(gate_done.sem, gate_done.at(i + 1))
                        act.activation(sg[u][:, :], GUB[u][0:ROWS, 0:I], ACT.Silu).then_inc(act_done.sem, 1)

                def keep_h(i, phase):
                    u = phase % 2
                    act.wait_ge(h_turned.sem, h_turned.at(i + 1))
                    act.activation(hT[u][:, :], HT[u][0:I, 0:ROWS], ACT.Copy).then_inc(h_kept.sem, 1)

                def step(i, phase):
                    if exists(i + 1):
                        keep_x(i + 1, phase + 1)
                    if exists(i - 2):
                        keep_h(i - 2, phase - 2)
                    if exists(i):
                        gate_act(i, phase)

                keep_x(0, 0)
                steps(act, step)

            @block.vector
            def _(dve):
                def clip(i, phase):
                    u = phase % 2
                    dve.wait_ge(gate_done.sem, gate_done.at(i + 1))
                    dve.tensor_scalar(g[u][:, :], GUB[u][0:ROWS, 0:I], 7.0, None, ALU.min) \
                       .then_inc(clipped.sem, 1)
                    dve.tensor_scalar(up[u][:, :], GUB[u][0:ROWS, I:GU], -7.0, 7.0, ALU.max, ALU.min) \
                       .then_inc(clipped.sem, 1)

                def hidden(i, phase):
                    u = phase % 2
                    if which == 0:
                        dve.wait_ge(clipped.sem, clipped.at(i * 2 + 2))
                        dve.wait_ge(act_done.sem, act_done.at(i + 1))
                        dve.tensor_tensor(g[u][:, :], g[u][:, :], sg[u][:, :], ALU.mult).then_inc(gated.sem, 1)
                        dve.wait_ge(gated.sem, gated.at(i + 1))
                        dve.scalar_tensor_tensor(out=h[u][:, :], in0=up[u][:, :], scalar=1.0, in1=g[u][:, :],
                                                 op0=ALU.add, op1=ALU.mult).then_inc(hidden_done.sem, 1)
                    else:
                        dve.wait_ge(act_done.sem, act_done.at(i + 1))
                        dve.tensor_tensor(h[u][:, :], sg[u][:, :], GUB[u][0:ROWS, I:GU], ALU.mult) \
                           .then_inc(hidden_done.sem, 1)

                def keep_y(i, phase):
                    u, r = phase % 2, phase % NR
                    dve.wait_ge(rows_out[r].sem, rows_out[r].at(i * (16 // NR) - r * (16 // NR)))
                    dve.wait_ge(down_done.sem, down_done.at(i + 1))
                    dve.tensor_copy(yo[r][:, :], YB[u][0:ROWS, 0:D_MODEL]).then_inc(y_kept.sem, 1)

                def step(i, phase):
                    if exists(i) and which == 0:
                        clip(i, phase)
                    if exists(i - 4):
                        keep_y(i - 4, phase)
                    if exists(i):
                        hidden(i, phase)

                steps(dve, step)
    for u in range(NR):
        rows_in[u].counted(16 * (NT // NR))
        rows_out[u].counted(16 * (NT // NR))
    for w in (x_turned, x_kept, gate_done, act_done, hidden_done, h_turned, h_kept, down_done, y_kept):
        w.counted(NT)
    if which == 0:
        clipped.counted(2 * NT)
        gated.counted(NT)


class Heads:

    def __init__(self, name, heads, dim, kv_heads, scale, causal, rot=0, interleaved=False, window=0):
        self.name, self.H, self.D, self.KH, self.scale, self.causal = name, heads, dim, kv_heads, scale, causal
        self.rot, self.interleaved, self.window = rot, interleaved, window
        self.HG = 4
        self.G = heads // self.HG
        self.latent = kv_heads == 1
        self.parts = not self.latent
        self.cut = heads * dim > P * self.HG
        self.KT = min(4, kv_heads)


ROTARY = Heads("ra", 16, 16, 16, 0.25, True, rot=8, interleaved=True)
SINKS = Heads("sa", 32, 64, 8, 0.125, False, rot=16, window=64)
LATENT = Heads("la", 16, 128, 1, 1.0 / float(np.sqrt(128.0)), True)


def rotate(st, a, dst, src, n, tile, cos, sin, t1, t2):
    eng, R = st.eng, a.rot
    if a.interleaved:
        v = lambda x: x.rearrange("p (h r s) -> p h s r", h=n, s=2)
    else:
        v = lambda x: x.rearrange("p (h s r) -> p h s r", h=n, s=2)
    small = lambda x: x[:, 0:n * 2 * R].rearrange("p (h s r) -> p h s r", h=n, s=2)
    c_, s_ = (x[:, tile * R:(tile + 1) * R].rearrange("p (h r) -> p h r", h=1).to_broadcast([P, n, R])
              for x in (cos, sin))
    for half in range(2):
        eng.tensor_tensor(small(t1)[:, :, half, :], v(src)[:, :, half, 0:R], c_, ALU.mult)
        op = eng.tensor_tensor(small(t2)[:, :, half, :], v(src)[:, :, 1 - half, 0:R], s_, ALU.mult)
        if half == 0 and R * 2 < a.D:
            eng.tensor_copy(v(dst)[:, :, :, R:], v(src)[:, :, :, R:])
    st.then(op)
    for half in range(2):
        minus = (half == 0) == a.interleaved
        op = eng.tensor_tensor(v(dst)[:, :, half, 0:R], small(t1)[:, :, half, :], small(t2)[:, :, half, :],
                               ALU.subtract if minus else ALU.add)
    return op


def attention(c, a):
    nc, t = c.nc, c.t
    QW = a.HG * a.D
    KW = a.KH * a.D
    HD = a.H * a.D
    OC = HD // P
    UN = TPB * a.HG
    with ExitStack() as s:
        sb = lambda name, shape, dt=F32: s.enter_context(nc.sbuf_tensor(f"{a.name}_{name}", shape, dt))
        sig = {n: counter(c, "at_" + n) for n in (
            "loaded", "made", "whigh", "wlow", "xkept", "xlow", "kvp", "kput", "vput", "kturned", "kkept",
            "klow", "qp", "qraw", "qput", "qturned", "qkept", "qlow", "ylow",
            "scored", "maxed", "negged", "exped", "turned", "kept_d", "kept_a", "summed", "normed", "own_k",
            "own_q", "own_n", "own_o", "yturned", "ykept", "outp", "added")}
        at = lambda n, v: (sig[n].sem, sig[n].at(v))
        inc = lambda n: (sig[n].sem, 1)
        yb = sb("y", [P, TPB * HD])
        if a.cut:
            wide = OC * D_MODEL if a.latent else KC * KW
            RAW = (yb[:, 0:KC * HD], sb("w_k", [P, KC * KW])[:, :], yb[:, KC * HD:KC * HD + wide])
            PARTS = [[sb(f"w{i}_{w}", [P, raw.shape[1]], F32R) for w in range(2)] for i, raw in enumerate(RAW)]
            (w_q, w_k, third), (WQ, WK, THIRD) = RAW, PARTS
            if a.latent:
                w_o, WO = third, THIRD
            else:
                w_v, WV, w_o = third, THIRD, sb("w_o", [P, OC * D_MODEL])
                WO = [w_o]
        else:
            w_q, w_k, w_o = sb("w_q", [P, KC * HD]), sb("w_k", [P, KC * KW]), sb("w_o", [P, OC * D_MODEL])
            w_v = sb("w_v", [P, KC * KW])
            WQ, WK, WV, WO = [w_q], [w_k], [w_v], [w_o]
        fold = lambda w, src: (w[:, :].rearrange("p (k n) -> p k n", k=KC), src.rearrange("(k p) n -> p k n", p=P))
        LOADS = [fold(w_q, t[a.name + "_wq"]), fold(w_k, t[a.name + "_wk"]),
                 (w_o[:, :].rearrange("p (k n) -> p k n", k=OC),
                  t[a.name + "_wo"].rearrange("(k p) n -> p k n", p=P))]
        if not a.latent:
            LOADS.append(fold(w_v, t[a.name + "_wv"]))
        if a.rot:
            cos, sin = sb("cos", [P, TPB * a.rot]), sb("sin", [P, TPB * a.rot])
            for x, n in ((cos, "_cos"), (sin, "_sin")):
                LOADS.append((x[:, :].rearrange("p (t r) -> p t r", t=TPB),
                              t[a.name + n].rearrange("(t p) r -> p t r", p=P)))
        if a.latent:
            b_q, b_k, b_o = sb("b_q", [P, HD]), sb("b_k", [P, KW]), sb("b_o", [P, D_MODEL])
            LOADS += [(b_q[:, :], t["la_bq"].to_broadcast([P, HD])), (b_k[:, :], t["la_bk"].to_broadcast([P, KW])),
                      (b_o[:, :], t["la_bo"].to_broadcast([P, D_MODEL]))]
        if a.window:
            sink = sb("sink", [P, a.H])
            negsink = sb("negsink", [P, a.H])
            LOADS.append((sink[:, :], t["sinks"].to_broadcast([P, a.H])))

        def loads(sp):
            for dst, src in LOADS:
                sp.dma_start(dst, src).then_inc(sig["loaded"].sem, 16)

        xnT = sb("xnT", [P, KC * TOKENS + SEQ])
        layer_norm(c, xnT, loads=loads)

        MW = 2 * P if a.window else P
        mask, identb = sb("mask", [P, MW], BF16), sb("identb", [P, P], BF16)
        CUT, NC = (F32R, 2) if a.latent else (F32, 1)
        TRIPLE = ((0, 0), (0, 1), (1, 0)) if a.latent else ((0, 0),)
        XTRIPLE = ((0, 0), (0, 1), (1, 0)) if a.cut else ((0, 0),)
        xb = [sb(f"xb{w}", [P, KC * SEQ], F32R if a.cut else F32) for w in range(1 + a.cut)]
        REP = 2 if 4 * a.D <= 64 else 1
        WR = 2 * REP * a.D if a.parts else a.D
        PASSES = 2 if a.latent or REP == 1 else 1
        PART = F32R if a.parts else F32
        kst = sb("kst", [P, a.KH * WR], PART)
        kT = [sb(f"kT{w}", [WR, a.KH * SEQ], F32R) for w in range(NC)]
        VW = KW + P - a.D
        vv = sb("v", [P, TPB * VW])
        qst = sb("qst", [P, a.HG * WR], PART)
        qT = [[sb(f"qT{u}_{w}", [WR, a.HG * P], F32R) for w in range(PASSES)] for u in range(2)]
        pr = [sb(f"p{u}", [P, SEQ]) for u in range(4)]
        pT = [sb(f"pT{u}", [P, SEQ]) for u in range(2)]
        if a.parts:
            krot, qraw, qrot = sb("krot", [P, KW]), sb("qraw", [P, QW]), sb("qrot", [P, QW])
        mx, nm, rs = (sb(n, [P, 2 * a.HG]) for n in ("mx", "nm", "rs"))
        es, rinv = (sb(n, [P, 2 * a.HG]) for n in ("es", "rinv"))
        yT = [[sb(f"yT{u}_{w}", [P, min(4, OC) * P], CUT) for w in range(NC)] for u in range(2)]
        t1, t2 = (sb(n, [P, a.KH * 2 * a.rot]) if a.rot else None for n in ("t1", "t2"))
        t3, t4 = (sb(n, [P, a.HG * 2 * a.rot]) if a.rot else None for n in ("t3", "t4"))
        SC, PT, OB, QB, TQ = c.banks[0:2], c.banks[2:4], c.banks[4:6], c.banks[6], c.banks[7]
        keys = lambda qt: (qt + 1) * P if a.causal else SEQ
        KG = a.KH // a.KT
        ROUNDS = -(-OC // 4)
        RW = min(4, OC)
        CONSTS = 7 + (VW > KW)
        AHEAD, TURN = (1, 1) if a.parts else (3, 1)
        KEPT, QKEPT = ("klow", "qlow") if a.latent else ("kkept", "qkept")
        OWN_N = 3 if a.window else 1

        def groups(eng, steps):
            steps(0, True, False)
            with eng.Fori(0, a.G - 2) as j:
                steps(j + 1, False, False)
            steps(a.G - 1, False, True)

        def split(st, high, low, src, n):
            zero = c.zeros[:, :].bitcast(F32)[:, 0:a.D]
            if REP == 1:
                src = src.rearrange("p (h d) -> p h d", h=n)
                zero = zero.rearrange("p (h d) -> p h d", h=1).to_broadcast([P, n, a.D])
                high, low = high[:, :, 0, :], low[:, :, 0, :]
            else:
                src = src.rearrange("p (h r d) -> p h r d", h=n, r=1).to_broadcast([P, n, REP, a.D])
                zero = zero.rearrange("p (h r d) -> p h r d", h=1, r=1).to_broadcast([P, n, REP, a.D])
            st.then(st.eng.tensor_tensor(high, src, zero, ALU.add))
            return st.eng.tensor_tensor(low, src, high.bitcast(F32), ALU.subtract)

        def kept(I, u, before=0):
            return at("kept_d" if u % 2 == 0 else "kept_a", I * (UN // 2) + ((u - before) // 2 + 1))

        with nc.Block() as block:

            @block.gpsimd
            def _(pool):
                pool.memset(mask[:, :], 0.0).then_inc(*inc("made"))
                pool.memset(identb[:, :], 0.0).then_inc(*inc("made"))
                pool.wait_ge(*at("made", 2))
                pool.affine_select(out=identb[:, :], in_=identb[:, :], compare_op=ALU.not_equal, fill=1.0,
                                   base=0, pattern=[[-1, P]], channel_multiplier=1).then_inc(*inc("made"))
                if a.window:
                    pool.memset(mask[:, :], NEG).then_inc(*inc("made"))
                    pool.wait_ge(*at("made", 4))
                    pool.affine_select(out=mask[:, :], in_=mask[:, :], compare_op=ALU.is_ge, fill=0.0,
                                       base=P, pattern=[[-1, MW]], channel_multiplier=1).then_inc(*inc("made"))
                    pool.wait_ge(*at("made", 5))
                    pool.affine_select(out=mask[:, :], in_=mask[:, :], compare_op=ALU.is_gt, fill=0.0,
                                       base=a.window - P, pattern=[[1, MW]], channel_multiplier=-1) \
                        .then_inc(*inc("made"))
                else:
                    pool.affine_select(out=mask[:, :], in_=mask[:, :], compare_op=ALU.is_ge, fill=NEG,
                                       base=0, pattern=[[-1, P]], channel_multiplier=1).then_inc(sig["made"].sem, 3)
                if VW > KW:
                    pool.memset(vv[:, :].rearrange("p (t n) -> p t n", t=TPB)[:, :, KW:], 0.0) \
                        .then_inc(*inc("made"))
                pool.memset(xnT[:, KC * TOKENS:], 0.0).then_inc(*inc("made"))
                if a.parts:
                    pool.wait_ge(*at("loaded", 16 * len(LOADS)))
                    with pool.Fori(0, BATCH) as b:
                        with pool.Fori(0, a.G) as g:
                            for qt in range(TPB):
                                t = (b * a.G + g) * TPB + qt
                                st = Steps(pool, sig["own_q"])
                                st.loop = t * 3
                                pool.wait_ge(*at("qraw", t + 1))
                                st.then(rotate(st, a, qrot[:, :], qraw[:, :], a.HG, qt, cos, sin, t3, t4))
                                pool.wait_ge(*at("qturned", t))
                                parts = qst[:, :].rearrange("p (h s r d) -> p h s r d", r=REP, s=2, d=a.D)
                                split(st, parts[:, :, 0, :, :], parts[:, :, 1, :, :], qrot[:, :], a.HG) \
                                    .then_inc(*inc("qput"))

            @block.tensor
            def _(pe):
                pe.wait_ge(*at("made", CONSTS))
                pe.wait_ge(*at("loaded", 16 * len(LOADS)))
                if a.cut:
                    pe.wait_ge(*at("wlow", len(RAW)))

                def carry_wait(bank):
                    if WR == 64:
                        pe.matmul(bank[:, 0:1], c.zeros[:, 0:P], c.zeros[:, 0:1], start=True, stop=True)

                with pe.Fori(0, BATCH) as b:

                    def keys_values(i):
                        n = b * TPB + i
                        if i >= 2:
                            pe.wait_ge(*at("kput", n - 1))
                            if not a.latent:
                                pe.wait_ge(*at("vput", n - 1))
                        for w, bank in ((WK, SC[i % 2]),) + (() if a.latent else ((WV, OB[i % 2]),)):
                            for k in range(KC):
                                for x_, w_ in XTRIPLE:
                                    last = pe.matmul(bank[:, 0:KW],
                                                     xb[x_][:, k * SEQ + i * P:k * SEQ + (i + 1) * P],
                                                     w[w_][:, k * KW:(k + 1) * KW], start=(k == 0 and x_ + w_ == 0),
                                                     stop=(k == KC - 1 and (x_, w_) == XTRIPLE[-1]))
                        last.then_inc(*inc("kvp"))

                    def turn_keys(i):
                        n = b * TPB + i
                        pe.wait_ge(*at("kput", n + 1))
                        for m in range(KG):
                            pe.wait_ge(*at(KEPT, n * KG + max(m - 1, 0)))
                            carry_wait(PT[m % 2])
                            for hh in range(a.KT):
                                h = m * a.KT + hh
                                src = vv[:, i * VW:i * VW + KW] if a.latent else \
                                    kst[:, h * WR:(h + 1) * WR].bitcast(F32)
                                last = pe.transpose(PT[m % 2][0:WR, hh * P:(hh + 1) * P], src, c.ident[:, :])
                            last.then_inc(*inc("kturned"))

                    def project(t, g, qt):
                        pe.wait_ge(*at("qraw" if a.parts else "qput", t))
                        for k in range(KC):
                            for x_, w_ in XTRIPLE:
                                last = pe.matmul(QB[:, 0:QW], xb[x_][:, k * SEQ + qt * P:k * SEQ + (qt + 1) * P],
                                                 WQ[w_][:, bass.ds(g * QW + k * HD, QW)],
                                                 start=(k == 0 and x_ + w_ == 0),
                                                 stop=(k == KC - 1 and (x_, w_) == XTRIPLE[-1]))
                        last.then_inc(*inc("qp"))

                    def turn_q(t):
                        pe.wait_ge(*at("qput", t + 1))
                        pe.wait_ge(*at(QKEPT, t))
                        carry_wait(TQ)
                        for hh in range(a.HG):
                            last = pe.transpose(TQ[0:WR, hh * P:(hh + 1) * P],
                                                qst[:, hh * WR:(hh + 1) * WR].bitcast(F32), c.ident[:, :])
                        last.then_inc(*inc("qturned"))

                    def score(g, u):
                        qt, hh = divmod(u, a.HG)
                        bank = SC[u % 2]
                        if a.latent:
                            pairs = tuple((q_, kT[k_][:, 0:keys(qt)]) for q_, k_ in TRIPLE)
                        else:
                            key = kT[0][:, bass.ds(g * (SEQ * (a.HG if a.KH == a.H else 1))
                                                   + (hh * SEQ if a.KH == a.H else 0), keys(qt))]
                            pairs = tuple((q_, key) for q_ in range(PASSES))
                        for w, (q_, key) in enumerate(pairs):
                            pe.matmul(bank[:, 0:keys(qt)], qT[qt % 2][q_][:, hh * P:(hh + 1) * P], key,
                                      start=(w == 0), stop=False)
                        lo = max(qt * P - (MW - P), 0)
                        hi = (qt + 1) * P
                        pe.matmul(bank[:, lo:hi], identb[:, :], mask[:, MW - (hi - lo):MW],
                                  start=False, stop=True).then_inc(*inc("scored"))

                    def turn_p(I, u, before, earliest):
                        qt, n = u // a.HG, I * UN + (u - before)
                        pe.wait_ge(*at("exped", n + 1))
                        if not earliest:
                            pe.wait_ge(*kept(I, u - 2, before))
                        for kb in range(keys(qt) // P):
                            last = pe.transpose(PT[u % 2][:, kb * P:(kb + 1) * P],
                                                pr[u % 4][:, kb * P:(kb + 1) * P], c.ident[:, :])
                        last.then_inc(*inc("turned"))

                    def values(I, g, u, before, earliest):
                        qt, hh = divmod(u, a.HG)
                        pe.wait_ge(*kept(I, u, before))
                        if hh == 0 and not earliest:
                            pe.wait_ge(*at("normed", I * TPB + ((u - before) // a.HG - 1)))
                        nb = keys(qt) // P
                        for kb in range(nb):
                            heads = a.HG if a.KH == a.H else 1
                            if a.latent:
                                v = vv[:, kb * VW:(kb + 1) * VW]
                            else:
                                v = vv[:, bass.ds(g * (heads * a.D) + (kb * VW + hh % heads * a.D
                                                                       - before // UN * heads * a.D), P)]
                            last = pe.matmul(OB[qt % 2][:, hh * P:(hh + 1) * P],
                                             pT[u % 2][:, kb * P:(kb + 1) * P], v,
                                             start=(kb == 0), stop=(kb == nb - 1))
                        last.then_inc(*inc("summed"))

                    def steps(g, first, last):
                        I = b * a.G + g
                        t0 = I * TPB
                        for u in range(UN):
                            if u % a.HG == 0 and (u or not first):
                                pe.wait_ge(*at(QKEPT, t0 + (u // a.HG + 1)))
                            qt, next_ = u // a.HG + 1, u // a.HG + 2
                            if u % a.HG == TURN and (qt < TPB or not last):
                                turn_q(t0 + qt)
                            if u % a.HG == AHEAD and (next_ < TPB or not last):
                                project(t0 + next_, *((g, next_) if next_ < TPB else (g + 1, next_ - TPB)))
                            if u >= 2:
                                turn_p(I, u - 2, 0, first and u < 4)
                            elif not first:
                                turn_p(I, u - 2 + UN, UN, False)
                            score(g, u)
                            if u >= 3:
                                values(I, g, u - 3, 0, first and u < 3 + 2 * a.HG)
                            elif not first:
                                values(I, g, u - 3 + UN, UN, False)
                        if last:
                            turn_p(I, UN - 2, 0, False)
                            values(I, g, UN - 3, 0, False)
                            turn_p(I, UN - 1, 0, False)
                            values(I, g, UN - 2, 0, False)
                            values(I, g, UN - 1, 0, False)

                    pe.wait_ge(*at("xlow" if a.cut else "xkept", b + 1))
                    for i in range(TPB):
                        keys_values(i)
                        if i >= 1:
                            turn_keys(i - 1)
                        if i == 1:
                            pe.wait_ge(*at("added", b * TPB))
                            project(b * (a.G * TPB), 0, 0)
                    turn_keys(TPB - 1)
                    turn_q(b * (a.G * TPB))
                    project(b * (a.G * TPB) + 1, 0, 1)
                    pe.wait_ge(*at(KEPT, (b + 1) * (TPB * KG)))
                    if not a.latent:
                        pe.wait_ge(*at("vput", (b + 1) * TPB))
                    pe.wait_ge(*at(QKEPT, b * (a.G * TPB) + 1))
                    groups(pe, steps)

                    OUT = (QB, TQ)
                    YKEPT = "ylow" if a.latent else "ykept"

                    def turn_y(r):
                        qt, m = divmod(r, ROUNDS)
                        if m == 0:
                            pe.wait_ge(*at("normed", (b + 1) * (a.G * TPB) - (TPB - 1 - qt)))
                        if r >= 2:
                            pe.wait_ge(*at(YKEPT, b * (TPB * ROUNDS) + (r - 1)))
                        for k in range(RW):
                            ch = qt * HD + (m * RW + k) * P
                            last = pe.transpose(PT[r % 2][:, k * P:(k + 1) * P], yb[:, ch:ch + P], c.ident[:, :])
                        last.then_inc(*inc("yturned"))

                    def product(r):
                        qt, m = divmod(r, ROUNDS)
                        pe.wait_ge(*at(YKEPT, b * (TPB * ROUNDS) + (r + 1)))
                        if m == 0 and qt >= 2:
                            pe.wait_ge(*at("added", b * TPB + (qt - 1)))
                        for k in range(RW):
                            for y_, w_ in TRIPLE:
                                last = pe.matmul(OUT[qt % 2][:, 0:D_MODEL], yT[r % 2][y_][:, k * P:(k + 1) * P],
                                                 WO[w_][:, (m * RW + k) * D_MODEL:(m * RW + k + 1) * D_MODEL],
                                                 start=(m == 0 and k == 0 and y_ + w_ == 0),
                                                 stop=(m == ROUNDS - 1 and k == RW - 1 and (y_, w_) == TRIPLE[-1]))
                        if m == ROUNDS - 1:
                            last.then_inc(*inc("outp"))

                    for r in range(TPB * ROUNDS):
                        turn_y(r)
                        if r:
                            product(r - 1)
                    product(TPB * ROUNDS - 1)

            @block.scalar
            def _(act):
                def keep_x(b):
                    for k in range(KC):
                        last = act.activation(xb[0][:, k * SEQ:(k + 1) * SEQ],
                                              xnT[:, bass.ds(b * SEQ + k * TOKENS, SEQ)], ACT.Copy)
                    last.then_inc(*inc("xkept"))

                act.wait_ge(*at("made", CONSTS))
                keep_x(0)
                if a.cut:
                    act.wait_ge(*at("loaded", 16 * len(LOADS)))
                    for raw, w in zip(RAW, PARTS):
                        act.activation(w[0][:, :], raw, ACT.Copy).then_inc(*inc("whigh"))
                with act.Fori(0, BATCH) as b:

                    def keep_keys(i):
                        n = b * TPB + i
                        for m in range(KG):
                            act.wait_ge(*at("kturned", n * KG + m + 1))
                            act.activation(kT[0][:, :].rearrange("p (h n) -> p h n", h=a.KH)
                                           [:, m * a.KT:(m + 1) * a.KT, i * P:(i + 1) * P],
                                           PT[m % 2][0:WR, 0:a.KT * P].rearrange("p (h n) -> p h n", h=a.KT),
                                           ACT.Copy).then_inc(*inc("kkept"))

                    def keep_q(t, qt):
                        act.wait_ge(*at("qturned", t + 1))
                        last = act.activation(qT[qt % 2][0][:, :], TQ[0:WR, :], ACT.Copy)
                        if PASSES == 1 or a.latent:
                            last.then_inc(*inc("qkept"))

                    def fetch_q(t):
                        if a.parts:
                            act.wait_ge(*at("qp", t + 1))
                            act.wait_ge(*at("qput", t))
                            act.activation(qraw[:, :], QB[:, 0:QW], ACT.Copy).then_inc(*inc("qraw"))

                    def keep_swapped(qt):
                        if PASSES == 2 and not a.latent:
                            for x, y in ((0, a.D), (a.D, 0)):
                                last = act.activation(qT[qt % 2][1][x:x + a.D, :], TQ[y:y + a.D, :], ACT.Copy)
                            last.then_inc(*inc("qkept"))

                    def expo(I, u, earliest):
                        qt, hh = divmod(u, a.HG)
                        col, n = (qt % 2) * a.HG + hh, I * UN + u
                        act.wait_ge(*at("negged", n + 1))
                        if not earliest:
                            act.wait_ge(*at("turned", I * UN + (u - 3)))
                        act.activation(pr[u % 4][:, 0:keys(qt)], SC[u % 2][:, 0:keys(qt)], ACT.Exp,
                                       bias=nm[:, col:col + 1], scale=a.scale,
                                       accum_out=rs[:, col:col + 1]).then_inc(*inc("exped"))

                    def keep_p(I, u, before, earliest):
                        if u % 2 == 0:
                            return
                        w = keys(u // a.HG)
                        act.wait_ge(*at("turned", I * UN + (u - before + 1)))
                        if not earliest:
                            act.wait_ge(*at("summed", I * UN + (u - before - 1)))
                        act.activation(pT[u % 2][:, 0:w], PT[u % 2][:, 0:w], ACT.Copy).then_inc(*inc("kept_a"))

                    def steps(g, first, last):
                        I = b * a.G + g
                        for u in range(UN):
                            qt = u // a.HG + 1
                            if u % a.HG == TURN and (qt < TPB or not last):
                                act.wait_ge(*at("scored", I * UN + (qt - 1) * a.HG))
                                keep_q(I * TPB + qt, qt)
                            if u % a.HG == 3 and (qt < TPB or not last):
                                keep_swapped(qt)
                            if u >= 2:
                                keep_p(I, u - 2, 0, first and u < 4)
                            elif not first:
                                keep_p(I, u - 2 + UN, UN, False)
                            expo(I, u, first and u < 4)
                            if u % a.HG == AHEAD and (qt + 1 < TPB or not last):
                                fetch_q(I * TPB + qt + 1)
                            if a.window and u % a.HG == a.HG - 1:
                                cut = slice((qt - 1) % 2 * a.HG, ((qt - 1) % 2 + 1) * a.HG)
                                act.wait_ge(*at("own_n", (I * TPB + (qt - 1)) * OWN_N + 1))
                                act.activation(es[:, cut], es[:, cut], ACT.Exp).then_inc(*inc("maxed"))
                        if last:
                            keep_p(I, UN - 2, 0, False)
                            keep_p(I, UN - 1, 0, False)

                    for i in range(TPB):
                        if not a.latent:
                            act.wait_ge(*at("kvp", b * TPB + i + 1))
                            act.activation(vv[:, i * VW:i * VW + KW], OB[i % 2][:, 0:KW],
                                           ACT.Copy).then_inc(*inc("vput"))
                        if i >= 1:
                            keep_keys(i - 1)
                        if i == 1:
                            fetch_q(b * (a.G * TPB))
                    keep_keys(TPB - 1)
                    keep_q(b * (a.G * TPB), 0)
                    keep_swapped(0)
                    fetch_q(b * (a.G * TPB) + 1)
                    groups(act, steps)
                    act.wait_ge(*at("qp", (b + 1) * (a.G * TPB)))
                    keep_x(b + 1)
                    for r in range(TPB * ROUNDS):
                        act.wait_ge(*at("yturned", b * (TPB * ROUNDS) + (r + 1)))
                        act.activation(yT[r % 2][0][:, :], PT[r % 2][:, 0:RW * P], ACT.Copy).then_inc(*inc("ykept"))

            @block.vector
            def _(dve):
                dve.wait_ge(*at("loaded", 16 * len(LOADS)))
                if a.window:
                    dve.tensor_scalar(negsink[:, :], sink[:, :], -1.0, None, ALU.mult).then_inc(*inc("own_o"))
                    dve.wait_ge(*at("own_o", 1))

                def low_x(b):
                    dve.wait_ge(*at("xkept", b + 1))
                    for k in range(KC):
                        last = dve.tensor_tensor(xb[1][:, k * SEQ:(k + 1) * SEQ],
                                                 xnT[:, bass.ds(b * SEQ + k * TOKENS, SEQ)],
                                                 xb[0][:, k * SEQ:(k + 1) * SEQ].bitcast(F32), ALU.subtract)
                    last.then_inc(*inc("xlow"))

                def low(part, bank, w, high_done, done):
                    dve.wait_ge(*high_done)
                    dve.tensor_tensor(part[1][:, w], bank, part[0][:, w].bitcast(F32), ALU.subtract) \
                       .then_inc(*inc(done))

                if a.cut:
                    low_x(0)
                    for i, (raw, w) in enumerate(zip(RAW, PARTS)):
                        dve.wait_ge(*at("whigh", i + 1))
                        dve.tensor_tensor(w[1][:, :], raw, w[0][:, :].bitcast(F32), ALU.subtract) \
                           .then_inc(*inc("wlow"))

                with dve.Fori(0, BATCH) as b:

                    def low_keys(i):
                        if a.latent:
                            low(kT, PT[0][:, 0:P], slice(i * P, (i + 1) * P), at("kkept", b * TPB + i + 1), "klow")

                    def low_q(t, qt):
                        if a.latent:
                            low(qT[qt % 2], TQ[:, :], slice(0, a.HG * P), at("qkept", t + 1), "qlow")

                    def put_keys(i):
                        n = b * TPB + i
                        dve.wait_ge(*at("kvp", n + 1))
                        if a.latent:
                            dve.tensor_tensor(vv[:, i * VW:i * VW + KW], SC[i % 2][:, 0:KW], b_k[:, :], ALU.add) \
                               .then_inc(*inc("kput"))
                        else:
                            dve.wait_ge(*at("kturned", n * KG))
                            st = Steps(dve, sig["own_k"])
                            st.loop = n * 3
                            st.then(rotate(st, a, krot[:, :], SC[i % 2][:, 0:KW], a.KH, i,
                                           cos, sin, t1, t2))
                            parts = kst[:, :].rearrange("p (h r s d) -> p h r s d", r=REP, s=2, d=a.D)
                            split(st, parts[:, :, :, 0, :], parts[:, :, :, 1, :], krot[:, :], a.KH) \
                                .then_inc(*inc("kput"))

                    def put_q(t, g):
                        if a.latent:
                            dve.wait_ge(*at("qp", t + 1))
                            dve.wait_ge(*at("qturned", t))
                            dve.tensor_tensor(qst[:, :], QB[:, :], b_q[:, bass.ds(g * QW, QW)], ALU.add) \
                               .then_inc(*inc("qput"))

                    def maximum(I, g, u):
                        qt, hh = divmod(u, a.HG)
                        col = (qt % 2) * a.HG + hh
                        dve.wait_ge(*at("scored", I * UN + (u + 1)))
                        dve.reduce_max(mx[:, col:col + 1], SC[u % 2][:, 0:keys(qt)], AX) \
                           .then_inc(*inc("own_o"))
                        dve.wait_ge(*at("own_o", I * UN + (u + 1 + bool(a.window))))
                        if a.window:
                            dve.scalar_tensor_tensor(out=nm[:, col:col + 1], in0=mx[:, col:col + 1],
                                                     scalar=-a.scale, in1=negsink[:, bass.ds(g * a.HG + hh, 1)],
                                                     op0=ALU.mult, op1=ALU.min).then_inc(*inc("negged"))
                        else:
                            dve.tensor_scalar(nm[:, col:col + 1], mx[:, col:col + 1], -a.scale, None,
                                              ALU.mult).then_inc(*inc("negged"))

                    def keep_p(I, u, before, earliest):
                        if u % 2 == 1:
                            return
                        w = keys(u // a.HG)
                        dve.wait_ge(*at("turned", I * UN + (u - before + 1)))
                        if not earliest:
                            dve.wait_ge(*at("summed", I * UN + (u - before - 1)))
                        dve.tensor_copy(pT[u % 2][:, 0:w], PT[u % 2][:, 0:w]).then_inc(*inc("kept_d"))

                    def sink_minus_max(I, g, qt):
                        cut = slice((qt % 2) * a.HG, (qt % 2 + 1) * a.HG)
                        dve.wait_ge(*at("negged", I * UN + (qt + 1) * a.HG))
                        dve.tensor_tensor(es[:, cut], nm[:, cut], sink[:, bass.ds(g * a.HG, a.HG)],
                                          ALU.add).then_inc(*inc("own_n"))

                    def normalize(I, g, qt, before):
                        cut = slice((qt % 2) * a.HG, (qt % 2 + 1) * a.HG)
                        t = I * TPB + (qt - before * TPB)
                        dve.wait_ge(*at("summed", I * UN + ((qt + 1) * a.HG - before * UN)))
                        own = 0
                        if a.window:
                            dve.wait_ge(*at("maxed", t + 1))
                            dve.tensor_tensor(rs[:, cut], rs[:, cut], es[:, cut], ALU.add) \
                               .then_inc(*inc("own_n"))
                            own = 2
                            dve.wait_ge(*at("own_n", t * OWN_N + own))
                        dve.reciprocal(rinv[:, cut], rs[:, cut]).then_inc(*inc("own_n"))
                        dve.wait_ge(*at("own_n", t * OWN_N + (own + 1)))
                        dve.tensor_tensor(
                            yb[:, bass.ds(g * QW + (qt * HD - before * QW), QW)]
                            .rearrange("p (h d) -> p h d", h=a.HG),
                            OB[qt % 2][:, :].rearrange("p (h n) -> p h n", h=a.HG)[:, :, 0:a.D],
                            rinv[:, cut].rearrange("p (h o) -> p h o", o=1).to_broadcast([P, a.HG, a.D]),
                            ALU.mult).then_inc(*inc("normed"))

                    def steps(g, first, last):
                        I = b * a.G + g
                        for u in range(UN):
                            qt = u // a.HG + 1
                            if u % a.HG == TURN + 1 and (qt < TPB or not last):
                                low_q(I * TPB + qt, qt)
                            maximum(I, g, u)
                            if a.window and u % a.HG == a.HG - 1:
                                sink_minus_max(I, g, qt - 1)
                            if u >= 2:
                                keep_p(I, u - 2, 0, first and u < 4)
                            elif not first:
                                keep_p(I, u - 2 + UN, UN, False)
                            if u % a.HG == AHEAD and (qt + 1 < TPB or not last):
                                put_q(I * TPB + qt + 1, g if qt + 1 < TPB else g + 1)
                            if u % a.HG == 2:
                                if u >= 3:
                                    normalize(I, g, qt - 2, 0)
                                elif not first:
                                    normalize(I, g, TPB - 1, 1)
                        if last:
                            keep_p(I, UN - 2, 0, False)
                            keep_p(I, UN - 1, 0, False)
                            normalize(I, g, TPB - 1, 0)

                    for i in range(TPB):
                        put_keys(i)
                        if i >= 1:
                            low_keys(i - 1)
                        if i == 1:
                            put_q(b * (a.G * TPB), 0)
                    low_keys(TPB - 1)
                    low_q(b * (a.G * TPB), 0)
                    put_q(b * (a.G * TPB) + 1, 0)
                    groups(dve, steps)
                    if a.cut:
                        low_x(b + 1)
                    for qt in range(TPB):
                        n = b * TPB + qt
                        if a.latent:
                            for r in range(qt * ROUNDS + (qt > 0), (qt + 1) * ROUNDS + (qt < TPB - 1)):
                                low(yT[r % 2], PT[r % 2][:, 0:RW * P], slice(0, RW * P),
                                    at("ykept", b * (TPB * ROUNDS) + r + 1), "ylow")
                        at_x = c.x[:, bass.ds(b * (TPB * D_MODEL) + qt * D_MODEL, D_MODEL)]
                        if a.latent:
                            dve.tensor_tensor(at_x, at_x, b_o[:, :], ALU.add).then_inc(*inc("own_k"))
                            dve.wait_ge(*at("own_k", n + 1))
                        dve.wait_ge(*at("outp", n + 1))
                        dve.tensor_tensor(at_x, at_x, (QB, TQ)[qt % 2][:, 0:D_MODEL], ALU.add) \
                           .then_inc(*inc("added"))
        NI = BATCH * a.G
        for n, v in dict(
                loaded=16 * len(LOADS), made=CONSTS, whigh=3 if a.cut else 0, wlow=3 if a.cut else 0,
                xlow=BATCH + 1 if a.cut else 0, klow=TILES if a.latent else 0, qlow=NI * TPB if a.latent else 0,
                ylow=TILES * ROUNDS if a.latent else 0,
                qraw=NI * TPB if a.parts else 0, xkept=BATCH + 1, kvp=TILES, kput=TILES,
                vput=0 if a.latent else TILES,
                kturned=TILES * KG, kkept=TILES * KG, qp=NI * TPB, qput=NI * TPB, qturned=NI * TPB, qkept=NI * TPB,
                scored=NI * UN, negged=NI * UN, exped=NI * UN, turned=NI * UN, kept_d=NI * UN // 2,
                kept_a=NI * UN // 2, summed=NI * UN, normed=NI * TPB, maxed=NI * TPB if a.window else 0,
                own_k=TILES * (3 if a.parts else 1), own_q=NI * TPB * 3 if a.parts else 0,
                own_n=NI * TPB * OWN_N, own_o=NI * UN + bool(a.window),
                yturned=TILES * ROUNDS, ykept=TILES * ROUNDS, outp=TILES, added=TILES).items():
            sig[n].counted(v)


LAYERS = ["mamba", "moe0", "rotary", "moe0", "sinks", "moe1", "latent", "moe1"]
STAGES = {"mamba": mamba, "moe0": lambda c: moe(c, 0), "moe1": lambda c: moe(c, 1),
          "rotary": lambda c: attention(c, ROTARY), "sinks": lambda c: attention(c, SINKS),
          "latent": lambda c: attention(c, LATENT)}


def build_program(nc, t, layers=LAYERS):
    with ExitStack() as ctx:
        c = setup(nc, ctx, t)
        load_residual(c)
        for name in layers:
            STAGES[name](c)
        store_residual(c)


def host_layout(inputs):
    f = lambda name: np.asarray(inputs[name])
    cols = lambda a: np.ascontiguousarray(a.reshape(-1, P).T)
    gu0 = np.concatenate([f("L0_ffn_w_gate"), f("L0_ffn_w_up")], axis=2)
    gu1 = f("L1_ffn_gate_up_proj").transpose(0, 2, 1)
    pack = lambda w: w.reshape(w.shape[0], KC, P, w.shape[2]).transpose(2, 0, 1, 3).reshape(P, -1)
    rq, rk, rv = np.split(f("L0_attn_b_w_atten").T, 3, axis=1)
    sq, sk, sv = np.split(f("L1_attn_a_W_qkv"), (SINKS.H * SINKS.D, (SINKS.H + SINKS.KH) * SINKS.D), axis=1)
    position = np.arange(SEQ, dtype=np.float32)
    theta_r = np.outer(position, 1.0 / np.float32(10000.0) ** (np.arange(0, 16, 2, dtype=np.float32) / 16))
    theta_s = np.outer(position, np.float32(1.0 / 1024.0) ** np.linspace(0.0, 1.0, 16, dtype=np.float32))
    return {
        "ra_wq": rq, "ra_wk": rk, "ra_wv": rv, "ra_wo": f("L0_attn_b_w_proj").T,
        "ra_cos": np.cos(theta_r).astype(np.float32), "ra_sin": np.sin(theta_r).astype(np.float32),
        "sa_wq": sq, "sa_wk": sk, "sa_wv": sv, "sa_wo": f("L1_attn_a_W_out"),
        "sa_cos": np.cos(theta_s).astype(np.float32), "sa_sin": np.sin(theta_s).astype(np.float32),
        "sinks": f("L1_attn_a_s").reshape(1, -1),
        "la_wq": f("L1_attn_b_W_d"), "la_wk": f("L1_attn_b_W_lat"), "la_wo": f("L1_attn_b_W_proj"),
        "la_bq": f("L1_attn_b_b_d")[None, :], "la_bk": f("L1_attn_b_b_lat")[None, :],
        "la_bo": f("L1_attn_b_b_proj")[None, :],
        "w_gu0": pack(gu0), "w_gu1": pack(gu1),
        "w_dn0": f("L0_ffn_w_down").transpose(1, 0, 2).reshape(M0_I, -1),
        "w_dn1": f("L1_ffn_down_proj").transpose(2, 0, 1).reshape(M1_I, -1),
        "gate0T": f("L0_ffn_gate_w").T, "gate_b": f("L0_ffn_gate_b")[None, :],
        "b_all": np.concatenate([f("L0_ffn_b_gate"), f("L0_ffn_b_up"), f("L0_ffn_b_down")], axis=1),
        "gate1": f("L1_ffn_gate_weight"), "o2n": f("L1_ffn_old_to_new")[:, None],
        "x": f("L0_attn_a_hidden_states"),
        "in_wT": f("L0_attn_a_in_proj_w").T, "conv_w": f("L0_attn_a_conv_w"),
        "conv_b": cols(f("L0_attn_a_conv_b")), "D": cols(f("L0_attn_a_D")), "dt_b": cols(f("L0_attn_a_dt_proj_b")),
        "A_log": f("L0_attn_a_A_log"), "x_wT": f("L0_attn_a_x_proj_w").T,
        "dt_wT": f("L0_attn_a_dt_proj_w").T, "out_wT": f("L0_attn_a_out_proj_w").T,
    }


SCRATCH = {"scratch_bc": (2 * D_STATE, TOKENS)}
for _which, _rows in ((0, M0_TILES * P), (1, M1_E * M1_CAP)):
    SCRATCH[f"scratch_xs{_which}"] = SCRATCH[f"scratch_ys{_which}"] = (_rows, D_MODEL)


def make(nc, arrays, layers=LAYERS):
    t = {n: nc.dram_tensor(f"in_{n}", a.shape, mybir.dt.from_np(a.dtype), kind="ExternalInput").ap()
         for n, a in arrays.items()}
    for n, shape in SCRATCH.items():
        t[n] = nc.dram_tensor(n, shape, F32, kind="Internal").ap()
    t["out"] = nc.dram_tensor("out", (BATCH, SEQ, D_MODEL), F32, kind="ExternalOutput").ap()
    build_program(nc, t, layers)


def kernel(**inputs):
    import concourse.bacc as bacc
    from concourse.bass_utils import run_bass_kernel_spmd

    nc = bacc.Bacc("TRN2", target_bir_lowering=False, num_devices=1)
    arrays = {n: np.ascontiguousarray(a) for n, a in host_layout(inputs).items()}
    make(nc, arrays)
    got = run_bass_kernel_spmd(nc, [{f"in_{n}": a for n, a in arrays.items()}], core_ids=[0])
    return got.results[0]["out"]
```
